# Optimizing a Trainium2 kernel written in Bass

```python
import numpy as np
import jax
import jax.numpy as jnp

def _softmax(x, axis=-1):
    return jax.nn.softmax(x, axis=axis)

def _gelu(x):
    return jax.nn.gelu(x, approximate=True)

def _silu(x):
    return jax.nn.silu(x)

def _sigmoid(x):
    return jax.nn.sigmoid(x)

def _layernorm(x, axis=-1, eps=1e-05):
    m = jnp.mean(x, axis=axis, keepdims=True)
    v = jnp.var(x, axis=axis, keepdims=True)
    return (x - m) / jnp.sqrt(v + eps)

def _scatter_add(tgt, idx, src, axis=0):
    return tgt.at[idx].add(src)

def _segment_sum(src, seg, n):
    return jax.ops.segment_sum(src, seg, n)
kernel_name = 'mk_gps_d2_gnn_r8_828120'

def setup_inputs(seed: int=0):
    np.random.seed(seed)
    _w = jnp.asarray

    def _rec_inputs():
        import jax
        import jax.numpy as jnp
        _gk = jax.random.key(seed)
        x = -8.776e-05 + 1 * jax.random.normal(jax.random.fold_in(_gk, 1), (1250, 512), jnp.float32)
        _s = jax.random.randint(jax.random.fold_in(_gk, 2), (20000,), 0, 1250, jnp.int32)
        _d = jax.random.randint(jax.random.fold_in(_gk, 3), (20000,), 0, 1250, jnp.int32)
        _loop = jnp.arange(1250, dtype=jnp.int32)
        src = jnp.concatenate([_s, _d, _loop])
        dst = jnp.concatenate([_d, _s, _loop])
        _o = jnp.argsort(dst, stable=True)
        src = src[_o]
        dst = dst[_o]
        edge_attr_4 = 0.00171547 + 0.999346 * jax.random.normal(jax.random.fold_in(_gk, 11), (41250, 4), jnp.float32)
        edge_attr_8 = 0.000126197 + 0.999763 * jax.random.normal(jax.random.fold_in(_gk, 12), (41250, 8), jnp.float32)
        return (x, src, dst, edge_attr_4, edge_attr_8)
    x, src, dst, edge_attr_4, edge_attr_8 = _rec_inputs()

    def _L0_gnn_setup():
        import jax, jax.numpy as jnp
        import numpy as np
        MUL = 128
        N_NODES = 1250
        N_EDGES = 20000
        R_BASIS = 8
        HIDDEN = 64
        W_NUMEL = 4 * MUL
        SQRT3 = 3.0 ** 0.5
        SILU_2MOM = 1.679177
        AVG_NUM_NEIGHBORS = 10.0

        def _lin_irreps(x0, x1, W0, W1):
            y0 = x0 @ W0 / jnp.sqrt(jnp.float32(W0.shape[0]))
            y1 = jnp.einsum('num,uv->nvm', x1, W1) / jnp.sqrt(jnp.float32(W1.shape[0]))
            return (y0, y1)

        def _forward(node_feats, edge_attrs, edge_feats, edge_index, W_up0, W_up1, W_mlp1, W_mlp2, W_mlp3, W_mlp4, W_out0, W_out1):
            num_nodes = node_feats.shape[0]
            sender, receiver = (edge_index[0], edge_index[1])
            x0 = node_feats[:, :MUL]
            x1 = node_feats[:, MUL:].reshape(num_nodes, MUL, 3)
            x0, x1 = _lin_irreps(x0, x1, W_up0, W_up1)
            h = edge_feats
            for W in (W_mlp1, W_mlp2, W_mlp3):
                h = SILU_2MOM * jax.nn.silu(h @ W / jnp.sqrt(jnp.float32(W.shape[0])))
            tpw = h @ W_mlp4 / jnp.sqrt(jnp.float32(W_mlp4.shape[0]))
            w1, w2, w3, w4 = jnp.split(tpw, 4, axis=-1)
            s0 = x0[sender]
            s1 = x1[sender]
            y0 = edge_attrs[:, 0:1]
            y1 = edge_attrs[:, 1:4]
            p1 = w1 * s0 * y0
            p2 = (w2 * s0)[:, :, None] * y1[:, None, :]
            p3 = w3[:, :, None] * s1 * y0[:, None, :]
            p4 = w4 * jnp.einsum('eum,em->eu', s1, y1) / SQRT3
            m0 = jnp.concatenate([p1, p4], axis=-1)
            m1 = jnp.concatenate([p2, p3], axis=1)
            msg0 = jax.ops.segment_sum(m0, receiver, num_segments=num_nodes)
            msg1 = jax.ops.segment_sum(m1, receiver, num_segments=num_nodes)
            o0, o1 = _lin_irreps(msg0, msg1, W_out0, W_out1)
            out = jnp.concatenate([o0, o1.reshape(num_nodes, 3 * MUL)], axis=-1)
            return out / AVG_NUM_NEIGHBORS
        key = jax.random.key(seed)
        ks = jax.random.split(key, 12)
        rn = lambda k, s: jax.random.normal(k, s, dtype=jnp.float32)
        return {'node_feats': rn(ks[0], (N_NODES, 4 * MUL)), 'edge_attrs': rn(ks[1], (N_EDGES, 4)), 'edge_feats': rn(ks[2], (N_EDGES, R_BASIS)), 'edge_index': jax.random.randint(ks[3], (2, N_EDGES), 0, N_NODES), 'W_up0': rn(ks[4], (MUL, MUL)), 'W_up1': rn(ks[5], (MUL, MUL)), 'W_mlp1': rn(ks[6], (R_BASIS, HIDDEN)), 'W_mlp2': rn(ks[7], (HIDDEN, HIDDEN)), 'W_mlp3': rn(ks[8], (HIDDEN, HIDDEN)), 'W_mlp4': rn(ks[9], (HIDDEN, W_NUMEL)), 'W_out0': rn(ks[10], (2 * MUL, MUL)), 'W_out1': rn(ks[11], (2 * MUL, MUL))}
    _L0_gnn_all = _L0_gnn_setup()
    _L0_gnn_in = {k: v for k, v in _L0_gnn_all.items() if k in ('W_up0', 'W_up1', 'W_mlp1', 'W_mlp2', 'W_mlp3', 'W_mlp4', 'W_out0', 'W_out1')}
    del _L0_gnn_all

    def _L0_mix_setup():
        import jax, jax.numpy as jnp
        import numpy as np
        import math
        H_DIM = 512
        QKV_DIM = 512
        NUM_HEADS = 8
        HEAD_DIM = QKV_DIM // NUM_HEADS
        B, S = (4, 1024)

        def _split_heads(t):
            Bn, Sn, _ = t.shape
            return t.reshape(Bn, Sn, NUM_HEADS, HEAD_DIM).transpose(0, 2, 1, 3)
        key = jax.random.key(seed)
        ks = jax.random.split(key, 9)
        sc = 1.0 / math.sqrt(H_DIM)
        return {'x': jax.random.normal(ks[0], (B, S, H_DIM), dtype=jnp.float32), 'Wq': jax.random.normal(ks[1], (QKV_DIM, H_DIM), dtype=jnp.float32) * sc, 'bq': jax.random.normal(ks[2], (QKV_DIM,), dtype=jnp.float32) * 0.01, 'Wk': jax.random.normal(ks[3], (QKV_DIM, H_DIM), dtype=jnp.float32) * sc, 'bk': jax.random.normal(ks[4], (QKV_DIM,), dtype=jnp.float32) * 0.01, 'Wv': jax.random.normal(ks[5], (QKV_DIM, H_DIM), dtype=jnp.float32) * sc, 'bv': jax.random.normal(ks[6], (QKV_DIM,), dtype=jnp.float32) * 0.01, 'Wl': jax.random.normal(ks[7], (H_DIM, QKV_DIM), dtype=jnp.float32) * sc, 'bl': jax.random.normal(ks[8], (H_DIM,), dtype=jnp.float32) * 0.01}
    _L0_mix_all = _L0_mix_setup()
    _L0_mix_in = {k: v for k, v in _L0_mix_all.items() if k in ('Wq', 'bq', 'Wk', 'bk', 'Wv', 'bv', 'Wl', 'bl')}
    del _L0_mix_all

    def _L0_ffn_setup():
        import jax, jax.numpy as jnp
        import numpy as np
        D = 512
        E = 8
        K = 2
        EXP = 4
        LN_EPS = 1e-05
        key = jax.random.key(seed)
        ks = jax.random.split(key, 8)
        B, T = (8, 256)
        Dh = D * EXP
        x = jax.random.normal(ks[0], (B, T, D), dtype=jnp.float32)
        ln_g = jnp.ones((D,), dtype=jnp.float32)
        ln_b = jnp.zeros((D,), dtype=jnp.float32)
        lim_r = np.sqrt(6.0 / (D + E)).astype(np.float32)
        w_r = jax.random.uniform(ks[1], (E, D), dtype=jnp.float32, minval=-lim_r, maxval=lim_r)
        b_r = jnp.zeros((E,), dtype=jnp.float32)
        lim1 = np.sqrt(6.0 / (D + Dh)).astype(np.float32)
        W1 = jax.random.uniform(ks[2], (E, D, Dh), dtype=jnp.float32, minval=-lim1, maxval=lim1)
        b1 = jnp.zeros((E, Dh), dtype=jnp.float32)
        W2 = jax.random.uniform(ks[3], (E, Dh, D), dtype=jnp.float32, minval=-lim1, maxval=lim1)
        b2 = jnp.zeros((E, D), dtype=jnp.float32)
        return {'x': x, 'ln_g': ln_g, 'ln_b': ln_b, 'w_r': w_r, 'b_r': b_r, 'W1': W1, 'b1': b1, 'W2': W2, 'b2': b2}
    _L0_ffn_all = _L0_ffn_setup()
    _L0_ffn_in = {k: v for k, v in _L0_ffn_all.items() if k in ('ln_g', 'ln_b', 'w_r', 'b_r', 'W1', 'b1', 'W2', 'b2')}
    del _L0_ffn_all

    def _L1_gnn_setup():
        import jax, jax.numpy as jnp
        import numpy as np
        N_NODES = 1250

        def gcn_conv(x, edge_index, W, b):
            n = x.shape[0]
            loop = jnp.arange(n)
            src = jnp.concatenate([edge_index[0], loop])
            dst = jnp.concatenate([edge_index[1], loop])
            deg = jax.ops.segment_sum(jnp.ones_like(dst, dtype=x.dtype), dst, num_segments=n)
            dinv = jnp.where(deg > 0, jax.lax.rsqrt(deg), 0.0)
            norm = dinv[src] * dinv[dst]
            h = x @ W
            msg = h[src] * norm[:, None]
            out = jax.ops.segment_sum(msg, dst, num_segments=n)
            return out + b
        key = jax.random.key(seed)
        k1, k2, k3, k4 = jax.random.split(key, 4)
        c = [512, 1024, 512]
        x = jax.random.normal(k1, (N_NODES, c[0]), dtype=jnp.float32)
        edge_index = jax.random.randint(k2, (2, 20000), 0, N_NODES, dtype=jnp.int64)
        W1 = jax.random.normal(k3, (c[0], c[1]), dtype=jnp.float32) / np.sqrt(c[0])
        b1 = jnp.zeros((c[1],), dtype=jnp.float32)
        W2 = jax.random.normal(k4, (c[1], c[2]), dtype=jnp.float32) / np.sqrt(c[1])
        b2 = jnp.zeros((c[2],), dtype=jnp.float32)
        return {'x': x, 'edge_index': edge_index, 'W1': W1, 'b1': b1, 'W2': W2, 'b2': b2}
    _L1_gnn_all = _L1_gnn_setup()
    _L1_gnn_in = {k: v for k, v in _L1_gnn_all.items() if k in ('W1', 'b1', 'W2', 'b2')}
    del _L1_gnn_all

    def _L1_mix_setup():
        import jax, jax.numpy as jnp
        import numpy as np
        HEADS = 8
        DIM_HEAD = 64
        LN_EPS = 1e-05
        key = jax.random.key(seed)
        k1, k2, k3, k4, k5 = jax.random.split(key, 5)
        B, N, C = (8, 512, 512)
        dim = HEADS * DIM_HEAD
        x = jax.random.normal(k1, (B, N, C), dtype=jnp.float32)
        w_qkv = jax.random.normal(k2, (C, dim * 3), dtype=jnp.float32) * (1.0 / np.sqrt(C))
        w_out = jax.random.normal(k3, (dim, C), dtype=jnp.float32) * (1.0 / np.sqrt(dim))
        b_out = jax.random.normal(k4, (C,), dtype=jnp.float32) * 0.01
        ln_scale = jnp.ones((C,), dtype=jnp.float32) + 0.02 * jax.random.normal(k5, (C,), dtype=jnp.float32)
        return {'x': x, 'w_qkv': w_qkv, 'w_out': w_out, 'b_out': b_out, 'ln_scale': ln_scale}
    _L1_mix_all = _L1_mix_setup()
    _L1_mix_in = {k: v for k, v in _L1_mix_all.items() if k in ('w_qkv', 'w_out', 'b_out', 'ln_scale')}
    del _L1_mix_all

    def _L1_ffn_setup():
        import jax, jax.numpy as jnp
        import numpy as np
        N_CONST = 6
        PARTITIONS_OF_6 = [(6,), (5, 1), (4, 2), (4, 1, 1), (3, 3), (3, 2, 1), (3, 1, 1, 1), (2, 2, 2), (2, 2, 1, 1), (2, 1, 1, 1, 1), (1, 1, 1, 1, 1, 1)]
        N_EXPERTS = 6
        TOP_K = 2

        def _partition_weights():
            w = np.zeros((len(PARTITIONS_OF_6), N_EXPERTS), dtype=np.float32)
            for i, partition in enumerate(PARTITIONS_OF_6):
                for j, part in enumerate(partition):
                    if j < N_EXPERTS:
                        w[i, j] = part / N_CONST
            return jnp.asarray(w)
        key = jax.random.key(seed)
        ks = jax.random.split(key, 6)
        B, S, D, F, E, P = (32, 256, 512, 341, 6, 11)
        scale_in = 1.0 / np.sqrt(D)
        scale_hid = 1.0 / np.sqrt(F)
        return {'x': jax.random.normal(ks[0], (B, S, D), dtype=jnp.float32), 'router_w': jax.random.normal(ks[1], (P, D), dtype=jnp.float32) * scale_in, 'W1': jax.random.normal(ks[2], (E, D, F), dtype=jnp.float32) * scale_in, 'b1': jax.random.normal(ks[3], (E, F), dtype=jnp.float32) * 0.01, 'W2': jax.random.normal(ks[4], (E, F, D), dtype=jnp.float32) * scale_hid, 'b2': jax.random.normal(ks[5], (E, D), dtype=jnp.float32) * 0.01}
    _L1_ffn_all = _L1_ffn_setup()
    _L1_ffn_in = {k: v for k, v in _L1_ffn_all.items() if k in ('router_w', 'W1', 'b1', 'W2', 'b2')}
    del _L1_ffn_all
    return {'x': x, 'src': src, 'dst': dst, 'edge_attr_4': edge_attr_4, 'edge_attr_8': edge_attr_8, 'L0_gnn_W_up0': _L0_gnn_in['W_up0'], 'L0_gnn_W_up1': _L0_gnn_in['W_up1'], 'L0_gnn_W_mlp1': _L0_gnn_in['W_mlp1'], 'L0_gnn_W_mlp2': _L0_gnn_in['W_mlp2'], 'L0_gnn_W_mlp3': _L0_gnn_in['W_mlp3'], 'L0_gnn_W_mlp4': _L0_gnn_in['W_mlp4'], 'L0_gnn_W_out0': _L0_gnn_in['W_out0'], 'L0_gnn_W_out1': _L0_gnn_in['W_out1'], 'L0_mix_Wq': _L0_mix_in['Wq'], 'L0_mix_bq': _L0_mix_in['bq'], 'L0_mix_Wk': _L0_mix_in['Wk'], 'L0_mix_bk': _L0_mix_in['bk'], 'L0_mix_Wv': _L0_mix_in['Wv'], 'L0_mix_bv': _L0_mix_in['bv'], 'L0_mix_Wl': _L0_mix_in['Wl'], 'L0_mix_bl': _L0_mix_in['bl'], 'L0_ffn_ln_g': _L0_ffn_in['ln_g'], 'L0_ffn_ln_b': _L0_ffn_in['ln_b'], 'L0_ffn_w_r': _L0_ffn_in['w_r'], 'L0_ffn_b_r': _L0_ffn_in['b_r'], 'L0_ffn_W1': _L0_ffn_in['W1'], 'L0_ffn_b1': _L0_ffn_in['b1'], 'L0_ffn_W2': _L0_ffn_in['W2'], 'L0_ffn_b2': _L0_ffn_in['b2'], 'L1_gnn_W1': _L1_gnn_in['W1'], 'L1_gnn_b1': _L1_gnn_in['b1'], 'L1_gnn_W2': _L1_gnn_in['W2'], 'L1_gnn_b2': _L1_gnn_in['b2'], 'L1_mix_w_qkv': _L1_mix_in['w_qkv'], 'L1_mix_w_out': _L1_mix_in['w_out'], 'L1_mix_b_out': _L1_mix_in['b_out'], 'L1_mix_ln_scale': _L1_mix_in['ln_scale'], 'L1_ffn_router_w': _L1_ffn_in['router_w'], 'L1_ffn_W1': _L1_ffn_in['W1'], 'L1_ffn_b1': _L1_ffn_in['b1'], 'L1_ffn_W2': _L1_ffn_in['W2'], 'L1_ffn_b2': _L1_ffn_in['b2']}

def reference(x, src, dst, edge_attr_4, edge_attr_8, L0_gnn_W_up0, L0_gnn_W_up1, L0_gnn_W_mlp1, L0_gnn_W_mlp2, L0_gnn_W_mlp3, L0_gnn_W_mlp4, L0_gnn_W_out0, L0_gnn_W_out1, L0_mix_Wq, L0_mix_bq, L0_mix_Wk, L0_mix_bk, L0_mix_Wv, L0_mix_bv, L0_mix_Wl, L0_mix_bl, L0_ffn_ln_g, L0_ffn_ln_b, L0_ffn_w_r, L0_ffn_b_r, L0_ffn_W1, L0_ffn_b1, L0_ffn_W2, L0_ffn_b2, L1_gnn_W1, L1_gnn_b1, L1_gnn_W2, L1_gnn_b2, L1_mix_w_qkv, L1_mix_w_out, L1_mix_b_out, L1_mix_ln_scale, L1_ffn_router_w, L1_ffn_W1, L1_ffn_b1, L1_ffn_W2, L1_ffn_b2):
    import jax
    import jax.numpy as jnp

    def _L0_gnn_ref(node_feats, edge_attrs, edge_feats, edge_index, W_up0, W_up1, W_mlp1, W_mlp2, W_mlp3, W_mlp4, W_out0, W_out1):
        import jax, jax.numpy as jnp
        import numpy as np
        MUL = 128
        N_NODES = 1250
        N_EDGES = 20000
        R_BASIS = 8
        HIDDEN = 64
        W_NUMEL = 4 * MUL
        SQRT3 = 3.0 ** 0.5
        SILU_2MOM = 1.679177
        AVG_NUM_NEIGHBORS = 10.0

        def _lin_irreps(x0, x1, W0, W1):
            y0 = x0 @ W0 / jnp.sqrt(jnp.float32(W0.shape[0]))
            y1 = jnp.einsum('num,uv->nvm', x1, W1) / jnp.sqrt(jnp.float32(W1.shape[0]))
            return (y0, y1)

        def _forward(node_feats, edge_attrs, edge_feats, edge_index, W_up0, W_up1, W_mlp1, W_mlp2, W_mlp3, W_mlp4, W_out0, W_out1):
            num_nodes = node_feats.shape[0]
            sender, receiver = (edge_index[0], edge_index[1])
            x0 = node_feats[:, :MUL]
            x1 = node_feats[:, MUL:].reshape(num_nodes, MUL, 3)
            x0, x1 = _lin_irreps(x0, x1, W_up0, W_up1)
            h = edge_feats
            for W in (W_mlp1, W_mlp2, W_mlp3):
                h = SILU_2MOM * jax.nn.silu(h @ W / jnp.sqrt(jnp.float32(W.shape[0])))
            tpw = h @ W_mlp4 / jnp.sqrt(jnp.float32(W_mlp4.shape[0]))
            w1, w2, w3, w4 = jnp.split(tpw, 4, axis=-1)
            s0 = x0[sender]
            s1 = x1[sender]
            y0 = edge_attrs[:, 0:1]
            y1 = edge_attrs[:, 1:4]
            p1 = w1 * s0 * y0
            p2 = (w2 * s0)[:, :, None] * y1[:, None, :]
            p3 = w3[:, :, None] * s1 * y0[:, None, :]
            p4 = w4 * jnp.einsum('eum,em->eu', s1, y1) / SQRT3
            m0 = jnp.concatenate([p1, p4], axis=-1)
            m1 = jnp.concatenate([p2, p3], axis=1)
            msg0 = jax.ops.segment_sum(m0, receiver, num_segments=num_nodes)
            msg1 = jax.ops.segment_sum(m1, receiver, num_segments=num_nodes)
            o0, o1 = _lin_irreps(msg0, msg1, W_out0, W_out1)
            out = jnp.concatenate([o0, o1.reshape(num_nodes, 3 * MUL)], axis=-1)
            return out / AVG_NUM_NEIGHBORS
        return _forward(node_feats, edge_attrs, edge_feats, edge_index, W_up0, W_up1, W_mlp1, W_mlp2, W_mlp3, W_mlp4, W_out0, W_out1)

    def _L0_mix_ref(x, Wq, bq, Wk, bk, Wv, bv, Wl, bl):
        import jax, jax.numpy as jnp
        import numpy as np
        import math
        H_DIM = 512
        QKV_DIM = 512
        NUM_HEADS = 8
        HEAD_DIM = QKV_DIM // NUM_HEADS
        B, S = (4, 1024)

        def _split_heads(t):
            Bn, Sn, _ = t.shape
            return t.reshape(Bn, Sn, NUM_HEADS, HEAD_DIM).transpose(0, 2, 1, 3)
        q = _split_heads(x @ Wq.T + bq)
        k = _split_heads(x @ Wk.T + bk)
        v = _split_heads(x @ Wv.T + bv)
        seq_len = q.shape[2]
        kv = jnp.einsum('bhsd,bhse->bhde', k, v) * (1.0 / math.sqrt(seq_len))
        out = jnp.einsum('bhsd,bhde->bhse', q, kv)
        out = out.transpose(0, 2, 1, 3).reshape(x.shape[0], seq_len, QKV_DIM)
        return out @ Wl.T + bl

    def _L0_ffn_ref(x, ln_g, ln_b, w_r, b_r, W1, b1, W2, b2):
        import jax, jax.numpy as jnp
        import numpy as np
        D = 512
        E = 8
        K = 2
        EXP = 4
        LN_EPS = 1e-05
        B, T, d = x.shape
        mu = jnp.mean(x, axis=-1, keepdims=True)
        var = jnp.mean(jnp.square(x - mu), axis=-1, keepdims=True)
        h = (x - mu) * jax.lax.rsqrt(var + LN_EPS) * ln_g + ln_b
        logits = jnp.einsum('btd,ed->bte', h, w_r) + b_r
        topk_vals, topk_idx = jax.lax.top_k(logits, K)
        gates = jax.nn.softmax(topk_vals, axis=-1)
        hf = h.reshape(B * T, d)
        hid = jax.nn.gelu(jnp.einsum('nd,edf->nef', hf, W1) + b1, approximate=False)
        expert_stack = jnp.einsum('nef,efd->ned', hid, W2) + b2
        idx_flat = topk_idx.reshape(B * T, K)
        gates_flat = gates.reshape(B * T, K)
        gathered = jnp.take_along_axis(expert_stack, idx_flat[:, :, None], axis=1)
        mixed = jnp.sum(gathered * gates_flat[:, :, None], axis=1).reshape(B, T, d)
        return x + mixed

    def _L1_gnn_ref(x, edge_index, W1, b1, W2, b2):
        import jax, jax.numpy as jnp
        import numpy as np
        N_NODES = 1250

        def gcn_conv(x, edge_index, W, b):
            n = x.shape[0]
            loop = jnp.arange(n)
            src = jnp.concatenate([edge_index[0], loop])
            dst = jnp.concatenate([edge_index[1], loop])
            deg = jax.ops.segment_sum(jnp.ones_like(dst, dtype=x.dtype), dst, num_segments=n)
            dinv = jnp.where(deg > 0, jax.lax.rsqrt(deg), 0.0)
            norm = dinv[src] * dinv[dst]
            h = x @ W
            msg = h[src] * norm[:, None]
            out = jax.ops.segment_sum(msg, dst, num_segments=n)
            return out + b
        h = jax.nn.relu(gcn_conv(x, edge_index, W1, b1))
        h = jax.nn.relu(gcn_conv(h, edge_index, W2, b2))
        return h

    def _L1_mix_ref(x, w_qkv, w_out, b_out, ln_scale):
        import jax, jax.numpy as jnp
        import numpy as np
        HEADS = 8
        DIM_HEAD = 64
        LN_EPS = 1e-05
        B, N, C = x.shape
        H, D = (HEADS, DIM_HEAD)
        qkv = jnp.einsum('bnc,cf->bnf', x, w_qkv)
        q, k, v = jnp.split(qkv, 3, axis=-1)
        q = q.reshape(B, N, H, D)
        k = k.reshape(B, N, H, D)
        v = v.reshape(B, N, H, D)
        q = jax.nn.softmax(q, axis=-1)
        k = jax.nn.softmax(k, axis=1)
        q = q / jnp.sqrt(jnp.asarray(D, dtype=q.dtype))
        v = v / N
        context = jnp.einsum('bnhd,bnhe->bhde', k, v)
        out = jnp.einsum('bhde,bnhd->bhen', context, q)
        out = out.transpose(0, 3, 1, 2).reshape(B, N, H * D)
        out = jnp.einsum('bnf,fc->bnc', out, w_out) + b_out
        mu = jnp.mean(out, axis=-1, keepdims=True)
        var = jnp.mean(jnp.square(out - mu), axis=-1, keepdims=True)
        out = (out - mu) * jax.lax.rsqrt(var + LN_EPS) * ln_scale
        return out

    def _L1_ffn_ref(x, router_w, W1, b1, W2, b2):
        import jax, jax.numpy as jnp
        import numpy as np
        N_CONST = 6
        PARTITIONS_OF_6 = [(6,), (5, 1), (4, 2), (4, 1, 1), (3, 3), (3, 2, 1), (3, 1, 1, 1), (2, 2, 2), (2, 2, 1, 1), (2, 1, 1, 1, 1), (1, 1, 1, 1, 1, 1)]
        N_EXPERTS = 6
        TOP_K = 2

        def _partition_weights():
            w = np.zeros((len(PARTITIONS_OF_6), N_EXPERTS), dtype=np.float32)
            for i, partition in enumerate(PARTITIONS_OF_6):
                for j, part in enumerate(partition):
                    if j < N_EXPERTS:
                        w[i, j] = part / N_CONST
            return jnp.asarray(w)
        pw = _partition_weights()
        token_repr = x.mean(axis=1)
        logits = token_repr @ router_w.T
        probs = jax.nn.softmax(logits, axis=-1)
        topk_vals, topk_idx = jax.lax.top_k(probs, TOP_K)
        topk_vals = topk_vals / topk_vals.sum(axis=-1, keepdims=True)
        expert_weights = jnp.einsum('bk,bke->be', topk_vals, pw[topk_idx])
        expert_weights = jnp.where(expert_weights > 1e-06, expert_weights, 0.0)
        h = jax.nn.gelu(jnp.einsum('bsd,edf->ebsf', x, W1) + b1[:, None, None, :], approximate=False)
        out_e = jnp.einsum('ebsf,efd->ebsd', h, W2) + b2[:, None, None, :]
        return jnp.einsum('be,ebsd->bsd', expert_weights, out_e)
    edge_index = jnp.stack([src, dst])
    xn = _layernorm(x, axis=-1)
    x = x + _L0_gnn_ref(xn, edge_attr_4, edge_attr_8, edge_index, L0_gnn_W_up0, L0_gnn_W_up1, L0_gnn_W_mlp1, L0_gnn_W_mlp2, L0_gnn_W_mlp3, L0_gnn_W_mlp4, L0_gnn_W_out0, L0_gnn_W_out1) + _L0_mix_ref(xn[None], L0_mix_Wq, L0_mix_bq, L0_mix_Wk, L0_mix_bk, L0_mix_Wv, L0_mix_bv, L0_mix_Wl, L0_mix_bl)[0]
    x = x + _L0_ffn_ref(_layernorm(x, axis=-1)[None], L0_ffn_ln_g, L0_ffn_ln_b, L0_ffn_w_r, L0_ffn_b_r, L0_ffn_W1, L0_ffn_b1, L0_ffn_W2, L0_ffn_b2)[0]
    xn = _layernorm(x, axis=-1)
    x = x + _L1_gnn_ref(xn, edge_index, L1_gnn_W1, L1_gnn_b1, L1_gnn_W2, L1_gnn_b2) + _L1_mix_ref(xn[None], L1_mix_w_qkv, L1_mix_w_out, L1_mix_b_out, L1_mix_ln_scale)[0]
    x = x + _L1_ffn_ref(_layernorm(x, axis=-1)[None], L1_ffn_router_w, L1_ffn_W1, L1_ffn_b1, L1_ffn_W2, L1_ffn_b2)[0]
    return x

_drawn_inputs = setup_inputs


def setup_inputs(seed=0):
    import zlib

    import numpy as np

    out = dict(_drawn_inputs(seed))
    spreads = {'L0_ffn_ln_g': (1.0, 0.6),
     'L0_ffn_ln_b': (0.0, 0.8),
     'L0_ffn_b_r': (0.0, 2.0),
     'L0_ffn_b1': (0.0, 0.8),
     'L0_ffn_b2': (0.0, 0.8),
     'L1_gnn_b1': (0.0, 0.8),
     'L1_gnn_b2': (0.0, 2.0)}
    factors = {'L0_gnn_W_out0': 2.81,
     'L0_mix_bq': 6.472,
     'L0_mix_bk': 8.0,
     'L0_mix_bv': 8.0,
     'L0_mix_bl': 58.166,
     'L0_ffn_w_r': 2.921,
     'L0_ffn_W1': 2.862,
     'L1_gnn_W1': 8.0,
     'L1_gnn_W2': 8.0,
     'L1_mix_w_qkv': 8.0,
     'L1_mix_w_out': 8.0,
     'L1_mix_ln_scale': 62.387,
     'L1_ffn_router_w': 8.0,
     'L1_ffn_W1': 3.125,
     'L1_ffn_b1': 64.0,
     'L1_ffn_W2': 2.791,
     'L1_ffn_b2': 64.0}
    for name, (base, spread) in spreads.items():
        noise = np.random.default_rng([zlib.crc32(name.encode()), seed]).standard_normal(out[name].shape)
        drawn = base * np.exp(spread * noise) if base else spread * noise
        out[name] = jnp.asarray(drawn.astype(out[name].dtype))
    for name, factor in factors.items():
        out[name] = (out[name] * factor).astype(out[name].dtype)
    return out
```

```python
import math
from contextlib import ExitStack

import concourse.bass as bass
from concourse import mybir

P = 128
F32 = mybir.dt.float32
BF16 = mybir.dt.bfloat16
F16 = mybir.dt.float16
F32R = mybir.dt.float32r
I32 = mybir.dt.int32
ALU = mybir.AluOpType
ACT = mybir.ActivationFunctionType
AX_X = mybir.AxisListType.X
RMAX = bass.bass_isa.ReduceOp.max

SILU_2MOM = 1.679177
AVG_NUM_NEIGHBORS = 10.0
LN_EPS = 1e-5


class BankRing:

    def __init__(self, banks):
        self.banks, self.n, self.at = banks, 0, {}

    def plan(self, keys):
        for key in keys:
            self.at[key] = (self.n % self.banks, self.n // self.banks)
            self.n += 1

    def uses(self, bank):
        return self.n // self.banks + (self.n % self.banks > bank)


def graph_block_kernel(nc, A, out):
    N, D = A["x"].shape
    E = A["src"].shape[0]
    NT = -(-N // P)
    NP = NT * P
    C = D // P
    MUL = A["L0_gnn_W_up0"].shape[0]
    HID = A["L0_gnn_W_mlp2"].shape[0]
    R = A["edge_attr_8"].shape[1]
    Y = A["edge_attr_4"].shape[1]
    J = 4
    U = J * P
    UNITS = -(-E // U)
    FULL = E // U
    PAIRS = 2
    TURNS = -(-UNITS // (2 * PAIRS))
    EPAD = TURNS * 2 * PAIRS * U
    HEADS, HD = 8, D // 8

    def rows(t):
        return min(P, N - t * P)

    ctx = ExitStack()
    with ctx:
        def sb(name, shape, dt=F32):
            return ctx.enter_context(nc.sbuf_tensor(name, shape, dt))

        def sem(name):
            return ctx.enter_context(nc.semaphore(name))

        def dram(name, shape, dt=F32):
            return nc.dram_tensor(name, shape, dt).ap()

        sender_table = dram("sender_table", (NP, D))
        edge_in = dram("edge_in", (EPAD, R))
        edge_hidden = dram("edge_hidden", (2, TURNS * 2 * PAIRS, 2, P, P))

        ident = sb("ident", [P, P])
        table = sb("table", [P, NP])
        iota_nodes = table[:, 0:NP // 2].bitcast(F16)
        assert NP <= 2048
        block_lo = sb("block_lo", [P, NT])
        unit_id = sb("unit_id", [P, 1])
        zeros16 = sb("zeros16", [P, D], BF16)
        x_rows = sb("x_rows", [P, NT, D])
        xn_T = sb("xn_T", [P, C, NP])
        stats = sb("stats", [P, NT, 6])
        meanvar = sb("meanvar", [P, NT, 2])
        rstd = sb("rstd", [P, NT])
        big_a = sb("big_a", [P, NT * NP])
        big_b = sb("big_b", [P, NT * NP])
        ln_rows = big_a[:, 0:NT * D].rearrange("p (t d) -> p t d", d=D)
        sender_rows = big_a[:, NT * D:2 * NT * D].rearrange("p (t d) -> p t d", d=D)
        k_rows = big_b[:, 0:NT * D].rearrange("p (t d) -> p t d", d=D)
        v_rows = big_b[:, NT * D:2 * NT * D].rearrange("p (t d) -> p t d", d=D)
        adj_rows = big_a[:, :].rearrange("p (t n) -> p t n", n=NP)
        msg_rows = big_b[:, 0:NT * 2 * D].rearrange("p (t d) -> p t d", d=2 * D)

        with ExitStack() as overlay:
            def sb_r(name, shape):
                return overlay.enter_context(nc.sbuf_tensor(name, shape, F32R))

            h3_hi = [sb_r(f"h3_hi{a}", [P, 2, 2, P]) for a in range(PAIRS)]
            h3_lo = [sb_r(f"h3_lo{a}", [P, 2, 2, P]) for a in range(PAIRS)]
            h3_slot = [sb_r(f"h3_slot{q}", [P, 2, P]) for q in range(2)]
            w4_hi = sb_r("w4_hi", [P, 4 * MUL])
            w4_lo = sb_r("w4_lo", [P, 4 * MUL])
        OVERLAY = 4 * 4 * P + 2 * 2 * P + 2 * 4 * MUL
        wide = sb("wide", [P, 5 * C * D])

        def weight(region, i):
            return region[:, i * C * D:(i + 1) * C * D].rearrange("p (c d) -> p c d", d=D)

        spare_a, spare_b = big_a[:, 2 * NT * D:], big_b[:, 2 * NT * D:]
        w_rows = {"Wk": weight(wide, 0), "Wv": weight(wide, 1), "Wl": weight(wide, 2), "Wq": weight(big_a, 0)}
        w_T = {"Wk": weight(wide, 3), "Wv": weight(wide, 4), "Wl": weight(spare_a, 0)}
        m2, m3 = weight(wide, 0), weight(wide, 1)
        mix_bias = sb("mix_bias", [P, D])
        w_up = sb("w_up", [P, 2, MUL])
        bq_col = sb("bq_col", [P, C])
        b_row = {n: sb(f"{n}_row", [P, D]) for n in ("bk", "bv", "bl")}
        kv_T = sb("kv_T", [P, C, P])
        w_mlp1 = sb("w_mlp1", [J * R, 2, 2 * HID])
        w_mlp2 = sb("w_mlp2", [P, P])
        w_mlp3 = sb("w_mlp3", [P, P])
        w_mlp4 = sb("w_mlp4", [P, 4 * MUL])
        w_out = sb("w_out", [P, 2, 2, MUL])

        dst_units = big_b[0:UNITS, 0:U].bitcast(I32)
        dst_unitf = big_b[0:UNITS, U:2 * U]
        unit_max = sb("unit_max", [UNITS, 1])
        unit_min = sb("unit_min", [UNITS, 1])
        touch = sb("touch", [UNITS, 4, NT])
        reach = sb("reach", [UNITS, 2 * NT])
        reach_all = sb("reach_all", [UNITS, 2 * NT])
        span_f = sb("span_f", [1, 2, NT])
        span = sb("span", [1, 2, NT], I32)
        dst_int = sb("dst_int", [P, UNITS, J], I32)
        src_int = sb("src_int", [P, UNITS, J], I32)
        edges = spare_b[:, 0:UNITS * J * (Y + 2)].rearrange("p (u k) -> p u k", u=UNITS)
        class Space:
            def __init__(self, region):
                self.region, self.used = region, 0

            def take(self, n):
                self.used += n
                return self.region[:, self.used - n:self.used]

        mlp_space = Space(wide[:, OVERLAY:])
        ea_slot = [mlp_space.take(2 * J * R).rearrange("p (h k) -> p h k", h=2) for a in range(PAIRS)]
        ea_T = [mlp_space.take(2 * P)[0:J * R, :] for a in range(PAIRS)]
        h_slot = [mlp_space.take(4 * P) for a in range(PAIRS)]
        h3_out = [mlp_space.take(4 * P).rearrange("p (u q n) -> p u q n", u=2, q=2) for a in range(PAIRS)]
        edge_space = Space(xn_T[:, :, :].rearrange("p c n -> p (c n)")[:, 2 * D:])
        edge_slot = edge_space.take(J * (Y + 2))
        idx_slot = [sb(f"idx_slot{j}", [P, 1], I32) for j in range(J)]
        sent = [edge_space.take(D) for j in range(J)]
        hot_f = edge_space.take(2 * P).rearrange("p (k n) -> p k n", k=2)
        hot_y = edge_space.take(2 * Y * P).rearrange("p (k y n) -> p k y n", k=2, y=Y)
        dot = edge_space.take(2 * MUL).rearrange("p (k n) -> p k n", k=2)
        edge_space2 = Space(wide[:, OVERLAY:])
        scaled = edge_space2.take(2 * 3 * MUL).rearrange("p (k m u) -> p k m u", k=2, m=3)
        prod = edge_space2.take(2 * 6 * MUL).rearrange("p (k n) -> p k n", k=2)
        hot_dst = edge_space2.take(P).bitcast(BF16).rearrange("p (k n) -> p k n", k=2)
        hot_src = edge_space2.take(NP).bitcast(BF16).rearrange("p (k n) -> p k n", k=2)
        msg_T = edge_space2.take(4 * D).rearrange("p (k n) -> p k n", k=2)
        assert edge_space.used <= C * NP - 2 * D and max(mlp_space.used, edge_space2.used) <= 5 * C * D - OVERLAY

        psum = ctx.enter_context(nc.psum_tensor("psum", [P, 8, 512], F32))
        msg_psum = psum[:, 0:2, :].rearrange("p k n -> p (k n)")
        adj_psum = psum[:, 2:5, :].rearrange("p k n -> p (k n)")
        tile_w = [psum[:, 5 + k, :] for k in range(2)]
        ring = BankRing(8)

        ring.plan([("wT", w, c) for w in ("Wk", "Wv", "Wl") for c in range(C)])
        ring.plan([("xT", t) for t in range(NT)])
        ring.plan([("sender", t) for t in range(NT)])
        ring.plan([(w, t) for t in range(NT) for w in ("Wk", "Wv")])
        ring.plan([("kvT",)])
        ring.plan([("m2", c) for c in range(C)])
        ring.plan([("m3", c) for c in range(C)] + [("mix_bias",)])
        ring.plan([("mix", t) for t in range(NT)])
        before_edges = [ring.uses(b) for b in range(8)]
        ring.plan([(k, t) for t in range(NT) for k in ("msgT0", "msgT1", "conv")])

        bank_full = [sem(f"bank_full{b}") for b in range(8)]
        bank_free = [sem(f"bank_free{b}") for b in range(8)]
        loads = {}

        def load_sem(name):
            loads[name] = sem(f"{name}_loaded")
            return loads[name]

        for n in ("x", "w_up", "Wk", "Wv", "Wl", "Wq", "bq", "bk", "bv", "bl", "mlp", "w_out", "dst_units",
                  "edge_tables", "edge_in"):
            load_sem(n)
        consts_ready = sem("consts_ready")
        ident_zeroed = sem("ident_zeroed")
        padding_ready = sem("padding_ready")
        dve_step = sem("dve_step")
        stats_ready = sem("stats_ready")
        std_ready = sem("std_ready")
        ln_ready = [sem(f"ln_ready{n}") for n in range(7)]
        gathers_started = sem("gathers_started")
        sender_stored = sem("sender_stored")
        bq_ready = sem("bq_ready")
        reach_ready = sem("reach_ready")
        reach_max_ready = sem("reach_max_ready")
        span_ready = sem("span_ready")
        ea_loaded = [sem(f"ea_loaded{a}") for a in range(PAIRS)]
        ea_transposed = [sem(f"ea_transposed{a}") for a in range(PAIRS)]
        ea_T_ready = [sem(f"ea_T_ready{a}") for a in range(PAIRS)]
        layer_done = [sem(f"layer_done{a}") for a in range(PAIRS)]
        silu_done = [sem(f"silu_done{a}") for a in range(PAIRS)]
        h3_stored = [sem(f"h3_stored{a}") for a in range(PAIRS)]
        h3_out_free = [sem(f"h3_out_free{a}") for a in range(PAIRS)]
        h3_split = [sem(f"h3_split{a}") for a in range(PAIRS)]
        h3_loaded = [sem(f"h3_loaded{q}") for q in range(2)]
        w4_ready = sem("w4_ready")
        hi_ready = [sem(f"hi_ready{a}") for a in range(PAIRS)]
        dot_ready = sem("dot_ready")
        hot_ready = sem("hot_ready")
        hot_y_ready = sem("hot_y_ready")
        scaled_ready = sem("scaled_ready")
        weights_done = sem("weights_done")
        scatter_done = sem("scatter_done")
        products_done = sem("products_done")
        edge_slot_ready = sem("edge_slot_ready")
        gathered = [sem(f"gathered{j}") for j in range(J)]
        idx_ready = sem("idx_ready")
        msg_flushed = sem("msg_flushed")
        adj_flushed = sem("adj_flushed")
        out_stored = sem("out_stored")

        EX = A["L0_ffn_w_r"].shape[0]
        TOP = 2
        FH = A["L0_ffn_W1"].shape[2]
        FC = FH // P
        TILES = (TOP * N + EX * P) // P
        H1 = A["L1_gnn_b1"].shape[0]
        HC = H1 // P
        SE, SF = A["L1_ffn_b1"].shape
        SC = -(-SE * SF // P)
        PARTS = A["L1_ffn_router_w"].shape[0]
        GROUPS = [(g, min(512, NP - g)) for g in range(0, NP, 512)]
        KEY_COLS = [min(w, N - g) for g, w in GROUPS]

        adj_dram = dram("adj_dram", (P, NT, NP))
        tokens_sorted = dram("tokens_sorted", ((TILES + 1) * P, D))
        mixed_sorted = dram("mixed_sorted", (TILES * P, D))

        late = Space(table[:, 16:])
        late_dst = Space(dst_int[:, :, :].rearrange("p u j -> p (u j)").bitcast(F32))
        late_src = Space(src_int[:, :, :].rearrange("p u j -> p (u j)").bitcast(F32))
        ident16 = sb("ident16", [P, P], BF16)
        before_me = late_src.take(P)
        ones_col = sb("ones_col", [P, 1])
        real_row = sb("real_row", [P, 1])
        degree = sb("degree", [P, NT])
        dinv = sb("dinv", [P, NT])
        bias_rows = late_src.take(P)[0:HC + SC, :]
        bias_T = late.take(HC + SC)
        expert_bias_T = late.take(EX * FC)
        expert_b2 = w_mlp4[0:EX, :]
        routers_T = late.take(C * (EX + PARTS)).rearrange("p (a b) -> p a b", b=(EX + PARTS))
        router_bias = sb("router_bias", [P, EX])
        logits = late.take(NT * EX).rearrange("p (a b) -> p a b", b=EX)
        top_val = late.take(NT * 8).rearrange("p (a b) -> p a b", b=8)
        top_idx = late.take(NT * 8).bitcast(mybir.dt.uint32).rearrange("p (a b) -> p a b", b=8)
        choice_f = late.take(TOP * NT).rearrange("p (a b) -> p a b", b=NT)
        chosen = late.take(TOP * NT * EX).rearrange("p (k a b) -> p k a b", k=TOP, b=EX)
        member = late.take(NT * EX).rearrange("p (a b) -> p a b", b=EX)
        members_before = late.take((NT + 1) * EX).rearrange("p (a b) -> p a b", b=EX)
        place = late_dst.take(NT * EX).rearrange("p (a b) -> p a b", b=EX)
        tile_tests = late_dst.take(EX * NT).rearrange("p (a b) -> p a b", b=NT)
        first_tile = late.take(EX + 1)
        expert_tiles = late.take(EX)
        place_base = late.take(EX)
        first_tile_int = late.take(EX + 1)[0:1, :].bitcast(I32)
        slot_f = late.take(TOP * NT).rearrange("p (a b) -> p a b", b=NT)
        slot_int = late.take(TOP * NT).bitcast(I32).rearrange("p (a b) -> p a b", b=NT)
        gate = late.take(TOP * NT).rearrange("p (a b) -> p a b", b=NT)
        gap = late.take(NT)
        var2 = late.take(NT)
        rstd2 = late.take(NT)

        xn_flat = xn_T[:, :, :].rearrange("p c n -> p (c n)")
        router_rows = xn_flat[0:EX + PARTS, 0:D]
        expert_bias_rows = xn_flat[:, D:D + P]
        def grid(region, a, b, k):
            return region[:, a:a + b * k].rearrange("p (a k) -> p a k", k=k)

        adj_T = grid(big_b, 0, NT, NP)
        h0_rows = grid(wide, 0, NT, D)
        hx_rows = grid(wide, NT * D, NT, D)
        spare_x = FC * P + 3 * D
        gates_T = xn_flat[0:EX, spare_x:spare_x + NP]
        token_gates = grid(xn_flat, spare_x + NP, NT, EX)
        HALF = FC // 2
        ew1 = [grid(r, 0, C, FH) for r in (big_a, big_b)]
        ew2_lo = [grid(r, C * FH, HALF, D) for r in (big_a, big_b)]
        ew2_hi = [grid(wide, a * HALF * D, HALF, D) for a in range(2)]
        hid = grid(xn_flat, 0, FC, P)
        tile_rows = xn_flat[:, FC * P:FC * P + D]
        tile_T = grid(xn_flat, FC * P + D, C, P)
        tile_out = xn_flat[:, FC * P + 2 * D:FC * P + 3 * D]
        mixed = big_a[:, 0:TOP * NT * D].rearrange("p (t k d) -> p t k d", k=TOP, d=D)
        xn2_rows = grid(wide, 0, NT, D)
        z_rows = grid(wide, NT * D, NT, D)
        ah_T = grid(big_a, 0, C, NP)
        ah_rows = grid(big_a, NT * D, 2, D)
        gw1 = grid(big_a, (NT + 2) * D, C, H1)
        h1_T = grid(wide, 0, HC, NP)
        GW2_FIRST = 5
        gw2 = [big_a[:, (NT + 2) * D + C * H1 + i * D:(NT + 2) * D + C * H1 + (i + 1) * D] for i in range(GW2_FIRST)]
        gw2 += [big_a[:, i * D:(i + 1) * D] for i in range(HC - GW2_FIRST)]
        z2_rows = grid(big_a, (HC - GW2_FIRST) * D, NT, D)
        conv_out = grid(big_a, (HC - GW2_FIRST + NT) * D, 2, D)
        w_qkv = grid(wide, 0, C, 3 * D)
        w_att = grid(wide, 3 * C * D, C, D)
        m5 = grid(wide, 4 * C * D, C, D)
        EK = (HC - GW2_FIRST + NT) * D
        ek_T = grid(big_a, EK, C, NP)
        q_T = ek_T
        ek_rows = grid(big_a, 0, NT, D)
        q_rows = grid(big_b, 0, NT, D)
        att_rows = q_rows
        vx_rows = grid(big_b, NT * D, NT, D)
        k_max3 = late.take(C * len(GROUPS)).rearrange("p (a b) -> p a b", b=len(GROUPS))
        k_max = late.take(C)
        k_sum = late.take(C)
        k_scale = late.take(C)
        q_max = late.take(HEADS)
        q_sum = late.take(2 * HEADS).rearrange("p (a h) -> p a h", a=2)
        last_rows = vx_rows
        sw1 = wide[:, 0:C * SE * SF].rearrange("p (c e f) -> p c e f", c=C, e=SE)
        sw1_cols = wide[:, 0:C * SE * SF].rearrange("p (c h) -> p c h", c=C)
        SW2_FIRST = EK // D
        sw2 = [big_a[:, j * D:(j + 1) * D] for j in range(SW2_FIRST)]
        sw2 += [big_b[:, (2 * NT + j) * D:(2 * NT + j + 1) * D] for j in range(SC - SW2_FIRST)]
        UP_BANKS, Y_BANK, T_BANK = 4, 4, 5
        TG = 2 * P
        shid = [big_b[:, a * SC * TG:(a + 1) * SC * TG].rearrange("p (j n) -> p j n", n=TG) for a in range(2)]
        mean_col = late.take(C)
        route = late.take(PARTS)[0:1, :]
        route_top = late.take(8)[0:1, :]
        route_idx = late.take(8)[0:1, :].bitcast(mybir.dt.uint32)
        route_f = late.take(8)[0:1, :]
        route_coef = late.take(2 * PARTS)[0:1, :].rearrange("p (a b) -> p a b", b=PARTS)
        part_weights = late_src.take(SE * PARTS)[0:1, :].rearrange("p (a b) -> p a b", b=PARTS)
        part_prod = late.take(SE * PARTS)[0:1, :].rearrange("p (a b) -> p a b", b=PARTS)
        expert_w = late.take(2 * SE)[0:1, :].rearrange("p (a b) -> p a b", b=SE)
        expert_w_all = late.take(SE)
        expert_w_col = late.take(1)[0:SE, :]
        hidden_id = sb("hidden_id", [P, SC])
        past = late_dst.take((SE + 1) * SC).rearrange("p (a b) -> p a b", b=SC)
        hidden_w = late.take(SC)

        def hidden_rows(j):
            return min(P, SE * SF - j * P)

        ring.plan([("routersT",), ("expert_biasT",)])
        ring.plan([("adjT", s, g) for s in range(NT) for g in range(len(GROUPS))])
        ring.plan([("hT", t) for t in range(NT)] + [("logits",), ("rank",)])
        ring.plan([("gateT", g) for g in range(len(GROUPS))] + [("b2", t) for t in range(NT)] + [("biasT",)])
        before_experts = [ring.uses(b) for b in range(8)]
        ring.plan([("xn2T", t) for t in range(NT)])
        ring.plan([("agg1", 0)] + [k for t in range(1, NT) for k in (("agg1", t), ("ahT", t - 1))] + [("ahT", NT - 1)])
        ring.plan([("h1T", f, g) for f in range(HC) for g in range(len(GROUPS))])
        ring.plan([(k, t) for k in ("y2", "agg2") for t in range(NT)])
        ring.plan([("kT", m, g) for m in range(C) for g in range(len(GROUPS))])
        ring.plan([("q", t) for t in range(NT)] + [("v", t) for t in range(NT)] + [("ek", t) for t in range(NT)])
        ring.plan([("ctxT",)] + [("m5", c) for c in range(C)])
        ring.plan([("qT", t) for t in range(NT)] + [("att", t) for t in range(NT)])
        ring.plan([("lastT", t) for t in range(NT)])
        ring.plan([("route",), ("expert_w",), ("b2_mix",)])
        TURN_TILES = [[t for t in range(g, min(g + TG // P, NT))] for g in range(0, NT, TG // P)]
        TG_N = len(TURN_TILES)

        def ffn_order():
            for g in range(TG_N + 1):
                if g < TG_N:
                    yield from [("up", g, j) for j in range(SC)]
                if g:
                    yield from [("down", t) for t in TURN_TILES[g - 1]]
        ring.plan(list(ffn_order()))

        for n in ("routers", "router_bias", "expert_bias", "biases", "ln_g", "ln_b", "gnn_b2", "expert_b2", "adj_T",
                  "gw1", "gw2_first", "gw2_last", "w_qkv", "w_att", "b_out", "ln_scale", "shared_b2", "sw1", "sw2"):
            load_sem(n)
        adj_stored = sem("adj_stored")
        tokens_zeroed = sem("tokens_zeroed")
        members_ready = sem("members_ready")
        gap_ready = sem("gap_ready")
        gap_exp = sem("gap_exp")
        gates_ready = sem("gates_ready")
        tiles_ready = sem("tiles_ready")
        slots_ready = sem("slots_ready")
        dinv_ready = sem("dinv_ready")
        z_ready = sem("z_ready")
        degree_ready = sem("degree_ready")
        degree_root = sem("degree_root")
        rows_scattered = sem("rows_scattered")
        ew1_loaded = [sem(f"ew1_loaded{a}") for a in range(2)]
        ew2_loaded = [sem(f"ew2_loaded{a}") for a in range(2)]
        tile_loaded = sem("tile_loaded")
        tile_transposed = sem("tile_transposed")
        tile_T_ready = sem("tile_T_ready")
        up_done = sem("up_done")
        gelu_done = sem("gelu_done")
        down_done = sem("down_done")
        tile_out_ready = sem("tile_out_ready")
        tile_stored = sem("tile_stored")
        mixed_zeroed = sem("mixed_zeroed")
        tile_out_free = sem("tile_out_free")
        experts_started = sem("experts_started")
        mixed_loaded = [sem(f"mixed_loaded{t}") for t in range(NT)]
        k_max_ready = sem("k_max_ready")
        ek_ready = sem("ek_ready")
        k_scale_ready = sem("k_scale_ready")
        q_exp = sem("q_exp")
        q_ready = sem("q_ready")
        mean_ready = sem("mean_ready")
        route_exp = sem("route_exp")
        route_weighted = sem("route_weighted")
        hidden_w_ready = sem("hidden_w_ready")
        sw2_ready = sem("sw2_ready")

        def partitions(n, largest):
            if n == 0:
                yield ()
            for part in range(min(n, largest), 0, -1):
                for rest in partitions(n - part, part):
                    yield (part, *rest)

        block = ctx.enter_context(nc.Block())

        def bank(key):
            return psum[:, ring.at[key][0], :]

        def claim(pe, key):
            b, n = ring.at[key]
            if n:
                pe.wait_ge(bank_free[b], n)
            return psum[:, b, :], bank_full[b]

        def filled(eng, key):
            b, n = ring.at[key]
            eng.wait_ge(bank_full[b], n + 1)
            return psum[:, b, :], bank_free[b]

        def drained(eng, key):
            b, n = ring.at[key]
            eng.wait_ge(bank_free[b], n + 1)

        def block_span(eng, b):
            lo = eng.value_load(span[0:1, 0, bass.ds(b, 1)], min_val=0, max_val=UNITS - 1)
            hi = eng.value_load(span[0:1, 1, bass.ds(b, 1)], min_val=1, max_val=UNITS)
            return lo, hi

        def expert_span(eng, e):
            lo = eng.value_load(first_tile_int[0:1, bass.ds(e, 1)], min_val=0, max_val=TILES - 1)
            hi = eng.value_load(first_tile_int[0:1, bass.ds(e + 1, 1)], min_val=1, max_val=TILES)
            return lo, hi

        def step_counter(eng, name):
            step = eng.alloc_register(name)
            eng.reg_mov(step, 0)
            return step

        def next_step(eng, step):
            eng.reg_add(step, step, 1)
            return eng.snap(step, min_val=1, max_val=NT * UNITS)

        tile_cols = [slice(t * P, t * P + P) for t in range(NT)]
        comp = [slice(0, MUL)] + [slice(MUL + m, D, 3) for m in range(3)]
        PAD_DMAS = -(-(EPAD - E) // (D // 2 // R))
        TABLE_DMAS = 3 * (1 + ((E - FULL * U) // J > 0) + ((E - FULL * U) % J > 0))

        @block.sync
        def _(sp):
            sp.wait_ge(padding_ready, 1)
            sp.dma_start(x_rows[:, 0:NT - 1, :], A["x"][0:(NT - 1) * P, :].rearrange("(t p) d -> p t d", p=P))\
                .then_inc(loads["x"], 16)
            sp.dma_start(x_rows[0:rows(NT - 1), NT - 1, :], A["x"][(NT - 1) * P:N, :]).then_inc(loads["x"], 16)
            for w in ("Wk", "Wv", "Wl"):
                sp.dma_start(w_rows[w], A[f"L0_mix_{w}"].rearrange("(c p) d -> p c d", p=P)).then_inc(loads[w], 16)
            sp.dma_start(w_up[:, 0, :], A["L0_gnn_W_up0"]).then_inc(loads["w_up"], 16)
            sp.dma_start(w_up[:, 1, :], A["L0_gnn_W_up1"]).then_inc(loads["w_up"], 16)
            for b in ("bk", "bv", "bl"):
                sp.dma_start(b_row[b][:, :], A[f"L0_mix_{b}"].rearrange("(a d) -> a d", a=1).to_broadcast([P, D]))\
                    .then_inc(loads[b], 16)
            sp.dma_start(bq_col[:, :], A["L0_mix_bq"].rearrange("(c p) -> p c", p=P), allow_slow_non_contiguous=True).then_inc(loads["bq"], 16)
            split = math.gcd(E, 11 * 15 * 2)
            sp.dma_start(edge_in[0:E, :].rearrange("(a b) r -> a (b r)", a=split),
                         A["edge_attr_8"].rearrange("(a b) r -> a (b r)", a=split)).then_inc(loads["edge_in"], 16)
            sp.wait_ge(padding_ready, 2)
            zero_row = zeros16[0:1, :].bitcast(F32)
            for e0 in range(E, EPAD, D // 2 // R):
                n = min(D // 2 // R, EPAD - e0)
                sp.dma_start(edge_in[e0:e0 + n, :].rearrange("(a b) r -> a (b r)", a=1), zero_row[:, 0:n * R])\
                    .then_inc(loads["edge_in"], 16)
            sp.wait_ge(padding_ready, 3)
            for j in range(J):
                sp.dma_start(w_mlp1[R * j:R * j + R, j // 2, HID * (j % 2):HID * (j % 2) + HID], A["L0_gnn_W_mlp1"])\
                    .then_inc(loads["mlp"], 16)
            for j in range(2):
                half = slice(HID * j, HID * j + HID)
                sp.dma_start(w_mlp2[half, half], A["L0_gnn_W_mlp2"]).then_inc(loads["mlp"], 16)
                sp.dma_start(w_mlp3[half, half], A["L0_gnn_W_mlp3"]).then_inc(loads["mlp"], 16)
                sp.dma_start(w_mlp4[half, :], A["L0_gnn_W_mlp4"]).then_inc(loads["mlp"], 16)
            for k in range(2):
                sp.dma_start(w_out[:, k, :, :], A[f"L0_gnn_W_out{k}"].rearrange("(c p) v -> p c v", p=P))\
                    .then_inc(loads["w_out"], 16)
            for t in range(NT):
                drained(sp, ("xT", t))
            sp.dma_start(w_rows["Wq"], A["L0_mix_Wq"].rearrange("(c p) d -> p c d", p=P)).then_inc(loads["Wq"], 16)
            for t in range(NT):
                drained(sp, ("sender", t))
            sp.dma_start(sender_table.rearrange("(t p) d -> p t d", p=P), sender_rows).then_inc(sender_stored, 16)
            sp.wait_ge(loads["edge_in"], 16 * (1 + PAD_DMAS))
            with sp.Fori(0, TURNS) as i:
                for a in range(PAIRS):
                    sp.wait_ge(ea_transposed[a], i + 1)
                    sp.dma_start(ea_slot[a][:, :, :], edge_in.rearrange("(u p j) r -> u p (j r)", p=P, j=J)
                                 [bass.ds(i * (2 * PAIRS) + 2 * a, 2), :, :].rearrange("u p k -> p u k"))\
                        .then_inc(ea_loaded[a], 16)
            for h in range(2):
                sp.dma_start(tokens_sorted.rearrange("(t p) d -> p t d", p=P)[:, :, h * (D // 2):(h + 1) * (D // 2)],
                             zeros16[:, :].bitcast(F32).unsqueeze(1).to_broadcast([P, TILES + 1, D // 2])).then_inc(tokens_zeroed, 16)
            sure = -(-TOP * N // P)
            for h in range(2):
                sp.dma_start(mixed_sorted[sure * P:, :].rearrange("(t p) d -> p t d", p=P)[:, :, h * (D // 2):(h + 1) * (D // 2)],
                             zeros16[:, :].bitcast(F32).unsqueeze(1).to_broadcast([P, TILES - sure, D // 2])).then_inc(mixed_zeroed, 16)
            for t in range(NT):
                drained(sp, ("mix", t))
            sp.dma_start(router_rows[0:EX, :], A["L0_ffn_w_r"]).then_inc(loads["routers"], 16)
            sp.dma_start(router_rows[EX:EX + PARTS, :], A["L1_ffn_router_w"]).then_inc(loads["routers"], 16)
            sp.dma_start(expert_bias_rows, A["L0_ffn_b1"].rearrange("e (c f) -> (e c) f", f=P)).then_inc(loads["expert_bias"], 16)

            def spread(dst, name, what):
                sp.dma_start(dst, A[name].rearrange("(a d) -> a d", a=1).to_broadcast([P, A[name].shape[0]]))\
                    .then_inc(loads[what], 16)

            spread(router_bias[:, :], "L0_ffn_b_r", "router_bias")
            spread(b_row["bk"][:, :], "L0_ffn_ln_g", "ln_g")
            spread(b_row["bv"][:, :], "L0_ffn_ln_b", "ln_b")
            spread(b_row["bl"][:, :], "L1_gnn_b2", "gnn_b2")
            sp.wait_ge(h3_out_free[0], 1 + TURNS)
            sp.wait_ge(h3_out_free[1], 1 + TURNS)
            sp.wait_ge(span_ready, 1)

            def hidden_load(q, unit):
                for part in range(2):
                    sp.dma_start(h3_slot[q][part * HID:(part + 1) * HID, :, :].bitcast(F32),
                                 edge_hidden[part, unit, q, :, :].rearrange("u (j c) n -> c (u j) n", c=HID))\
                        .then_inc(h3_loaded[q], 16)

            step = step_counter(sp, "sp_step")
            with sp.Fori(0, NT) as b:
                lo, hi = block_span(sp, b)
                with sp.Fori(lo, hi) as u:
                    s = next_step(sp, step)
                    for q in range(2):
                        sp.wait_ge(weights_done, s * J + 2 * q + 2)
                        hidden_load(q, bass.ds(u, 1))
            s = next_step(sp, step)
            sp.wait_ge(weights_done, s * J + 2)
            hidden_load(0, slice(0, 1))

            filled(sp, ("routersT",))
            sp.dma_start(expert_b2[:, :], A["L0_ffn_b2"]).then_inc(loads["expert_b2"], 16)
            sp.wait_ge(padding_ready, 4)
            sp.dma_start(bias_rows[0:HC, :], A["L1_gnn_b1"].rearrange("(c f) -> c f", f=P)).then_inc(loads["biases"], 16)
            flat_b1 = A["L1_ffn_b1"].rearrange("e f -> (e f)")
            sp.dma_start(bias_rows[HC:HC + SC - 1, :], flat_b1[0:(SC - 1) * P].rearrange("(c f) -> c f", f=P))\
                .then_inc(loads["biases"], 16)
            sp.dma_start(bias_rows[HC + SC - 1:HC + SC, 0:hidden_rows(SC - 1)],
                         flat_b1[(SC - 1) * P:SE * SF].rearrange("(c f) -> c f", c=1)).then_inc(loads["biases"], 16)
            for s in range(NT):
                for g in range(len(GROUPS)):
                    drained(sp, ("adjT", s, g))
            sp.dma_start(adj_dram, adj_T).then_inc(adj_stored, 16)

            def expert_weights(a, e, part):
                if part == 1:
                    src = A["L0_ffn_W1"][bass.ds(e, 1), :, :] if not isinstance(e, int) else A["L0_ffn_W1"][e:e + 1, :, :]
                    sp.dma_start(ew1[a], src.rearrange("e (c p) f -> p (e c) f", p=P)).then_inc(ew1_loaded[a], 16)
                else:
                    src = A["L0_ffn_W2"][bass.ds(e, 1), :, :] if not isinstance(e, int) else A["L0_ffn_W2"][e:e + 1, :, :]
                    src = src.rearrange("e (c p) d -> p (e c) d", p=P)
                    sp.dma_start(ew2_lo[a], src[:, 0:HALF, :]).then_inc(ew2_loaded[a], 16)
                    sp.dma_start(ew2_hi[a], src[:, HALF:FC, :]).then_inc(ew2_loaded[a], 16)

            expert_weights(0, 0, 1)
            sp.wait_ge(adj_stored, 16)
            expert_weights(1, 1, 1)
            sp.wait_ge(rows_scattered, 16 * TOP * NT)
            expert_weights(0, 0, 2)
            expert_weights(1, 1, 2)
            with sp.Fori(0, EX // 2 - 1) as i:
                for a in range(2):
                    end = sp.value_load(first_tile_int[0:1, bass.ds(2 * i + a + 1, 1)], min_val=1, max_val=TILES)
                    sp.wait_ge(down_done, end + 1)
                    expert_weights(a, 2 * i + a + 2, 1)
                    expert_weights(a, 2 * i + a + 2, 2)
            end = sp.value_load(first_tile_int[0:1, EX:EX + 1], min_val=EX, max_val=TILES)
            sp.wait_ge(down_done, end + 1)
            sp.dma_start(adj_T, adj_dram).then_inc(loads["adj_T"], 16)
            gw2_rows = A["L1_gnn_W2"].rearrange("(c p) d -> p c d", p=P)
            a0 = (NT + 2) * D + C * H1
            sp.dma_start(grid(big_a, a0, GW2_FIRST, D), gw2_rows[:, 0:GW2_FIRST, :]).then_inc(loads["gw2_first"], 16)
            sp.wait_ge(ln_ready[3], 1)
            sp.dma_start(gw1, A["L1_gnn_W1"].rearrange("(c p) f -> p c f", p=P)).then_inc(loads["gw1"], 16)
            filled(sp, ("b2", NT - 1))
            sp.dma_start(expert_b2[0:SE, :], A["L1_ffn_b2"]).then_inc(loads["shared_b2"], 16)
            spread(b_row["bk"][:, :], "L1_mix_b_out", "b_out")
            spread(b_row["bv"][:, :], "L1_mix_ln_scale", "ln_scale")
            for g in range(len(GROUPS)):
                filled(sp, ("h1T", HC - 1, g))
            sp.dma_start(grid(big_a, 0, HC - GW2_FIRST, D), gw2_rows[:, GW2_FIRST:, :]).then_inc(loads["gw2_last"], 16)
            filled(sp, ("y2", NT - 1))
            sp.dma_start(w_qkv, A["L1_mix_w_qkv"].rearrange("(c p) f -> p c f", p=P)).then_inc(loads["w_qkv"], 16)
            sp.dma_start(w_att, A["L1_mix_w_out"].rearrange("(c p) f -> p c f", p=P)).then_inc(loads["w_att"], 16)
            filled(sp, ("m5", C - 1))
            for e in range(SE):
                sp.dma_start(sw1[:, :, e, :], A["L1_ffn_W1"][e].rearrange("(c p) f -> p c f", p=P)).then_inc(loads["sw1"], 16)
            flat_w2 = A["L1_ffn_W2"].rearrange("e f d -> (e f) d")
            sp.dma_start(grid(big_a, 0, SW2_FIRST, D), flat_w2[0:SW2_FIRST * P, :].rearrange("(j p) d -> p j d", p=P))\
                .then_inc(loads["sw2"], 16)
            for j in range(SW2_FIRST, SC):
                r = hidden_rows(j)
                sp.dma_start(sw2[j][0:r, :], flat_w2[j * P:j * P + r, :]).then_inc(loads["sw2"], 16)
            for t in range(NT):
                drained(sp, ("down", t))
                sp.dma_start(out[t * P:t * P + rows(t), :], x_rows[0:rows(t), t, :]).then_inc(out_stored, 16)
            sp.wait_ge(out_stored, 16 * NT)

        @block.gpsimd
        def _(pool):
            nc.gpsimd.memset(x_rows[:, NT - 1, :], 0.0).then_inc(padding_ready, 1)
            nc.gpsimd.memset(zeros16[:, :], 0.0).then_inc(padding_ready, 1)
            nc.gpsimd.memset(w_mlp1[:, :, :], 0.0)
            nc.gpsimd.memset(w_mlp2[:, :], 0.0)
            nc.gpsimd.memset(w_mlp3[:, :], 0.0).then_inc(padding_ready, 1)
            nc.gpsimd.memset(ident[:, :], 0.0).then_inc(ident_zeroed, 1)
            nc.gpsimd.iota(iota_nodes[:, :], [[1, NP]], base=0, channel_multiplier=0,
                           allow_small_or_imprecise_dtypes=True)
            nc.gpsimd.iota(block_lo[:, :], [[P, NT]], base=0, channel_multiplier=0,
                           allow_small_or_imprecise_dtypes=True)
            nc.gpsimd.iota(unit_id[:, :], [[0, 1]], base=0, channel_multiplier=1,
                           allow_small_or_imprecise_dtypes=True)
            pool.wait_ge(ident_zeroed, 1)
            nc.gpsimd.affine_select(out=ident[:, :], in_=ident[:, :], compare_op=ALU.not_equal, fill=1.0, base=0,
                                    pattern=[[-1, P]], channel_multiplier=1).then_inc(consts_ready, 1)
            nc.gpsimd.memset(kv_T[:, :, :], 0.0)
            nc.gpsimd.memset(dst_int[:, :, :], -1)
            nc.gpsimd.memset(src_int[:, :, :], 0)
            nc.gpsimd.memset(edges[:, :, :], 0.0).then_inc(consts_ready, 1)
            pool.wait_ge(consts_ready, 2)
            tail = E - FULL * U
            q = tail // J
            for tab, a, w in ((dst_int[:, :, :], A["dst"], 1), (src_int[:, :, :], A["src"], 1),
                              (edges[:, :, J:J + J * Y], A["edge_attr_4"].rearrange("e y -> (e y)"), Y)):
                pool.dma_start(tab[:, 0:FULL, :], a[0:FULL * U * w].rearrange("(u p k) -> p u k", p=P, k=J * w))\
                    .then_inc(loads["edge_tables"], 16)
                if q:
                    pool.dma_start(tab[0:q, FULL, :], a[FULL * U * w:(FULL * U + q * J) * w]
                                   .rearrange("(p k) -> p k", k=J * w)).then_inc(loads["edge_tables"], 16)
                if tail % J:
                    pool.dma_start(tab[q:q + 1, FULL, 0:tail % J * w], a[(FULL * U + q * J) * w:E * w]
                                   .rearrange("(p k) -> p k", p=1)).then_inc(loads["edge_tables"], 16)
            pool.dma_start(dst_units[0:UNITS - 1, :], A["dst"][0:(UNITS - 1) * U].rearrange("(u k) -> u k", k=U))\
                .then_inc(loads["dst_units"], 16)
            pool.dma_start(dst_units[UNITS - 1:UNITS, :], A["dst"][E - U:E].rearrange("(u k) -> u k", k=U))\
                .then_inc(loads["dst_units"], 16)
            nc.gpsimd.memset(ones_col[:, :], 1.0)
            nc.gpsimd.iota(hidden_id[:, :], [[P, SC]], base=0, channel_multiplier=1, allow_small_or_imprecise_dtypes=True)
            nc.gpsimd.tensor_scalar(real_row[:, :], unit_id[:, :], float(rows(NT - 1)), None, ALU.is_lt)
            nc.gpsimd.tensor_copy(ident16[:, :], ident[:, :]).then_inc(consts_ready, 1)
            pool.wait_ge(reach_ready, 1)
            nc.gpsimd.partition_all_reduce(reach_all[:, :], reach[:, :], UNITS, RMAX).then_inc(reach_max_ready, 1)
            for a in range(PAIRS):
                pool.sem_inc(h3_out_free[a], 1)
            with pool.Fori(0, TURNS) as i:
                for a in range(PAIRS):
                    pool.wait_ge(h3_split[a], i + 2)
                    for part, h3 in enumerate((h3_hi[a], h3_lo[a])):
                        pool.dma_start(edge_hidden[part, bass.ds(i * (2 * PAIRS) + 2 * a, 2), :, :, :].rearrange("u q p n -> p (u q) n"),
                                       h3[:, :, :, :].bitcast(F32).rearrange("p u q n -> p (u q) n")).then_inc(h3_stored[a], 16)
                for a in range(PAIRS):
                    pool.wait_ge(h3_stored[a], i * 32 + 32)
                    pool.sem_inc(h3_out_free[a], 1)
            pool.wait_ge(sender_stored, 16)
            pool.wait_ge(loads["edge_tables"], 16 * TABLE_DMAS)
            pool.wait_ge(span_ready, 1)
            pool.sem_inc(idx_ready, J)
            step = step_counter(pool, "pool_step")
            with pool.Fori(0, NT) as b:
                lo, hi = block_span(pool, b)
                with pool.Fori(lo, hi) as u:
                    s = next_step(pool, step)
                    for j in range(J):
                        pool.wait_ge(products_done, s * J + j + 1)
                        nc.gpsimd.tensor_copy(idx_slot[j][:, :], src_int[:, bass.ds(u, 1), j]).then_inc(idx_ready, 1)
                        pool.wait_ge(idx_ready, s * J + j + 1)
                        pool.sem_inc(gathers_started, 1)
                        nc.gpsimd.indirect_dma_start(
                            out=sent[j][:, :], out_offset=None, in_=sender_table,
                            in_offset=bass.IndirectOffsetOnAxis(ap=idx_slot[j][:, 0:1], axis=0),
                            bounds_check=NP - 1, oob_is_err=False).then_inc(gathered[j], 16)

            nc.gpsimd.memset(bias_rows, 0.0).then_inc(padding_ready, 1)
            nc.gpsimd.memset(part_weights, 0.0)
            nc.gpsimd.memset(before_me, 0.0).then_inc(ident_zeroed, 1)
            pool.wait_ge(ident_zeroed, 2)
            for i, parts in enumerate(partitions(SE, SE)):
                for j, part in enumerate(parts):
                    nc.gpsimd.memset(part_weights[:, j, i:i + 1], part / SE)
            nc.gpsimd.affine_select(out=before_me, in_=before_me, compare_op=ALU.is_ge, fill=1.0, base=0,
                                    pattern=[[-1, P]], channel_multiplier=1).then_inc(consts_ready, 1)
            pool.wait_ge(slots_ready, 1)
            pool.wait_ge(ln_ready[2], NT)
            pool.wait_ge(tokens_zeroed, 32)
            for t in range(NT):
                for k in range(TOP):
                    r = rows(t)
                    nc.gpsimd.indirect_dma_start(
                        out=tokens_sorted, out_offset=bass.IndirectOffsetOnAxis(ap=slot_int[0:r, k, t:t + 1], axis=0),
                        in_=hx_rows[0:r, t, :], in_offset=None,
                        bounds_check=(TILES + 1) * P - 1, oob_is_err=False).then_inc(rows_scattered, 16)
            pool.wait_ge(rows_scattered, 16 * TOP * NT)
            pool.dma_start(tile_rows, tokens_sorted[0:P, :]).then_inc(tile_loaded, 16)
            pool.wait_ge(mixed_zeroed, 32)
            count = pool.value_load(first_tile_int[0:1, EX:EX + 1], min_val=EX, max_val=TILES)
            with pool.Fori(0, count) as t:
                pool.wait_ge(tile_transposed, t + 1)
                pool.sem_inc(gathers_started, 1)
                pool.dma_start(tile_rows, tokens_sorted[bass.ds(t * P + P, P), :]).then_inc(tile_loaded, 16)
                pool.wait_ge(tile_out_ready, t + 2)
                pool.sem_inc(gathers_started, 1)
                pool.dma_start(mixed_sorted[bass.ds(t * P, P), :], tile_out).then_inc(tile_stored, 16)
                pool.wait_ge(tile_stored, t * 16 + 16)
                pool.sem_inc(tile_out_free, 1)
            for t in range(NT):
                for k in range(TOP):
                    r = rows(t)
                    nc.gpsimd.indirect_dma_start(
                        out=mixed[0:r, t, k, :], out_offset=None, in_=mixed_sorted,
                        in_offset=bass.IndirectOffsetOnAxis(ap=slot_int[0:r, k, t:t + 1], axis=0),
                        bounds_check=TILES * P - 1, oob_is_err=False).then_inc(mixed_loaded[t], 16)
            pool.wait_ge(hidden_w_ready, 1)
            pool.wait_ge(loads["sw2"], 16 * (1 + SC - SW2_FIRST))
            for j in range(SC):
                r = hidden_rows(j)
                nc.gpsimd.tensor_scalar(sw2[j][0:r, :], sw2[j][0:r, :], hidden_w[0:r, j:j + 1], None, ALU.mult)\
                    .then_inc(sw2_ready, 1)

        @block.scalar
        def _(act):
            def deviations(n, dst=rstd):
                act.wait_ge(stats_ready, n + 1)
                nc.scalar.activation(dst[:, :], meanvar[:, :, 1], ACT.Sqrt).then_inc(std_ready, 1)

            deviations(0)
            for w in ("Wk", "Wv", "Wl"):
                for c in range(C):
                    full, free = filled(act, ("wT", w, c))
                    nc.scalar.activation(w_T[w][:, c, :], full, ACT.Copy).then_inc(free, 1)
            for t in range(NT):
                full, free = filled(act, ("xT", t))
                nc.scalar.activation(xn_T[:, :, tile_cols[t]], full.rearrange("p (c n) -> p c n", c=C), ACT.Copy)\
                    .then_inc(free, 1)
            for t in range(NT):
                full, free = filled(act, ("sender", t))
                nc.scalar.activation(sender_rows[:, t, :], full, ACT.Copy, scale=MUL ** -0.5).then_inc(free, 1)
            full, free = filled(act, ("kvT",))
            act.wait_ge(consts_ready, 2)
            full = full.rearrange("p (c n) -> p c n", c=C)
            nc.scalar.activation(kv_T[0:HD, :, 0:HD], full[0:HD, :, 0:HD], ACT.Copy, scale=N ** -0.5)
            nc.scalar.activation(kv_T[HD:P, :, HD:P], full[HD:P, :, HD:P], ACT.Copy, scale=N ** -0.5).then_inc(free, 1)
            for c in range(C):
                full, free = filled(act, ("m2", c))
                nc.scalar.activation(m2[:, c, :], full, ACT.Copy).then_inc(free, 1)
            for c in range(C):
                full, free = filled(act, ("m3", c))
                nc.scalar.activation(m3[:, c, :], full, ACT.Copy).then_inc(free, 1)
            for a in range(PAIRS):
                act.sem_inc(silu_done[a], 3)
            with act.Fori(0, TURNS) as i:
                for layer in range(3):
                    for a in range(PAIRS):
                        act.wait_ge(layer_done[a], i * 3 + layer + 4)
                        dst = h_slot[a][:, :]
                        src = psum[:, 2 * a + 1, :]
                        if layer == 2:
                            act.wait_ge(h3_split[a], i + 1)
                            dst = h3_out[a][:, :, :, :].rearrange("p u q n -> p q u n")
                            src = src.rearrange("p (q u n) -> p q u n", q=2, u=2)
                        scale = R ** -0.5 if layer == 0 else SILU_2MOM * HID ** -0.5
                        nc.scalar.activation(dst, src, ACT.Silu, scale=scale).then_inc(silu_done[a], 1)
            for a in range(PAIRS):
                act.wait_ge(h3_out_free[a], 1 + TURNS)
            act.wait_ge(span_ready, 1)
            act.sem_inc(adj_flushed, 1)
            act.sem_inc(hot_y_ready, J)
            act.sem_inc(scaled_ready, J)
            step = step_counter(act, "act_step")
            with act.Fori(0, NT) as b:
                lo, hi = block_span(act, b)
                with act.Fori(lo, hi) as u:
                    s = next_step(act, step)
                    act.wait_ge(edge_slot_ready, s)
                    for j in range(J):
                        k = j % 2
                        y = [edge_slot[:, J + Y * j + y:J + Y * j + y + 1] for y in range(Y)]
                        act.wait_ge(gathered[j], s * 16)
                        act.wait_ge(products_done, s * J + J + j - 1)
                        for m in range(3):
                            last = nc.scalar.activation(scaled[:, k, m, :], sent[j][:, MUL + m * MUL:2 * MUL + m * MUL], ACT.Copy, scale=y[1 + m])
                        last.then_inc(scaled_ready, 1)
                        act.wait_ge(hot_ready, s * J + j + 1)
                        act.wait_ge(scatter_done, s * J + J + j - 1)
                        for i in range(Y):
                            last = nc.scalar.activation(hot_y[:, k, i, :], hot_f[:, k, :], ACT.Copy, scale=y[i])
                        last.then_inc(hot_y_ready, 1)
                act.wait_ge(scatter_done, s * J + 2 * J)
                nc.scalar.activation(adj_rows[:, bass.ds(b, 1), :].rearrange("p b n -> p (b n)"),
                                     adj_psum[:, 0:NP], ACT.Copy).then_inc(adj_flushed, 1)
            alpha = SILU_2MOM * HID ** -0.5 * (2 * MUL) ** -0.5 / AVG_NUM_NEIGHBORS
            for t in range(NT):
                if t >= 2:
                    filled(act, ('conv', t - 2))
                full, free = filled(act, ("msgT0", t))
                nc.scalar.activation(msg_T[:, t % 2, 0:D], full, ACT.Copy, scale=alpha).then_inc(free, 1)
                full, free = filled(act, ("msgT1", t))
                nc.scalar.activation(msg_T[:, t % 2, D:2 * D - P], full[:, 0:D - P], ACT.Copy, scale=alpha)
                nc.scalar.activation(msg_T[:, t % 2, 2 * D - P:], full[:, D - P:], ACT.Copy, scale=alpha * 3 ** -0.5)\
                    .then_inc(free, 1)

            act.wait_ge(degree_ready, NT)
            nc.scalar.activation(dinv[:, :], degree[:, :], ACT.Sqrt).then_inc(degree_root, 1)
            full, free = filled(act, ("routersT",))
            nc.scalar.activation(routers_T[:, :, :], full[:, 0:C * (EX + PARTS)].rearrange("p (c e) -> p c e", c=C), ACT.Copy)\
                .then_inc(free, 1)
            full, free = filled(act, ("expert_biasT",))
            nc.scalar.activation(expert_bias_T[:, :], full[:, 0:P], ACT.Copy).then_inc(free, 1)

            def adjacency(s0, s1):
                for s in range(s0, s1):
                    for g, (g0, w) in enumerate(GROUPS):
                        full, free = filled(act, ("adjT", s, g))
                        nc.scalar.activation(adj_T[:, s, g0:g0 + w], full[:, 0:w], ACT.Copy).then_inc(free, 1)

            adjacency(0, 5)
            deviations(1)
            deviations(2, rstd2)
            adjacency(5, NT)
            for t in range(NT):
                full, free = filled(act, ("hT", t))
                nc.scalar.activation(xn_T[:, :, tile_cols[t]], full.rearrange("p (c n) -> p c n", c=C), ACT.Copy)\
                    .then_inc(free, 1)
            act.wait_ge(gap_ready, 1)
            nc.scalar.activation(gap[:, :], gap[:, :], ACT.Exp).then_inc(gap_exp, 1)
            for g, (g0, w) in enumerate(GROUPS):
                full, free = filled(act, ("gateT", g))
                nc.scalar.activation(gates_T[:, g0:g0 + w], full[0:EX, 0:w], ACT.Copy).then_inc(free, 1)
            full, free = filled(act, ("biasT",))
            nc.scalar.activation(bias_T[:, :], full[:, 0:HC + SC], ACT.Copy).then_inc(free, 1)
            act.wait_ge(tiles_ready, 1)
            act.sem_inc(gelu_done, UP_BANKS)
            with act.Fori(0, EX // 2) as i:
                for a in range(2):
                    lo, hi = expert_span(act, 2 * i + a)
                    with act.Fori(lo, hi) as t:
                        for f in range(FC):
                            act.wait_ge(up_done, t * FC + f + 1)
                            nc.scalar.activation(hid[:, f, :], psum[:, f % UP_BANKS, 0:P], ACT.Gelu,
                                                 bias=expert_bias_T[:, bass.ds(i * (2 * FC) + a * FC + f, 1)]).then_inc(gelu_done, 1)
            deviations(3)

            def transposed(key, dst, t, n=None):
                full, free = filled(act, (key, t))
                n = P if n is None else n
                nc.scalar.activation(dst[:, :, t * P:t * P + n], full.rearrange("p (c n) -> p c n", c=C)[:, :, 0:n], ACT.Copy)\
                    .then_inc(free, 1)

            for t in range(NT):
                transposed("xn2T", xn_T, t)
            act.wait_ge(dinv_ready, 1)
            for t in range(NT):
                if t >= 2:
                    filled(act, ("ahT", t - 2))
                full, free = filled(act, ("agg1", t))
                nc.scalar.activation(ah_rows[:, t % 2, :], full, ACT.Copy, scale=dinv[:, t:t + 1]).then_inc(free, 1)
                if t:
                    transposed("ahT", ah_T, t - 1)
            transposed("ahT", ah_T, NT - 1)
            for f in range(HC):
                for g, (g0, w) in enumerate(GROUPS):
                    full, free = filled(act, ("h1T", f, g))
                    nc.scalar.activation(h1_T[:, f, g0:g0 + w], full[:, 0:w], ACT.Relu, bias=bias_T[:, f:f + 1]).then_inc(free, 1)
            for t in range(NT):
                full, free = filled(act, ("y2", t))
                nc.scalar.activation(z2_rows[:, t, :], full, ACT.Copy, scale=dinv[:, t:t + 1]).then_inc(free, 1)
            for m in range(C):
                act.wait_ge(k_max_ready, m + 1)
                for g, (g0, w) in enumerate(GROUPS):
                    full, free = filled(act, ("kT", m, g))
                    n = KEY_COLS[g]
                    nc.scalar.activation(ek_T[:, m, g0:g0 + n], full[:, 0:n], ACT.Exp, bias=k_max[:, m:m + 1]).then_inc(free, 1)
            for t in range(NT):
                drained(act, ("q", t))
                nc.scalar.activation(q_rows[:, t, :], q_rows[:, t, :], ACT.Exp).then_inc(q_exp, 1)
            for t in range(NT):
                full, free = filled(act, ("v", t))
                nc.scalar.activation(vx_rows[:, t, :], full, ACT.Copy).then_inc(free, 1)
            for t in range(NT):
                full, free = filled(act, ("ek", t))
                r = rows(t)
                nc.scalar.activation(ek_rows[0:r, t, :], full[0:r, :], ACT.Copy).then_inc(free, 1)
            full, free = filled(act, ("ctxT",))
            full = full.rearrange("p (c n) -> p c n", c=C)
            nc.scalar.activation(kv_T[0:HD, :, 0:HD], full[0:HD, :, 0:HD], ACT.Copy)
            nc.scalar.activation(kv_T[HD:P, :, HD:P], full[HD:P, :, HD:P], ACT.Copy).then_inc(free, 1)
            act.wait_ge(k_scale_ready, 1)
            for c in range(C):
                full, free = filled(act, ("m5", c))
                nc.scalar.activation(m5[:, c, :], full, ACT.Copy, scale=k_scale[:, c:c + 1]).then_inc(free, 1)
            for t in range(NT):
                transposed("qT", q_T, t)
            deviations(4)
            deviations(5)
            for t in range(NT):
                transposed("lastT", xn_T, t)
            drained(act, ("route",))
            nc.scalar.activation(route[:, :], route[:, :], ACT.Exp).then_inc(route_exp, 1)
            for key in ffn_order():
                if key[0] == "up":
                    _, g, j = key
                    n, r = len(TURN_TILES[g]) * P, hidden_rows(j)
                    if g >= 2:
                        filled(act, ("down", TURN_TILES[g - 2][-1]))
                    full, free = filled(act, key)
                    nc.scalar.activation(shid[g % 2][0:r, j, 0:n], full[0:r, 0:n], ACT.Gelu,
                                         bias=bias_T[0:r, HC + j:HC + j + 1]).then_inc(free, 1)

        @block.vector
        def _(dve):
            steps = [0]

            def settle(ins):
                steps[0] += 1
                ins.then_inc(dve_step, 1)
                dve.wait_ge(dve_step, steps[0])

            def layer_norm(src, dst, n):
                for t in range(NT):
                    last = nc.vector.bn_stats(stats[:, t, :], src[:, t, :])
                settle(last)
                for t in range(NT):
                    last = nc.vector.bn_aggr(meanvar[:, t, :], stats[:, t, :])
                settle(last)
                nc.vector.tensor_scalar(meanvar[:, :, 1], meanvar[:, :, 1], LN_EPS, None, ALU.add).then_inc(stats_ready, 1)
                dve.wait_ge(std_ready, n + 1)
                settle(nc.vector.reciprocal(rstd[:, :], rstd[:, :]))
                for t in range(NT):
                    nc.vector.tensor_scalar(dst[:, t, :], src[:, t, :], meanvar[:, t, 0:1], rstd[:, t:t + 1],
                                            ALU.subtract, ALU.mult).then_inc(ln_ready[n], 1)

            dve.wait_ge(loads["x"], 32)
            layer_norm(x_rows, ln_rows, 0)
            dve.wait_ge(loads["dst_units"], 32)
            dve.wait_ge(consts_ready, 1)
            settle(nc.vector.tensor_copy(dst_unitf[:, :], dst_units[:, :]))
            nc.vector.tensor_reduce(unit_max[:, :], dst_unitf[:, :], AX_X, ALU.max)
            settle(nc.vector.tensor_reduce(unit_min[:, :], dst_unitf[:, :], AX_X, ALU.min))
            lo_u = block_lo[0:UNITS, :]
            nc.vector.tensor_scalar(touch[:, 0, :], lo_u, unit_max[:, :], None, ALU.is_le)
            nc.vector.tensor_scalar(touch[:, 1, :], lo_u, float(P - 1), unit_min[:, :], ALU.add, ALU.is_ge)
            nc.vector.tensor_scalar(touch[:, 3, 0:1], unit_id[0:UNITS, :], -1.0, float(UNITS), ALU.mult, ALU.add)
            settle(nc.vector.tensor_scalar(touch[:, 3, 1:2], unit_id[0:UNITS, :], 1.0, None, ALU.add))
            settle(nc.vector.tensor_tensor(touch[:, 2, :], touch[:, 0, :], touch[:, 1, :], ALU.mult))
            nc.vector.tensor_scalar(reach[:, 0:NT], touch[:, 2, :], touch[:, 3, 0:1], None, ALU.mult)
            nc.vector.tensor_scalar(reach[:, NT:], touch[:, 2, :], touch[:, 3, 1:2], None, ALU.mult).then_inc(reach_ready, 1)
            dve.wait_ge(reach_max_ready, 1)
            settle(nc.vector.tensor_scalar(span_f[:, 0, :], reach_all[0:1, 0:NT], -1.0, float(UNITS), ALU.mult, ALU.add))
            settle(nc.vector.tensor_scalar(span_f[:, 0, :], span_f[:, 0, :], float(UNITS - 1), None, ALU.min))
            settle(nc.vector.tensor_scalar(span_f[:, 1, :], span_f[:, 0, :], 1.0, None, ALU.add))
            settle(nc.vector.tensor_tensor(span_f[:, 1, :], span_f[:, 1, :], reach_all[0:1, NT:], ALU.max))
            nc.vector.tensor_copy(span[:, :, :], span_f[:, :, :]).then_inc(span_ready, 1)
            dve.wait_ge(loads["edge_tables"], 16 * TABLE_DMAS)
            nc.vector.tensor_copy(edges[:, :, 0:J], dst_int[:, :, :])
            settle(nc.vector.tensor_copy(edges[:, :, J + J * Y:], src_int[:, :, :]))
            dve.wait_ge(loads["bk"], 16)
            dve.wait_ge(loads["bv"], 16)
            for t in range(NT):
                for w, b, dst in (("Wk", "bk", k_rows), ("Wv", "bv", v_rows)):
                    full, free = filled(dve, (w, t))
                    nc.vector.tensor_tensor(dst[:, t, :], full, b_row[b][:, :], ALU.add).then_inc(free, 1)
            dve.wait_ge(loads["bl"], 16)
            full, free = filled(dve, ("mix_bias",))
            nc.vector.tensor_tensor(mix_bias[:, :], full, b_row["bl"][:, :], ALU.add).then_inc(free, 1)
            drained(dve, ("mix_bias",))
            for t in range(NT):
                settle(nc.vector.tensor_tensor(x_rows[:, t, :], x_rows[:, t, :], mix_bias[:, :], ALU.add))
                full, free = filled(dve, ("mix", t))
                nc.vector.tensor_tensor(x_rows[:, t, :], full, x_rows[:, t, :], ALU.add).then_inc(free, 1)
            dve.wait_ge(loads["mlp"], 16 * (J + 6))
            settle(nc.vector.tensor_copy(w4_hi[:, :], w_mlp4[:, :]))
            nc.vector.tensor_tensor(w4_lo[:, :], w_mlp4[:, :], w4_hi[:, :].bitcast(F32), ALU.subtract).then_inc(w4_ready, 1)
            def edge_inputs(a, turn, layers):
                dve.wait_ge(ea_transposed[a], turn + 2)
                dve.wait_ge(layer_done[a], layers)
                nc.vector.tensor_copy(ea_T[a][:, :], psum[0:J * R, 2 * a, 0:2 * P]).then_inc(ea_T_ready[a], 1)

            def split_hidden(a, turn, layers):
                dve.wait_ge(silu_done[a], layers)
                dve.wait_ge(h3_out_free[a], turn + 1)
                settle_turn(nc.vector.tensor_copy(h3_hi[a][:, :, :, :], h3_out[a][:, :, :, :]), a, turn)
                nc.vector.tensor_tensor(h3_lo[a][:, :, :, :], h3_out[a][:, :, :, :], h3_hi[a][:, :, :, :].bitcast(F32),
                                        ALU.subtract).then_inc(h3_split[a], 1)

            def settle_turn(ins, a, turn):
                ins.then_inc(hi_ready[a], 1)
                dve.wait_ge(hi_ready[a], turn + 1)

            for a in range(PAIRS):
                dve.sem_inc(h3_split[a], 1)
                edge_inputs(a, 0, 1)
            with dve.Fori(0, TURNS - 1) as i:
                for a in range(PAIRS):
                    edge_inputs(a, i + 1, i * 3 + 4)
                for a in range(PAIRS):
                    split_hidden(a, i, i * 3 + 6)
            for a in range(PAIRS):
                split_hidden(a, TURNS - 1, (TURNS - 1) * 3 + 6)
            for a in range(PAIRS):
                dve.wait_ge(h3_out_free[a], 1 + TURNS)
            dve.sem_inc(products_done, 2 * J)
            dve.sem_inc(hot_ready, J)
            dve.sem_inc(dot_ready, J)
            dve.sem_inc(msg_flushed, 1)
            step = step_counter(dve, "dve_step_no")
            with dve.Fori(0, NT) as b:
                lo, hi = block_span(dve, b)
                with dve.Fori(lo, hi) as u:
                    s = next_step(dve, step)
                    dve.wait_ge(hot_y_ready, s * J)
                    dve.wait_ge(products_done, s * J + J)
                    nc.vector.tensor_copy(edge_slot[:, :], edges[:, bass.ds(u, 1), :].rearrange("p u k -> p (u k)"))\
                        .then_inc(edge_slot_ready, 1)
                    dve.wait_ge(edge_slot_ready, s)
                    nodes = iota_nodes[:, bass.ds(b * P, P)]
                    for j in range(J):
                        k = j % 2
                        dst = edge_slot[:, j:j + 1]
                        dve.wait_ge(scatter_done, s * J + J + j - 1)
                        nc.vector.tensor_scalar(hot_f[:, k, :], nodes, dst, None, ALU.is_equal).then_inc(hot_ready, 1)
                        nc.vector.tensor_scalar(hot_dst[:, k, :], nodes, dst, None, ALU.is_equal)
                        src = edge_slot[:, J + J * Y + j:J + J * Y + j + 1]
                        nc.vector.tensor_scalar(hot_src[:, k, :], iota_nodes[:, :], src, None, ALU.is_equal)
                        dve.wait_ge(scaled_ready, s * J + j + 1)
                        nc.vector.tensor_reduce(dot[:, k, :], scaled[:, k, :, :].rearrange("p m u -> p u m"), AX_X, ALU.add)\
                            .then_inc(dot_ready, 1)
                        dve.wait_ge(weights_done, s * J + J + j + 1)
                        w = tile_w[k].rearrange("p (q u) -> p q u", q=4)
                        o = prod[:, k, :].rearrange("p (c u) -> p c u", u=MUL)
                        s0 = sent[j][:, 0:MUL].rearrange("p (a u) -> p a u", a=1)
                        s1 = sent[j][:, MUL:].rearrange("p (m u) -> p m u", u=MUL)
                        nc.vector.tensor_tensor(o[:, 0:5:4, :], w[:, 0:2, :], s0.to_broadcast([P, 2, MUL]), ALU.mult)
                        nc.vector.tensor_tensor(o[:, 1:4, :], s1, w[:, 2:3, :].to_broadcast([P, 3, MUL]), ALU.mult)
                        dve.wait_ge(dot_ready, s * J + j + 1)
                        nc.vector.tensor_tensor(o[:, 5, :], w[:, 3, :], dot[:, k, :], ALU.mult).then_inc(products_done, 1)
                dve.wait_ge(scatter_done, s * J + 2 * J)
                nc.vector.tensor_copy(msg_rows[:, bass.ds(b, 1), :].rearrange("p b n -> p (b n)"), msg_psum[:, :])\
                    .then_inc(msg_flushed, 1)
                dve.wait_ge(adj_flushed, b + 2)
                nc.vector.tensor_reduce(degree[:, bass.ds(b, 1)], adj_rows[:, bass.ds(b, 1), :].rearrange("p b n -> p (b n)"),
                                        AX_X, ALU.add).then_inc(degree_ready, 1)
            for t in range(NT):
                full, free = filled(dve, ("conv", t))
                settle(nc.vector.tensor_tensor(x_rows[:, t, 0:MUL], full[:, 0:MUL], x_rows[:, t, 0:MUL], ALU.add))
                v = x_rows[:, t, MUL:].rearrange("p (u m) -> p m u", m=3)
                nc.vector.tensor_tensor(v, full[:, MUL:].rearrange("p (m u) -> p m u", m=3), v, ALU.add).then_inc(free, 1)

            nc.vector.memset(members_before[:, 0, :], 0.0)
            settle(nc.vector.memset(first_tile[:, 0:1], 0.0))
            layer_norm(x_rows, h0_rows, 1)
            settle(nc.vector.tensor_scalar(var2[:, :], meanvar[:, :, 1], -LN_EPS, None, ALU.add))
            settle(nc.vector.tensor_tensor(var2[:, :], var2[:, :], rstd[:, :], ALU.mult))
            settle(nc.vector.tensor_tensor(var2[:, :], var2[:, :], rstd[:, :], ALU.mult))
            nc.vector.tensor_scalar(meanvar[:, :, 1], var2[:, :], LN_EPS, None, ALU.add).then_inc(stats_ready, 1)
            dve.wait_ge(std_ready, 3)
            settle(nc.vector.reciprocal(rstd2[:, :], rstd2[:, :]))
            dve.wait_ge(loads["ln_g"], 16)
            dve.wait_ge(loads["ln_b"], 16)
            for t in range(NT):
                nc.vector.scalar_tensor_tensor(hx_rows[:, t, :], h0_rows[:, t, :], rstd2[:, t:t + 1], b_row["bk"][:, :],
                                               ALU.mult, ALU.mult)
                settle(nc.vector.tensor_tensor(x_rows[:, t, :], x_rows[:, t, :], h0_rows[:, t, :], ALU.add))
                nc.vector.tensor_tensor(hx_rows[:, t, :], hx_rows[:, t, :], b_row["bv"][:, :], ALU.add).then_inc(ln_ready[2], 1)
            dve.wait_ge(loads["router_bias"], 16)
            full, free = filled(dve, ("logits",))
            nc.vector.tensor_tensor(logits[:, :, :], full[:, 0:NT * EX].rearrange("p (t e) -> p t e", e=EX),
                                    router_bias[:, :].unsqueeze(1).to_broadcast([P, NT, EX]), ALU.add).then_inc(free, 1)
            drained(dve, ("logits",))
            for t in range(NT):
                last = nc.vector.max(top_val[:, t, :], logits[:, t, :])
            settle(last)
            nc.vector.tensor_tensor(gap[:, :], top_val[:, :, 1], top_val[:, :, 0], ALU.subtract).then_inc(gap_ready, 1)
            for t in range(NT):
                last = nc.vector.max_index(top_idx[:, t, :], top_val[:, t, :], logits[:, t, :])
            settle(last)
            settle(nc.vector.tensor_copy(choice_f[:, :, :], top_idx[:, :, 0:TOP].rearrange("p t k -> p k t")))
            ids = iota_nodes[:, 0:EX].unsqueeze(1).to_broadcast([P, NT, EX])
            for k in range(TOP):
                last = nc.vector.tensor_tensor(chosen[:, k, :, :], ids, choice_f[:, k, :].unsqueeze(2).to_broadcast([P, NT, EX]),
                                               ALU.is_equal)
            settle(last)
            settle(nc.vector.tensor_tensor(member[:, :, :], chosen[:, 0, :, :], chosen[:, 1, :, :], ALU.add))
            settle(nc.vector.tensor_scalar(member[:, NT - 1, :], member[:, NT - 1, :], real_row[:, :], None, ALU.mult))
            for t in range(NT):
                last = nc.vector.tensor_tensor(members_before[:, t + 1, :], members_before[:, t, :], member[:, t, :], ALU.add)
                if t + 1 < NT:
                    settle(last)
            last.then_inc(members_ready, 1)
            dve.wait_ge(gap_exp, 1)
            settle(nc.vector.tensor_scalar(gate[:, 0, :], gap[:, :], 1.0, None, ALU.add))
            settle(nc.vector.reciprocal(gate[:, 0, :], gate[:, 0, :]))
            settle(nc.vector.tensor_tensor(gate[:, 1, :], gap[:, :], gate[:, 0, :], ALU.mult))
            full, free = filled(dve, ("rank",))
            counts = full[:, NT * EX:(NT + 1) * EX]
            settle(nc.vector.tensor_tensor(tile_tests[:, :, :], counts.unsqueeze(2).to_broadcast([P, EX, NT]),
                                           block_lo[:, :].unsqueeze(1).to_broadcast([P, EX, NT]), ALU.is_gt))
            settle(nc.vector.tensor_reduce(expert_tiles[:, :], tile_tests[:, :, :], AX_X, ALU.add))
            settle(nc.vector.tensor_scalar(expert_tiles[:, :], expert_tiles[:, :], 1.0, None, ALU.max))
            for e in range(EX):
                settle(nc.vector.tensor_tensor(first_tile[:, e + 1:e + 2], first_tile[:, e:e + 1], expert_tiles[:, e:e + 1], ALU.add))
            nc.vector.tensor_copy(first_tile_int[:, :], first_tile[0:1, :]).then_inc(tiles_ready, 1)
            settle(nc.vector.tensor_scalar(place_base[:, :], first_tile[:, 0:EX], float(P), None, ALU.mult))
            nc.vector.tensor_tensor(place[:, :, :], full[:, 0:NT * EX].rearrange("p (t e) -> p t e", e=EX),
                                    place_base[:, :].unsqueeze(1).to_broadcast([P, NT, EX]), ALU.add).then_inc(free, 1)
            drained(dve, ("rank",))
            for k in range(TOP):
                settle(nc.vector.tensor_tensor(member[:, :, :], chosen[:, k, :, :], place[:, :, :], ALU.mult))
                settle(nc.vector.tensor_reduce(slot_f[:, k, :], member[:, :, :], AX_X, ALU.add))
            nc.vector.tensor_copy(slot_int[:, :, :], slot_f[:, :, :]).then_inc(slots_ready, 1)
            for k in range(TOP):
                settle(nc.vector.tensor_tensor(chosen[:, k, :, :], chosen[:, k, :, :],
                                               gate[:, k, :].unsqueeze(2).to_broadcast([P, NT, EX]), ALU.mult))
            nc.vector.tensor_tensor(token_gates[:, :, :], chosen[:, 0, :, :], chosen[:, 1, :, :], ALU.add).then_inc(gates_ready, 1)
            for t in range(NT):
                full, free = filled(dve, ("b2", t))
                nc.vector.tensor_tensor(x_rows[:, t, :], full, x_rows[:, t, :], ALU.add).then_inc(free, 1)
            dve.wait_ge(degree_root, 1)
            nc.vector.reciprocal(dinv[:, :], dinv[:, :]).then_inc(dinv_ready, 1)
            def tile_transposed_out(n):
                dve.wait_ge(tile_transposed, n)
                nc.vector.tensor_copy(tile_T[:, :, :], psum[:, T_BANK, :].rearrange("p (c n) -> p c n", c=C)).then_inc(tile_T_ready, 1)

            dve.sem_inc(tile_out_ready, 1)
            tile_transposed_out(1)
            count = dve.value_load(first_tile_int[0:1, EX:EX + 1], min_val=EX, max_val=TILES)
            dve.sem_inc(tile_out_free, 1)
            with dve.Fori(0, count) as t:
                tile_transposed_out(t + 2)
                dve.wait_ge(down_done, t + 2)
                dve.wait_ge(tile_out_free, t + 1)
                nc.vector.tensor_copy(tile_out, psum[:, Y_BANK, :]).then_inc(tile_out_ready, 1)
            for t in range(NT):
                r = rows(t)
                dve.wait_ge(mixed_loaded[t], 16 * TOP)
                for k in range(TOP):
                    settle(nc.vector.scalar_tensor_tensor(x_rows[0:r, t, :], mixed[0:r, t, k, :], gate[0:r, k, t:t + 1],
                                                          x_rows[0:r, t, :], ALU.mult, ALU.add))
            layer_norm(x_rows, xn2_rows, 3)
            dve.wait_ge(dinv_ready, 1)
            settle(nc.vector.tensor_tensor(rstd2[:, :], rstd[:, :], dinv[:, :], ALU.mult))
            for t in range(NT):
                nc.vector.tensor_scalar(z_rows[:, t, :], x_rows[:, t, :], meanvar[:, t, 0:1], rstd2[:, t:t + 1],
                                        ALU.subtract, ALU.mult).then_inc(z_ready, 1)
            dve.wait_ge(loads["gnn_b2"], 16)
            for t in range(NT):
                full, free = filled(dve, ("agg2", t))
                nc.vector.scalar_tensor_tensor(conv_out[:, t % 2, :], full, dinv[:, t:t + 1], b_row["bl"][:, :], ALU.mult, ALU.add)\
                    .then_inc(free, 1)
                drained(dve, ("agg2", t))
                settle(nc.vector.scalar_tensor_tensor(x_rows[:, t, :], conv_out[:, t % 2, :], 0.0, x_rows[:, t, :], ALU.max, ALU.add))
            for m in range(C):
                for g, n in enumerate(KEY_COLS):
                    b, uses = ring.at[("kT", m, g)]
                    dve.wait_ge(bank_full[b], uses + 1)
                    last = nc.vector.tensor_reduce(k_max3[:, m, g:g + 1], psum[:, b, 0:n], AX_X, ALU.max)
                settle(last)
                settle(nc.vector.tensor_reduce(k_max[:, m:m + 1], k_max3[:, m, :], AX_X, ALU.max))
                nc.vector.tensor_scalar(k_max[:, m:m + 1], k_max[:, m:m + 1], -1.0, None, ALU.mult).then_inc(k_max_ready, 1)

            def heads(rows_ap):
                return rows_ap.rearrange("p (h d) -> p h d", h=HEADS)

            def queries(t):
                full, free = filled(dve, ("q", t))
                settle(nc.vector.tensor_reduce(q_max[:, :], heads(full), AX_X, ALU.max))
                nc.vector.tensor_tensor(heads(q_rows[:, t, :]), heads(full), q_max[:, :].unsqueeze(2).to_broadcast([P, HEADS, HD]),
                                        ALU.subtract).then_inc(free, 1)
                drained(dve, ("q", t))

            def normalised_queries(t):
                dve.wait_ge(q_exp, t + 1)
                settle(nc.vector.tensor_reduce(q_sum[:, t % 2, :], heads(q_rows[:, t, :]), AX_X, ALU.add))
                settle(nc.vector.reciprocal(q_sum[:, t % 2, :], q_sum[:, t % 2, :]))
                nc.vector.tensor_tensor(heads(q_rows[:, t, :]), heads(q_rows[:, t, :]),
                                        q_sum[:, t % 2, :].unsqueeze(2).to_broadcast([P, HEADS, HD]), ALU.mult).then_inc(q_ready, 1)

            queries(0)
            for t in range(1, NT):
                queries(t)
                normalised_queries(t - 1)
            normalised_queries(NT - 1)
            for m in range(C):
                for g in range(len(GROUPS)):
                    drained(dve, ("kT", m, g))
            settle(nc.vector.tensor_reduce(k_sum[:, :], ek_T[:, :, 0:N], AX_X, ALU.add))
            settle(nc.vector.tensor_scalar(k_sum[:, :], k_sum[:, :], float(N) * HD ** 0.5, None, ALU.mult))
            nc.vector.reciprocal(k_scale[:, :], k_sum[:, :]).then_inc(k_scale_ready, 1)
            dve.wait_ge(loads["b_out"], 16)
            dve.wait_ge(loads["ln_scale"], 16)
            for t in range(NT):
                full, free = filled(dve, ("att", t))
                nc.vector.tensor_tensor(att_rows[:, t, :], full, b_row["bk"][:, :], ALU.add).then_inc(free, 1)
                drained(dve, ("att", t))
            layer_norm(att_rows, att_rows, 4)
            for t in range(NT):
                dve.wait_ge(ln_ready[4], t + 1)
                settle(nc.vector.tensor_tensor(att_rows[:, t, :], att_rows[:, t, :], b_row["bv"][:, :], ALU.mult))
                settle(nc.vector.tensor_tensor(x_rows[:, t, :], x_rows[:, t, :], att_rows[:, t, :], ALU.add))
            layer_norm(x_rows, last_rows, 5)
            for t in range(NT):
                drained(dve, ("lastT", t))
            settle(nc.vector.tensor_reduce(mean_col[:, :], xn_T[:, :, 0:N], AX_X, ALU.add))
            nc.vector.tensor_scalar(mean_col[:, :], mean_col[:, :], 1.0 / N, None, ALU.mult).then_inc(mean_ready, 1)
            full, free = filled(dve, ("route",))
            settle(nc.vector.tensor_reduce(route_f[:, 0:1], full[0:1, 0:PARTS], AX_X, ALU.max))
            nc.vector.tensor_scalar(route[:, :], full[0:1, 0:PARTS], route_f[:, 0:1], None, ALU.subtract).then_inc(free, 1)
            drained(dve, ("route",))
            dve.wait_ge(route_exp, 1)
            settle(nc.vector.tensor_reduce(route_f[:, 1:2], route[:, :], AX_X, ALU.add))
            settle(nc.vector.reciprocal(route_f[:, 1:2], route_f[:, 1:2]))
            settle(nc.vector.tensor_scalar(route[:, :], route[:, :], route_f[:, 1:2], None, ALU.mult))
            settle(nc.vector.max(route_top[:, :], route[:, :]))
            settle(nc.vector.max_index(route_idx[:, :], route_top[:, :], route[:, :]))
            settle(nc.vector.tensor_copy(route_f[:, 2:4], route_idx[:, 0:2]))
            settle(nc.vector.tensor_reduce(route_f[:, 4:5], route_top[:, 0:2], AX_X, ALU.add))
            settle(nc.vector.reciprocal(route_f[:, 4:5], route_f[:, 4:5]))
            settle(nc.vector.tensor_scalar(route_f[:, 6:8], route_top[:, 0:2], route_f[:, 4:5], None, ALU.mult))
            for k in range(2):
                last = nc.vector.tensor_scalar(route_coef[:, k, :], iota_nodes[0:1, 0:PARTS], route_f[:, 2 + k:3 + k],
                                               route_f[:, 6 + k:7 + k], ALU.is_equal, ALU.mult)
            settle(last)
            settle(nc.vector.tensor_tensor(route_coef[:, 0, :], route_coef[:, 0, :], route_coef[:, 1, :], ALU.add))
            settle(nc.vector.tensor_tensor(part_prod[:, :, :], part_weights[:, :, :],
                                           route_coef[:, 0, :].unsqueeze(1).to_broadcast([1, SE, PARTS]), ALU.mult))
            settle(nc.vector.tensor_reduce(expert_w[:, 0, :], part_prod[:, :, :], AX_X, ALU.add))
            settle(nc.vector.tensor_scalar(expert_w[:, 1, :], expert_w[:, 0, :], 1e-6, None, ALU.is_gt))
            nc.vector.tensor_tensor(expert_w[:, 0, :], expert_w[:, 0, :], expert_w[:, 1, :], ALU.mult).then_inc(route_weighted, 1)
            full, free = filled(dve, ("expert_w",))
            nc.vector.tensor_copy(expert_w_col[:, :], full[0:SE, SE:SE + 1])
            nc.vector.tensor_copy(expert_w_all[:, :], full[:, 0:SE]).then_inc(free, 1)
            drained(dve, ("expert_w",))
            for e in range(SE + 1):
                last = nc.vector.tensor_scalar(past[:, e, :], hidden_id[:, :], float(e * SF), None, ALU.is_ge)
            settle(last)
            settle(nc.vector.tensor_tensor(past[:, 0:SE, :], past[:, 0:SE, :], past[:, 1:, :], ALU.subtract))
            settle(nc.vector.tensor_tensor(past[:, 0:SE, :], past[:, 0:SE, :],
                                           expert_w_all[:, :].unsqueeze(2).to_broadcast([P, SE, SC]), ALU.mult))
            nc.vector.tensor_reduce(hidden_w[:, :], past[:, 0:SE, :].rearrange("p e j -> p j e"), AX_X, ALU.add)\
                .then_inc(hidden_w_ready, 1)
            full, free = filled(dve, ("b2_mix",))
            nc.vector.tensor_copy(mix_bias[:, :], full).then_inc(free, 1)
            drained(dve, ("b2_mix",))
            for t in range(NT):
                settle(nc.vector.tensor_tensor(x_rows[:, t, :], x_rows[:, t, :], mix_bias[:, :], ALU.add))
            for t in range(NT):
                full, free = filled(dve, ("down", t))
                nc.vector.tensor_tensor(x_rows[:, t, :], full, x_rows[:, t, :], ALU.add).then_inc(free, 1)

        @block.tensor
        def _(pe):
            pe.wait_ge(consts_ready, 1)
            for w in ("Wk", "Wv", "Wl"):
                pe.wait_ge(loads[w], 16)
                for c in range(C):
                    out_b, full = claim(pe, ("wT", w, c))
                    for o in range(C):
                        cols = slice(c * P, c * P + P) if w == "Wl" else comp[c]
                        last = nc.tensor.transpose(out_b[:, o * P:o * P + P], w_rows[w][:, o, cols], ident[:, :])
                    last.then_inc(full, 1)
            for t in range(NT):
                pe.wait_ge(ln_ready[0], t + 1)
                out_b, full = claim(pe, ("xT", t))
                for c in range(C):
                    last = nc.tensor.transpose(out_b[:, c * P:c * P + P], ln_rows[:, t, comp[c]], ident[:, :])
                last.then_inc(full, 1)
            pe.wait_ge(loads["w_up"], 32)
            for t in range(NT):
                drained(pe, ("xT", t))
                out_b, full = claim(pe, ("sender", t))
                for c in range(C):
                    last = nc.tensor.matmul(out_b[:, c * P:c * P + P], xn_T[:, c, tile_cols[t]], w_up[:, min(c, 1), :],
                                            start=True, stop=True)
                last.then_inc(full, 1)
            for w in ("Wk", "Wv", "Wl"):
                for c in range(C):
                    drained(pe, ("wT", w, c))
            for t in range(NT):
                for w in ("Wk", "Wv"):
                    out_b, full = claim(pe, (w, t))
                    for c in range(C):
                        last = nc.tensor.matmul(out_b, xn_T[:, c, tile_cols[t]], w_T[w][:, c, :], start=(c == 0), stop=(c == C - 1))
                    last.then_inc(full, 1)
            out_b, full = claim(pe, ("kvT",))
            for t in range(NT):
                drained(pe, ("Wk", t))
                drained(pe, ("Wv", t))
            for c in range(C):
                for t in range(NT):
                    r = slice(0, rows(t))
                    last = nc.tensor.matmul(out_b[:, c * P:c * P + P], v_rows[r, t, c * P:c * P + P],
                                            k_rows[r, t, c * P:c * P + P], start=(t == 0), stop=(t == NT - 1))
            last.then_inc(full, 1)
            drained(pe, ("kvT",))
            for c in range(C):
                out_b, full = claim(pe, ("m2", c))
                nc.tensor.matmul(out_b, kv_T[:, c, :], w_T["Wl"][:, c, :], start=True, stop=True).then_inc(full, 1)
            for c in range(C):
                drained(pe, ("m2", c))
            pe.wait_ge(loads["Wq"], 16)
            for i in range(C):
                out_b, full = claim(pe, ("m3", i))
                for c in range(C):
                    last = nc.tensor.matmul(out_b, w_rows["Wq"][:, c, comp[i]], m2[:, c, :], start=(c == 0), stop=(c == C - 1))
                last.then_inc(full, 1)
            pe.wait_ge(loads["bq"], 16)
            out_b, full = claim(pe, ("mix_bias",))
            for c in range(C):
                last = nc.tensor.matmul(out_b, bq_col[:, c:c + 1].to_broadcast([P, P]), m2[:, c, :],
                                        start=(c == 0), stop=(c == C - 1))
            last.then_inc(full, 1)
            for c in range(C):
                drained(pe, ("m3", c))
            for t in range(NT):
                out_b, full = claim(pe, ("mix", t))
                for c in range(C):
                    last = nc.tensor.matmul(out_b, xn_T[:, c, tile_cols[t]], m3[:, c, :], start=(c == 0), stop=(c == C - 1))
                last.then_inc(full, 1)
            for b in range(8):
                pe.wait_ge(bank_free[b], before_edges[b])
            pe.wait_ge(loads["mlp"], 16 * (J + 6))
            for a in range(PAIRS):
                pe.sem_inc(ea_transposed[a], 1)
                pe.sem_inc(layer_done[a], 3)
            with pe.Fori(0, TURNS) as i:
                for a in range(PAIRS):
                    pe.wait_ge(ea_loaded[a], i * 16 + 16)
                    pe.wait_ge(silu_done[a], i * 3 + 3)
                    for h in range(2):
                        last = nc.tensor.transpose(psum[0:J * R, 2 * a, h * P:h * P + P], ea_slot[a][:, h, :], ident[:, :])
                    last.then_inc(ea_transposed[a], 1)
                for a in range(PAIRS):
                    pe.wait_ge(ea_T_ready[a], i + 1)
                    for q in range(2):
                        last = nc.tensor.matmul(psum[:, 2 * a + 1, q * 2 * P:(q + 1) * 2 * P], w_mlp1[:, q, :], ea_T[a][:, :],
                                                start=True, stop=True)
                    last.then_inc(layer_done[a], 1)
                for layer, w in ((1, w_mlp2), (2, w_mlp3)):
                    for a in range(PAIRS):
                        pe.wait_ge(silu_done[a], i * 3 + 3 + layer)
                        nc.tensor.matmul(psum[:, 2 * a + 1, :], w[:, :], h_slot[a][:, :], start=True, stop=True)\
                            .then_inc(layer_done[a], 1)
            for a in range(PAIRS):
                pe.wait_ge(silu_done[a], 3 + 3 * TURNS)

            def tile_weights(j):
                lhs = h3_slot[j // 2][:, j % 2, :]
                nc.tensor.matmul(tile_w[j % 2], lhs, w4_hi[:, :], start=True, stop=False)
                nc.tensor.matmul(tile_w[j % 2], lhs, w4_lo[:, :], start=False, stop=True).then_inc(weights_done, 1)

            pe.sem_inc(weights_done, 2 * J)
            pe.sem_inc(scatter_done, 2 * J)
            pe.wait_ge(padding_ready, 2)
            pe.wait_ge(consts_ready, 3)
            pe.wait_ge(span_ready, 1)
            pe.wait_ge(w4_ready, 1)
            pe.wait_ge(h3_loaded[0], 32)
            tile_weights(0)
            step = step_counter(pe, "pe_step")
            with pe.Fori(0, NT) as b:
                lo, hi = block_span(pe, b)
                pe.wait_ge(msg_flushed, b + 1)
                pe.wait_ge(adj_flushed, b + 1)
                for k in range(5):
                    nc.tensor.matmul(psum[:, k, :], zeros16[:, 0:P], zeros16[:, :], start=True, stop=False, skip_group_check=True)
                nc.tensor.matmul(adj_psum[:, bass.ds(b * P, P)], ident16[:, :], ident16[:, :], start=False, stop=True, skip_group_check=True)
                with pe.Fori(lo, hi) as u:
                    s = next_step(pe, step)
                    for j in range(J):
                        k = j % 2
                        if j == 1:
                            pe.wait_ge(h3_loaded[1], s * 32)
                        if j == J - 1:
                            pe.wait_ge(h3_loaded[0], s * 32 + 32)
                        tile_weights((j + 1) % J)
                        pe.wait_ge(products_done, s * J + J + j + 1)
                        pe.wait_ge(hot_y_ready, s * J + j + 1)
                        nc.tensor.matmul(psum[:, 0, :], hot_y[:, k, 0, :], prod[:, k, 0:D], start=False, stop=True, skip_group_check=True)
                        for m in range(3):
                            nc.tensor.matmul(psum[:, 1, m * MUL:m * MUL + MUL], hot_y[:, k, 1 + m, :],
                                             prod[:, k, D:D + MUL], start=False, stop=True, skip_group_check=True)
                        nc.tensor.matmul(psum[:, 1, 3 * MUL:], hot_f[:, k, :], prod[:, k, D + MUL:], start=False, stop=True,
                                         skip_group_check=True)
                        for a0 in range(0, NP, 512):
                            n = min(512, NP - a0)
                            last = nc.tensor.matmul(adj_psum[:, a0:a0 + n], hot_dst[:, k, :], hot_src[:, k, a0:a0 + n],
                                                    start=False, stop=True, skip_group_check=True)
                        last.then_inc(scatter_done, 1)
            pe.wait_ge(msg_flushed, NT + 1)
            pe.wait_ge(adj_flushed, NT + 1)
            pe.wait_ge(loads["w_out"], 32)
            def transposed_messages(t):
                for h in range(2):
                    out_b, full = claim(pe, (f"msgT{h}", t))
                    for c in range(C):
                        last = nc.tensor.transpose(out_b[:, c * P:c * P + P], msg_rows[:, t, h * D + c * P:h * D + c * P + P],
                                                   ident[:, :])
                    last.then_inc(full, 1)

            transposed_messages(0)
            for t in range(NT):
                if t + 1 < NT:
                    transposed_messages(t + 1)
                drained(pe, ("msgT0", t))
                drained(pe, ("msgT1", t))
                out_b, full = claim(pe, ("conv", t))

                def chunk(i):
                    return msg_T[:, t % 2, i * P:i * P + P]

                for c, (i0, i1) in enumerate(((0, 7), (4, 1), (5, 2), (6, 3))):
                    w = w_out[:, min(c, 1), :, :]
                    nc.tensor.matmul(out_b[:, c * P:c * P + P], chunk(i0), w[:, 0, :], start=True, stop=False)
                    last = nc.tensor.matmul(out_b[:, c * P:c * P + P], chunk(i1), w[:, 1, :], start=False, stop=True)
                last.then_inc(full, 1)
            def transposes(key, pieces):
                out_b, full = claim(pe, key)
                at = 0
                for piece in pieces:
                    r, n = piece.shape
                    last = nc.tensor.transpose(out_b[0:n, at:at + r], piece, ident[0:r, 0:r])
                    at += r
                last.then_inc(full, 1)

            def chunks(row):
                return [row[:, c * P:c * P + P] for c in range(row.shape[1] // P)]

            pe.wait_ge(loads["routers"], 32)
            transposes(("routersT",), chunks(router_rows))
            pe.wait_ge(loads["expert_bias"], 16)
            transposes(("expert_biasT",), [expert_bias_rows])
            for s in range(NT):
                for g, (g0, w) in enumerate(GROUPS):
                    transposes(("adjT", s, g), [adj_rows[:, b, tile_cols[s]] for b in range(g0 // P, (g0 + w) // P)])
            for t in range(NT):
                pe.wait_ge(ln_ready[2], t + 1)
                transposes(("hT", t), chunks(hx_rows[:, t, :]))
            drained(pe, ("routersT",))
            out_b, full = claim(pe, ("logits",))
            for t in range(NT):
                drained(pe, ("hT", t))
                for c in range(C):
                    last = nc.tensor.matmul(out_b[:, t * EX:t * EX + EX], xn_T[:, c, tile_cols[t]], routers_T[:, c, 0:EX],
                                            start=(c == 0), stop=(c == C - 1))
            last.then_inc(full, 1)
            pe.wait_ge(members_ready, 1)
            pe.wait_ge(consts_ready, 4)
            out_b, full = claim(pe, ("rank",))
            nc.tensor.matmul(out_b[:, 0:(NT + 1) * EX], ones_col[:, :].to_broadcast([P, P]),
                             members_before[:, :, :].rearrange("p t e -> p (t e)"), start=True, stop=False, skip_group_check=True)
            nc.tensor.matmul(out_b[:, 0:NT * EX], before_me[:, :], member[:, :, :].rearrange("p t e -> p (t e)"),
                             start=False, stop=True, skip_group_check=True).then_inc(full, 1)
            pe.wait_ge(gates_ready, 1)
            for g, (g0, w) in enumerate(GROUPS):
                transposes(("gateT", g), [token_gates[:, t, :] for t in range(g0 // P, (g0 + w) // P)])
            pe.wait_ge(loads["expert_b2"], 16)
            for t in range(NT):
                drained(pe, ("gateT", min(t * P // 512, len(GROUPS) - 1)))
                out_b, full = claim(pe, ("b2", t))
                nc.tensor.matmul(out_b, gates_T[:, tile_cols[t]], expert_b2[:, :], start=True, stop=True).then_inc(full, 1)
            pe.wait_ge(loads["biases"], 48)
            transposes(("biasT",), [bias_rows[:, :]])
            for b in range(8):
                pe.wait_ge(bank_free[b], before_experts[b])

            def tile_transposes(n, loaded):
                pe.wait_ge(tile_loaded, loaded)
                pe.wait_ge(tile_T_ready, n)
                for c in range(C):
                    last = nc.tensor.transpose(psum[:, T_BANK, c * P:c * P + P], tile_rows[:, c * P:c * P + P], ident[:, :])
                last.then_inc(tile_transposed, 1)

            pe.wait_ge(tile_loaded, 16)
            for c in range(C):
                last = nc.tensor.transpose(psum[:, T_BANK, c * P:c * P + P], tile_rows[:, c * P:c * P + P], ident[:, :])
            last.then_inc(tile_transposed, 1)
            pe.sem_inc(down_done, 1)
            with pe.Fori(0, EX // 2) as i:
                for a in range(2):
                    lo, hi = expert_span(pe, 2 * i + a)
                    pe.wait_ge(ew1_loaded[a], i * 16 + 16)
                    pe.wait_ge(ew2_loaded[a], i * 32 + 32)
                    pe.sem_inc(experts_started, 1)
                    with pe.Fori(lo, hi) as t:
                        def down(f):
                            if f == 0:
                                pe.wait_ge(tile_out_ready, t + 1)
                            pe.wait_ge(gelu_done, t * FC + UP_BANKS + f + 1)
                            w2 = ew2_lo[a][:, f, :] if f < HALF else ew2_hi[a][:, f - HALF, :]
                            last = nc.tensor.matmul(psum[:, Y_BANK, :], hid[:, f, :], w2, start=(f == 0), stop=(f == FC - 1))
                            if f == FC - 1:
                                last.then_inc(down_done, 1)

                        pe.wait_ge(tile_T_ready, t + 1)
                        for f in range(FC):
                            pe.wait_ge(gelu_done, t * FC + f + 1)
                            for c in range(C):
                                last = nc.tensor.matmul(psum[:, f % UP_BANKS, 0:P], ew1[a][:, c, f * P:f * P + P], tile_T[:, c, :],
                                                        start=(c == 0), stop=(c == C - 1))
                            last.then_inc(up_done, 1)
                            if f >= 2:
                                down(f - 2)
                        pe.wait_ge(tile_loaded, t * 16 + 32)
                        for c in range(C):
                            last = nc.tensor.transpose(psum[:, T_BANK, c * P:c * P + P], tile_rows[:, c * P:c * P + P], ident[:, :])
                        last.then_inc(tile_transposed, 1)
                        down(FC - 2)
                        down(FC - 1)
            count = pe.value_load(first_tile_int[0:1, EX:EX + 1], min_val=EX, max_val=TILES)
            pe.wait_ge(tile_out_ready, count + 1)
            pe.wait_ge(tile_T_ready, count + 1)
            for t in range(NT):
                pe.wait_ge(ln_ready[3], t + 1)
                transposes(("xn2T", t), chunks(xn2_rows[:, t, :]))
            pe.wait_ge(loads["adj_T"], 16)

            def aggregate(key, rows_ap, t):
                out_b, full = claim(pe, (key, t))
                for s in range(NT):
                    last = nc.tensor.matmul(out_b, adj_T[:, s, tile_cols[t]], rows_ap[:, s, :], start=(s == 0), stop=(s == NT - 1))
                last.then_inc(full, 1)

            def project(key, t, lhs, rhs):
                out_b, full = claim(pe, (key, t))
                for c in range(len(rhs)):
                    last = nc.tensor.matmul(out_b[:, 0:rhs[c].shape[1]], lhs[:, c, tile_cols[t]], rhs[c], start=(c == 0), stop=(c == len(rhs) - 1))
                last.then_inc(full, 1)

            pe.wait_ge(z_ready, NT)
            aggregate("agg1", z_rows, 0)
            for t in range(1, NT + 1):
                if t < NT:
                    aggregate("agg1", z_rows, t)
                drained(pe, ("agg1", t - 1))
                transposes(("ahT", t - 1), chunks(ah_rows[:, (t - 1) % 2, :]))
            pe.wait_ge(loads["gw1"], 16)
            for t in range(NT):
                drained(pe, ("ahT", t))
            for f in range(HC):
                for g, (g0, w) in enumerate(GROUPS):
                    out_b, full = claim(pe, ("h1T", f, g))
                    for c in range(C):
                        last = nc.tensor.matmul(out_b[:, 0:w], gw1[:, c, f * P:f * P + P], ah_T[:, c, g0:g0 + w], start=(c == 0), stop=(c == C - 1))
                    last.then_inc(full, 1)
            for f in range(HC):
                for g in range(len(GROUPS)):
                    drained(pe, ("h1T", f, g))
            pe.wait_ge(loads["gw2_first"], 16)
            pe.wait_ge(loads["gw2_last"], 16)
            for t in range(NT):
                project("y2", t, h1_T, gw2)
            for t in range(NT):
                drained(pe, ("y2", t))
            for t in range(NT):
                aggregate("agg2", z2_rows, t)
            pe.wait_ge(loads["w_qkv"], 16)
            for m in range(C):
                for g, (g0, w) in enumerate(GROUPS):
                    out_b, full = claim(pe, ("kT", m, g))
                    for c in range(C):
                        last = nc.tensor.matmul(out_b[:, 0:w], w_qkv[:, c, D + m * P:D + m * P + P], xn_T[:, c, g0:g0 + w],
                                                start=(c == 0), stop=(c == C - 1))
                    last.then_inc(full, 1)
            for t in range(NT):
                project("q", t, xn_T, [w_qkv[:, c, 0:D] for c in range(C)])
            for t in range(NT):
                project("v", t, xn_T, [w_qkv[:, c, 2 * D:3 * D] for c in range(C)])
            for m in range(C):
                for g in range(len(GROUPS)):
                    drained(pe, ("kT", m, g))
            for t in range(NT):
                out_b, full = claim(pe, ("ek", t))
                r = rows(t)
                for c in range(C):
                    last = nc.tensor.transpose(out_b[0:r, c * P:c * P + P], ek_T[:, c, t * P:t * P + r], ident[:, :])
                last.then_inc(full, 1)
            for t in range(NT):
                drained(pe, ("v", t))
                drained(pe, ("ek", t))
            out_b, full = claim(pe, ("ctxT",))
            for c in range(C):
                for t in range(NT):
                    r = slice(0, rows(t))
                    last = nc.tensor.matmul(out_b[:, c * P:c * P + P], vx_rows[r, t, c * P:c * P + P],
                                            ek_rows[r, t, c * P:c * P + P], start=(t == 0), stop=(t == NT - 1))
            last.then_inc(full, 1)
            drained(pe, ("ctxT",))
            pe.wait_ge(loads["w_att"], 16)
            for c in range(C):
                out_b, full = claim(pe, ("m5", c))
                nc.tensor.matmul(out_b, kv_T[:, c, :], w_att[:, c, :], start=True, stop=True).then_inc(full, 1)
            pe.wait_ge(k_scale_ready, 1)
            for t in range(NT):
                pe.wait_ge(q_ready, t + 1)
                transposes(("qT", t), chunks(q_rows[:, t, :]))
            for c in range(C):
                drained(pe, ("m5", c))
            for t in range(NT):
                drained(pe, ("qT", t))
                project("att", t, q_T, [m5[:, c, :] for c in range(C)])
            for t in range(NT):
                pe.wait_ge(ln_ready[5], t + 1)
                transposes(("lastT", t), chunks(last_rows[:, t, :]))
            pe.wait_ge(mean_ready, 1)
            out_b, full = claim(pe, ("route",))
            for c in range(C):
                last = nc.tensor.matmul(out_b[0:1, 0:PARTS], mean_col[:, c:c + 1], routers_T[:, c, EX:EX + PARTS],
                                        start=(c == 0), stop=(c == C - 1))
            last.then_inc(full, 1)
            pe.wait_ge(route_weighted, 1)
            out_b, full = claim(pe, ("expert_w",))
            nc.tensor.matmul(out_b[:, 0:SE], ones_col[0:1, :].to_broadcast([1, P]), expert_w[:, 0, :], start=True, stop=True)
            nc.tensor.matmul(out_b[0:SE, SE:SE + 1], expert_w[:, 0, :], ones_col[0:1, :], start=True, stop=True).then_inc(full, 1)
            drained(pe, ("expert_w",))
            pe.wait_ge(loads["shared_b2"], 16)
            out_b, full = claim(pe, ("b2_mix",))
            nc.tensor.matmul(out_b, expert_w_col[:, :].to_broadcast([SE, P]), expert_b2[0:SE, :], start=True, stop=True).then_inc(full, 1)
            pe.wait_ge(loads["sw1"], 16 * SE)
            for t in range(NT):
                drained(pe, ("lastT", t))
            for key in ffn_order():
                out_b, full = claim(pe, key)
                if key[0] == "up":
                    _, g, j = key
                    n, r, n0 = len(TURN_TILES[g]) * P, hidden_rows(j), TURN_TILES[g][0] * P
                    for c in range(C):
                        last = nc.tensor.matmul(out_b[0:r, 0:n], sw1_cols[:, c, j * P:j * P + r], xn_T[:, c, n0:n0 + n],
                                                start=(c == 0), stop=(c == C - 1))
                else:
                    t = key[1]
                    g, off = t * P // TG, t * P % TG
                    if off == 0:
                        for j in range(SC):
                            drained(pe, ("up", g, j))
                    if t == 0:
                        pe.wait_ge(sw2_ready, SC)
                    for j in range(SC):
                        r = hidden_rows(j)
                        last = nc.tensor.matmul(out_b, shid[g % 2][0:r, j, off:off + P], sw2[j][0:r, :], start=(j == 0), stop=(j == SC - 1))
                last.then_inc(full, 1)


def kernel(**inputs):
    import numpy as _np
    import concourse.bacc as _bacc
    from concourse import mybir as _mybir
    from concourse.bass_utils import run_bass_kernel_spmd as _run

    nc = _bacc.Bacc("TRN2", target_bir_lowering=False, num_devices=1)
    arrays, aps = {}, {}
    for name, value in inputs.items():
        a = _np.ascontiguousarray(value)
        arrays[f"in_{name}"] = a
        aps[name] = nc.dram_tensor(f"in_{name}", a.shape, _mybir.dt.from_np(a.dtype), kind="ExternalInput").ap()
    out = nc.dram_tensor("out_x", aps["x"].shape, F32, kind="ExternalOutput").ap()
    graph_block_kernel(nc, aps, out)
    r = _run(nc, [arrays], core_ids=[0])
    return r.results[0]["out_x"]
```

```python
import math
from contextlib import ExitStack

import concourse.bass as bass
from concourse import mybir

P = 128
F32 = mybir.dt.float32
BF16 = mybir.dt.bfloat16
F16 = mybir.dt.float16
F32R = mybir.dt.float32r
I32 = mybir.dt.int32
ALU = mybir.AluOpType
ACT = mybir.ActivationFunctionType
AX_X = mybir.AxisListType.X
RMAX = bass.bass_isa.ReduceOp.max

SILU_2MOM = 1.679177
AVG_NUM_NEIGHBORS = 10.0
LN_EPS = 1e-5


class BankRing:

    def __init__(self, banks):
        self.banks, self.n, self.at = banks, 0, {}

    def plan(self, keys):
        for key in keys:
            self.at[key] = (self.n % self.banks, self.n // self.banks)
            self.n += 1

    def uses(self, bank):
        return self.n // self.banks + (self.n % self.banks > bank)


def graph_block_kernel(nc, A, out):
    N, D = A["x"].shape
    E = A["src"].shape[0]
    NT = -(-N // P)
    NP = NT * P
    C = D // P
    MUL = A["L0_gnn_W_up0"].shape[0]
    HID = A["L0_gnn_W_mlp2"].shape[0]
    R = A["edge_attr_8"].shape[1]
    Y = A["edge_attr_4"].shape[1]
    J = 4
    U = J * P
    UNITS = -(-E // U)
    FULL = E // U
    PAIRS = 3
    TURNS = -(-UNITS // (2 * PAIRS))
    EPAD = TURNS * 2 * PAIRS * U
    HEADS, HD = 8, D // 8

    def rows(t):
        return min(P, N - t * P)

    ctx = ExitStack()
    with ctx:
        def sb(name, shape, dt=F32):
            return ctx.enter_context(nc.sbuf_tensor(name, shape, dt))

        def sem(name):
            return ctx.enter_context(nc.semaphore(name))

        def dram(name, shape, dt=F32):
            return nc.dram_tensor(name, shape, dt).ap()

        sender_table = dram("sender_table", (NP, D))
        edge_in = dram("edge_in", (EPAD, R))
        edge_hidden = dram("edge_hidden", (2, TURNS * 2 * PAIRS, 2, P, P))

        ident = sb("ident", [P, P])
        table = sb("table", [P, NP])
        iota_nodes = table[:, 0:NP // 2].bitcast(F16)
        assert NP <= 2048
        block_lo = sb("block_lo", [P, NT])
        unit_id = sb("unit_id", [P, 1])
        zeros16 = sb("zeros16", [P, D], BF16)
        x_rows = sb("x_rows", [P, NT, D])
        xn_T = sb("xn_T", [P, C, NP])
        stats = sb("stats", [P, NT, 6])
        meanvar = sb("meanvar", [P, NT, 2])
        rstd = sb("rstd", [P, NT])
        big_a = sb("big_a", [P, NT * NP])
        big_b = sb("big_b", [P, NT * NP])
        ln_rows = big_a[:, 0:NT * D].rearrange("p (t d) -> p t d", d=D)
        sender_rows = big_a[:, NT * D:2 * NT * D].rearrange("p (t d) -> p t d", d=D)
        k_rows = big_b[:, 0:NT * D].rearrange("p (t d) -> p t d", d=D)
        v_rows = big_b[:, NT * D:2 * NT * D].rearrange("p (t d) -> p t d", d=D)
        adj_rows = big_a[:, :].rearrange("p (t n) -> p t n", n=NP)
        msg_rows = big_b[:, 0:NT * 2 * D].rearrange("p (t d) -> p t d", d=2 * D)

        with ExitStack() as overlay:
            def sb_r(name, shape):
                return overlay.enter_context(nc.sbuf_tensor(name, shape, F32R))

            h3_hi = [sb_r(f"h3_hi{a}", [P, 2, 2, P]) for a in range(PAIRS)]
            h3_lo = [sb_r(f"h3_lo{a}", [P, 2, 2, P]) for a in range(PAIRS)]
            h3_slot = [sb_r(f"h3_slot{q}", [P, 2, P]) for q in range(2)]
            w4_hi = sb_r("w4_hi", [P, 4 * MUL])
            w4_lo = sb_r("w4_lo", [P, 4 * MUL])
        OVERLAY = 2 * PAIRS * 4 * P + 2 * 2 * P + 2 * 4 * MUL
        wide = sb("wide", [P, 5 * C * D])

        def weight(region, i):
            return region[:, i * C * D:(i + 1) * C * D].rearrange("p (c d) -> p c d", d=D)

        spare_a, spare_b = big_a[:, 2 * NT * D:], big_b[:, 2 * NT * D:]
        w_rows = {"Wk": weight(wide, 0), "Wv": weight(wide, 1), "Wl": weight(wide, 2), "Wq": weight(big_a, 0)}
        w_T = {"Wk": weight(wide, 3), "Wv": weight(wide, 4), "Wl": weight(spare_a, 0)}
        m2, m3 = weight(wide, 0), weight(wide, 1)
        mix_bias = sb("mix_bias", [P, D])
        w_up = sb("w_up", [P, 2, MUL])
        bq_col = sb("bq_col", [P, C])
        b_row = {n: sb(f"{n}_row", [P, D]) for n in ("bk", "bv", "bl")}
        kv_T = sb("kv_T", [P, C, P])
        w_mlp1 = sb("w_mlp1", [J * R, 2, 2 * HID])
        w_mlp2 = sb("w_mlp2", [P, P])
        w_mlp3 = sb("w_mlp3", [P, P])
        w_mlp4 = sb("w_mlp4", [P, 4 * MUL])
        w_out = sb("w_out", [P, 2, 2, MUL])

        dst_units = big_b[0:UNITS, 0:U].bitcast(I32)
        dst_unitf = big_b[0:UNITS, U:2 * U]
        unit_max = sb("unit_max", [UNITS, 1])
        unit_min = sb("unit_min", [UNITS, 1])
        touch = sb("touch", [UNITS, 4, NT])
        reach = sb("reach", [UNITS, 2 * NT])
        reach_all = sb("reach_all", [UNITS, 2 * NT])
        span_f = sb("span_f", [1, 2, NT])
        span = sb("span", [1, 2, NT], I32)
        dst_int = sb("dst_int", [P, UNITS, J], I32)
        src_int = sb("src_int", [P, UNITS, J], I32)
        edges = spare_b[:, 0:UNITS * J * (Y + 2)].rearrange("p (u k) -> p u k", u=UNITS)
        class Space:
            def __init__(self, region):
                self.region, self.used = region, 0

            def take(self, n):
                self.used += n
                assert self.used <= self.region.shape[-1]
                return self.region[:, self.used - n:self.used]

        mlp_space = Space(wide[:, OVERLAY:])
        ea_slot = [mlp_space.take(2 * J * R).rearrange("p (h k) -> p h k", h=2) for a in range(PAIRS)]
        ea_T = [mlp_space.take(2 * P)[0:J * R, :] for a in range(PAIRS)]
        h_slot = [mlp_space.take(4 * P) for a in range(PAIRS)]
        h3_out = [mlp_space.take(4 * P).rearrange("p (u q n) -> p u q n", u=2, q=2) for a in range(PAIRS)]
        edge_space = Space(xn_T[:, :, :].rearrange("p c n -> p (c n)")[:, 2 * D:])
        edge_slot = edge_space.take(J * (Y + 2))
        idx_slot = [sb(f"idx_slot{j}", [P, 1], I32) for j in range(J)]
        sent = [edge_space.take(D) for j in range(J)]
        hot_f = edge_space.take(2 * P).rearrange("p (k n) -> p k n", k=2)
        hot_y = edge_space.take(2 * Y * P).rearrange("p (k y n) -> p k y n", k=2, y=Y)
        dot = edge_space.take(2 * MUL).rearrange("p (k n) -> p k n", k=2)
        edge_space2 = Space(wide[:, OVERLAY:])
        scaled = edge_space2.take(2 * 3 * MUL).rearrange("p (k m u) -> p k m u", k=2, m=3)
        prod = edge_space2.take(2 * 6 * MUL).rearrange("p (k n) -> p k n", k=2)
        hot_dst = edge_space2.take(P).bitcast(BF16).rearrange("p (k n) -> p k n", k=2)
        hot_src = edge_space2.take(NP).bitcast(BF16).rearrange("p (k n) -> p k n", k=2)
        msg_T = wide[:, 0:4 * D].rearrange("p (k n) -> p k n", k=2)
        assert edge_space.used <= C * NP - 2 * D and max(mlp_space.used, edge_space2.used) <= 5 * C * D - OVERLAY

        psum = ctx.enter_context(nc.psum_tensor("psum", [P, 8, 512], F32))
        msg_psum = psum[:, 0:2, :].rearrange("p k n -> p (k n)")
        adj_psum = psum[:, 2:5, :].rearrange("p k n -> p (k n)")
        tile_w = [psum[:, 5 + k, :] for k in range(2)]
        ring = BankRing(8)

        ring.plan([("wT", w, c) for w in ("Wk", "Wv", "Wl") for c in range(C)])
        ring.plan([("xT", t) for t in range(NT)])
        ring.plan([("sender", t) for t in range(NT)])
        ring.plan([(w, t) for t in range(NT) for w in ("Wk", "Wv")])
        ring.plan([("kvT",)])
        ring.plan([("m2", c) for c in range(C)])
        ring.plan([("m3", c) for c in range(C)] + [("mix_bias",)])
        ring.plan([("mix", t) for t in range(NT)])
        before_edges = [ring.uses(b) for b in range(8)]
        def chain_order():
            yield from [("routersT",), ("expert_biasT",), ("msgT0", 0), ("msgT1", 0), ("router_bias",)]
            for t in range(NT):
                if t + 1 < NT:
                    yield from [("msgT0", t + 1), ("msgT1", t + 1)]
                yield ("conv", t)
                if t >= 3:
                    yield ("logits", t - 3)
                if t >= 2:
                    yield ("hT", t - 2)
            for t in range(NT - 2, NT):
                yield from [("logits", t - 1), ("hT", t)]
            yield ("logits", NT - 1)
        ring.plan(list(chain_order()))

        bank_full = [sem(f"bank_full{b}") for b in range(8)]
        bank_free = [sem(f"bank_free{b}") for b in range(8)]
        loads = {}

        def load_sem(name):
            loads[name] = sem(f"{name}_loaded")
            return loads[name]

        for n in ("x", "x_rest", "w_up", "Wk", "Wv", "Wl", "Wq", "bq", "bk", "bv", "bl", "mlp", "w_out", "dst_units",
                  "edge_tables", "edge_in"):
            load_sem(n)
        consts_ready = sem("consts_ready")
        ident_zeroed = sem("ident_zeroed")
        padding_ready = sem("padding_ready")
        dve_step = sem("dve_step")
        stats_ready = sem("stats_ready")
        std_ready = sem("std_ready")
        ln_ready = {n: sem(f"ln_ready{n}") for n in (0, 2, 3, 5)}
        gathers_started = sem("gathers_started")
        sender_stored = sem("sender_stored")
        bq_ready = sem("bq_ready")
        reach_ready = sem("reach_ready")
        reach_max_ready = sem("reach_max_ready")
        span_ready = sem("span_ready")
        ea_loaded = [sem(f"ea_loaded{a}") for a in range(PAIRS)]
        ea_transposed = [sem(f"ea_transposed{a}") for a in range(PAIRS)]
        ea_T_ready = [sem(f"ea_T_ready{a}") for a in range(PAIRS)]
        layer_done = [sem(f"layer_done{a}") for a in range(PAIRS)]
        silu_done = [sem(f"silu_done{a}") for a in range(PAIRS)]
        h3_stored = [sem(f"h3_stored{a}") for a in range(PAIRS)]
        h3_out_free = [sem(f"h3_out_free{a}") for a in range(PAIRS)]
        h3_split = [sem(f"h3_split{a}") for a in range(PAIRS)]
        h3_loaded = [sem(f"h3_loaded{q}") for q in range(2)]
        w4_ready = sem("w4_ready")
        hi_ready = [sem(f"hi_ready{a}") for a in range(PAIRS)]
        dot_ready = sem("dot_ready")
        hot_ready = sem("hot_ready")
        hot_y_ready = sem("hot_y_ready")
        scaled_ready = sem("scaled_ready")
        weights_done = sem("weights_done")
        scatter_done = sem("scatter_done")
        products_done = sem("products_done")
        edge_slot_ready = sem("edge_slot_ready")
        gathered = [sem(f"gathered{j}") for j in range(J)]
        idx_ready = sem("idx_ready")
        msg_flushed = sem("msg_flushed")
        adj_flushed = sem("adj_flushed")
        out_stored = sem("out_stored")

        EX = A["L0_ffn_w_r"].shape[0]
        TOP = 2
        FH = A["L0_ffn_W1"].shape[2]
        FC = FH // P
        TILES = (TOP * N + EX * P) // P
        H1 = A["L1_gnn_b1"].shape[0]
        HC = H1 // P
        SE, SF = A["L1_ffn_b1"].shape
        SC = -(-SE * SF // P)
        PARTS = A["L1_ffn_router_w"].shape[0]
        GROUPS = [(g, min(512, NP - g)) for g in range(0, NP, 512)]
        KEY_COLS = [min(w, N - g) for g, w in GROUPS]

        adj_dram = dram("adj_dram", (P, NT, NP))
        tokens_sorted = dram("tokens_sorted", ((TILES + 2) * P, D))
        mixed_sorted = dram("mixed_sorted", (TILES * P, D))

        late = Space(table[:, 16:])
        late_dst = Space(dst_int[:, :, :].rearrange("p u j -> p (u j)").bitcast(F32))
        late_src = Space(src_int[:, :, :].rearrange("p u j -> p (u j)").bitcast(F32))
        ident16 = sb("ident16", [P, P], BF16)
        before_me = late_src.take(P)
        ones_col = sb("ones_col", [P, 1])
        real_row = sb("real_row", [P, 1])
        dinv = sb("dinv", [P, NT])
        bias_rows = late_src.take(P)[0:HC + SC, :]
        bias_T = late.take(HC + SC)
        expert_bias_T = late.take(EX * FC)
        expert_b2 = w_mlp4[0:EX, :]
        routers_T = late.take(C * (EX + PARTS + 2)).rearrange("p (a b) -> p a b", b=(EX + PARTS + 2))
        router_bias = sb("router_bias", [P, EX])
        logits = late.take(NT * EX).rearrange("p (a b) -> p a b", b=EX)
        top_val = late.take(NT * 8).rearrange("p (a b) -> p a b", b=8)
        top_idx = late.take(NT * 8).bitcast(mybir.dt.uint32).rearrange("p (a b) -> p a b", b=8)
        choice_f = late.take(TOP * NT).rearrange("p (a b) -> p a b", b=NT)
        chosen = late.take(TOP * NT * EX).rearrange("p (k a b) -> p k a b", k=TOP, b=EX)
        routers_scaled = late_dst.take(C * EX).rearrange("p (c e) -> p c e", c=C)
        member = late.take(NT * EX).rearrange("p (a b) -> p a b", b=EX)
        members_before = late.take((NT + 1) * EX).rearrange("p (a b) -> p a b", b=EX)
        place = late_dst.take(NT * EX).rearrange("p (a b) -> p a b", b=EX)
        tile_tests = late_dst.take(EX * NT).rearrange("p (a b) -> p a b", b=NT)
        first_tile = late.take(EX + 1)
        expert_tiles = late.take(EX)
        place_base = late.take(EX)
        first_tile_int = late.take(EX + 1)[0:1, :].bitcast(I32)
        slot_f = late.take(TOP * NT).rearrange("p (a b) -> p a b", b=NT)
        slot_int = late.take(TOP * NT).bitcast(I32).rearrange("p (a b) -> p a b", b=NT)
        gate = late.take(TOP * NT).rearrange("p (a b) -> p a b", b=NT)
        gap = late.take(NT)
        ln_pair = late.take(2 * NT).rearrange("p (t k) -> p t k", k=2)
        ln_root = late.take(2 * NT).rearrange("p (t k) -> p t k", k=2)
        x_scale = late.take(NT)
        x_shift = late.take(NT)
        gate_by_slot = late.take(TOP * NT).rearrange("p (k t) -> p k t", k=TOP)
        slot_order = late.take(NT)
        slot_sorted = late.take(TOP * NT).rearrange("p (k t) -> p k t", k=TOP)

        xn_flat = xn_T[:, :, :].rearrange("p c n -> p (c n)")
        router_rows = xn_flat[0:EX + PARTS + 2, 0:D]
        expert_bias_rows = xn_flat[:, D:D + P]
        def grid(region, a, b, k):
            return region[:, a:a + b * k].rearrange("p (a k) -> p a k", k=k)

        adj_T = grid(big_b, 0, NT, NP)
        hx_rows = grid(wide, NT * D, NT, D)
        spare_x = FC * P + 3 * D
        gates_T = xn_flat[0:EX, spare_x:spare_x + NP]
        token_gates = grid(xn_flat, spare_x + NP, NT, EX)
        HALF = FC // 2
        ew1 = [grid(r, 0, C, FH) for r in (big_a, big_b)]
        ew2_lo = [grid(r, C * FH, HALF, D) for r in (big_a, big_b)]
        ew2_hi = [grid(wide, a * HALF * D, HALF, D) for a in range(2)]
        hid = grid(xn_flat, 0, FC, P)
        tile_rows = xn_flat[:, FC * P:FC * P + D]
        tile_T = grid(xn_flat, FC * P + D, C, P)
        tile_out = xn_flat[:, FC * P + 2 * D:FC * P + 3 * D]
        first_rows = [wide[:, t * D:(t + 1) * D] if t < HALF else wide[:, (HALF + t) * D:(HALF + t + 1) * D] for t in range(NT)]
        second_rows = [big_b[:, t * D:(t + 1) * D] for t in range(NT)]
        degree = late.take(NT)
        adj_in = grid(big_a, 0, NT, NP)
        xn2_rows = grid(wide, 0, NT, D)
        z_rows = grid(wide, NT * D, NT, D)
        ah_T = grid(big_b, 0, C, NP)
        ah_rows = grid(big_b, NT * D, 2, D)
        gw1 = grid(big_b, (NT + 2) * D, C, H1)
        h1_T = grid(wide, 0, HC, NP)
        GW2_FIRST = 5
        gw2 = [big_b[:, (NT + 2) * D + C * H1 + i * D:(NT + 2) * D + C * H1 + (i + 1) * D] for i in range(GW2_FIRST)]
        gw2 += [big_b[:, i * D:(i + 1) * D] for i in range(HC - GW2_FIRST)]
        z2_rows = grid(big_b, (HC - GW2_FIRST) * D, NT, D)
        conv_out = grid(big_b, (HC - GW2_FIRST + NT) * D, 2, D)
        w_qkv = grid(wide, 0, C, 3 * D)
        w_att = grid(wide, 3 * C * D, C, D)
        m5 = grid(wide, 4 * C * D, C, D)
        EK = (HC - GW2_FIRST + NT) * D
        ek_T = grid(big_b, EK, C, NP)
        q_T = ek_T
        ek_rows = grid(big_b, 0, NT, D)
        q_rows = grid(big_a, 0, NT, D)
        att_rows = q_rows
        vx_rows = grid(big_a, NT * D, NT, D)
        k_max3 = late.take(C * len(GROUPS)).rearrange("p (a b) -> p a b", b=len(GROUPS))
        k_max = late.take(C)
        k_sum = late.take(C)
        k_scale = late.take(C)
        q_max = late.take(HEADS)
        q_sum = late.take(2 * HEADS).rearrange("p (a h) -> p a h", a=2)
        last_rows = vx_rows
        sw1 = wide[:, 0:C * SE * SF].rearrange("p (c e f) -> p c e f", c=C, e=SE)
        sw1_cols = wide[:, 0:C * SE * SF].rearrange("p (c h) -> p c h", c=C)
        SW2_FIRST = EK // D
        sw2 = [big_b[:, j * D:(j + 1) * D] for j in range(SW2_FIRST)]
        sw2 += [big_a[:, (2 * NT + j) * D:(2 * NT + j + 1) * D] for j in range(SC - SW2_FIRST)]
        UP_BANKS, Y_BANK, T_BANK = 4, 4, 5
        TG = 2 * P
        shid = [big_a[:, a * SC * TG:(a + 1) * SC * TG].rearrange("p (j n) -> p j n", n=TG) for a in range(2)]
        mean_col = late.take(C)
        route = late.take(PARTS)[0:1, :]
        route_top = late.take(8)[0:1, :]
        route_idx = late.take(8)[0:1, :].bitcast(mybir.dt.uint32)
        route_f = late.take(8)[0:1, :]
        route_coef = late.take(2 * PARTS)[0:1, :].rearrange("p (a b) -> p a b", b=PARTS)
        part_weights = late_src.take(SE * PARTS)[0:1, :].rearrange("p (a b) -> p a b", b=PARTS)
        part_prod = late.take(SE * PARTS)[0:1, :].rearrange("p (a b) -> p a b", b=PARTS)
        expert_w = late.take(2 * SE)[0:1, :].rearrange("p (a b) -> p a b", b=SE)
        expert_w_all = late.take(SE)
        expert_w_col = late.take(1)[0:SE, :]
        hidden_id = sb("hidden_id", [P, SC])
        past = late_dst.take((SE + 1) * SC).rearrange("p (a b) -> p a b", b=SC)
        hidden_w = late.take(SC)

        def hidden_rows(j):
            return min(P, SE * SF - j * P)

        ADJ_FIRST = NT // 3
        ring.plan([("adjT", s, g) for s in range(ADJ_FIRST) for g in range(len(GROUPS))] + [("rank",)])
        ring.plan([("adjT", s, g) for s in range(ADJ_FIRST, NT) for g in range(len(GROUPS))])
        ring.plan([("gateT", g) for g in range(len(GROUPS))] + [("b2", t) for t in range(NT)] + [("biasT",)])
        before_experts = [ring.uses(b) for b in range(8)]
        AGG_OPEN = 6
        ring.plan([("agg1", t) for t in range(AGG_OPEN)])

        def agg_order():
            for t in range(AGG_OPEN, NT):
                yield ("agg1", t)
                u = 2 * (t - AGG_OPEN)
                yield from [("ahT", u), ("ahT", u + 1)]
            late_tiles = range(2 * (NT - AGG_OPEN), NT)
            for t in late_tiles:
                yield from [("xn2T", t - late_tiles[0]), ("ahT", t)]
            for t in range(len(late_tiles), NT):
                yield ("xn2T", t)
        ring.plan(list(agg_order()))
        ring.plan([("h1T", f, g) for f in range(HC) for g in range(len(GROUPS))])
        ring.plan([(k, t) for k in ("y2", "agg2") for t in range(NT)])
        ring.plan([("kT", m, g) for m in range(C) for g in range(len(GROUPS))])
        ring.plan([("q", t) for t in range(NT)] + [("v", t) for t in range(NT)] + [("ek", t) for t in range(NT)])
        ring.plan([("ctxT",)] + [("m5", c) for c in range(C)])
        ring.plan([("qT", t) for t in range(NT)] + [("att", t) for t in range(NT)])
        ring.plan([("lastT", t) for t in range(NT)])
        TURN_TILES = [[t for t in range(g, min(g + TG // P, NT))] for g in range(0, NT, TG // P)]
        TG_N = len(TURN_TILES)

        def ffn_order():
            for g in range(TG_N + 1):
                if g == 1:
                    yield ("route",)
                for j in range(SC if g < TG_N else 0):
                    if (g, j) == (1, SC // 2):
                        yield from [("expert_w",), ("b2_mix",)]
                    yield ("up", g, j)
                if g:
                    yield from [("down", t) for t in TURN_TILES[g - 1]]
        ring.plan(list(ffn_order()))

        for n in ("routers", "router_bias", "expert_bias", "biases", "ln_g", "ln_b", "gnn_b2", "expert_b2", "adj_T",
                  "gw1", "gw2_first", "gw2_last", "w_qkv", "w_att", "b_out", "ln_scale", "shared_b2", "sw1", "sw2"):
            load_sem(n)
        adj_stored = sem("adj_stored")
        tokens_zeroed = sem("tokens_zeroed")
        members_ready = sem("members_ready")
        gap_ready = sem("gap_ready")
        gap_exp = sem("gap_exp")
        gates_ready = sem("gates_ready")
        tiles_ready = sem("tiles_ready")
        slots_ready = sem("slots_ready")
        dinv_ready = sem("dinv_ready")
        z_ready = sem("z_ready")
        routers_ready = sem("routers_ready")
        rows_scattered = sem("rows_scattered")
        ew1_loaded = [sem(f"ew1_loaded{a}") for a in range(2)]
        ew2_loaded = [sem(f"ew2_loaded{a}") for a in range(2)]
        tile_loaded = sem("tile_loaded")
        tile_transposed = sem("tile_transposed")
        tile_T_ready = sem("tile_T_ready")
        up_done = sem("up_done")
        gelu_done = sem("gelu_done")
        down_done = sem("down_done")
        tile_out_ready = sem("tile_out_ready")
        tile_stored = sem("tile_stored")
        mixed_zeroed = sem("mixed_zeroed")
        tile_out_free = sem("tile_out_free")
        experts_started = sem("experts_started")
        first_loaded = sem("first_loaded")
        second_loaded = [sem(f"second_loaded{g}") for g in range(NT // 2)]
        k_max_ready = sem("k_max_ready")
        ek_ready = sem("ek_ready")
        k_scale_ready = sem("k_scale_ready")
        q_exp = sem("q_exp")
        q_ready = sem("q_ready")
        mean_ready = sem("mean_ready")
        route_exp = sem("route_exp")
        route_weighted = sem("route_weighted")
        hidden_w_ready = sem("hidden_w_ready")
        sw2_ready = sem("sw2_ready")

        def partitions(n, largest):
            if n == 0:
                yield ()
            for part in range(min(n, largest), 0, -1):
                for rest in partitions(n - part, part):
                    yield (part, *rest)

        block = ctx.enter_context(nc.Block())

        def bank(key):
            return psum[:, ring.at[key][0], :]

        def claim(pe, key):
            b, n = ring.at[key]
            if n:
                pe.wait_ge(bank_free[b], n)
            return psum[:, b, :], bank_full[b]

        def filled(eng, key):
            b, n = ring.at[key]
            eng.wait_ge(bank_full[b], n + 1)
            return psum[:, b, :], bank_free[b]

        def drained(eng, key):
            b, n = ring.at[key]
            eng.wait_ge(bank_free[b], n + 1)

        def block_span(eng, b):
            lo = eng.value_load(span[0:1, 0, bass.ds(b, 1)], min_val=0, max_val=UNITS - 1)
            hi = eng.value_load(span[0:1, 1, bass.ds(b, 1)], min_val=1, max_val=UNITS)
            return lo, hi

        def expert_bounds(eng, i):
            return [eng.value_load(first_tile_int[0:1, bass.ds(2 * i + k, 1)], min_val=min(k, 1), max_val=TILES - (k < 2))
                    for k in range(3)]

        def step_counter(eng, name):
            step = eng.alloc_register(name)
            eng.reg_mov(step, 0)
            return step

        def next_step(eng, step):
            eng.reg_add(step, step, 1)
            return eng.snap(step, min_val=1, max_val=NT * UNITS)

        tile_cols = [slice(t * P, t * P + P) for t in range(NT)]
        comp = [slice(0, MUL)] + [slice(MUL + m, D, 3) for m in range(3)]
        PAD_DMAS = -(-(EPAD - E) // (D // 2 // R))
        TABLE_DMAS = 3 * (1 + ((E - FULL * U) // J > 0) + ((E - FULL * U) % J > 0))

        @block.sync
        def _(sp):
            sp.wait_ge(padding_ready, 1)
            for name, t0, t1 in (("x", 0, NT // 2), ("x_rest", NT // 2, NT - 1)):
                sp.dma_start(x_rows[:, t0:t1, :], A["x"][t0 * P:t1 * P, :].rearrange("(t p) d -> p t d", p=P))\
                    .then_inc(loads[name], 16)
            sp.dma_start(x_rows[0:rows(NT - 1), NT - 1, :], A["x"][(NT - 1) * P:N, :]).then_inc(loads["x_rest"], 16)
            for w in ("Wk", "Wv", "Wl"):
                sp.dma_start(w_rows[w], A[f"L0_mix_{w}"].rearrange("(c p) d -> p c d", p=P)).then_inc(loads[w], 16)
            sp.dma_start(w_up[:, 0, :], A["L0_gnn_W_up0"]).then_inc(loads["w_up"], 16)
            sp.dma_start(w_up[:, 1, :], A["L0_gnn_W_up1"]).then_inc(loads["w_up"], 16)
            for b in ("bk", "bv", "bl"):
                sp.dma_start(b_row[b][:, :], A[f"L0_mix_{b}"].rearrange("(a d) -> a d", a=1).to_broadcast([P, D]))\
                    .then_inc(loads[b], 16)
            sp.dma_start(bq_col[:, :], A["L0_mix_bq"].rearrange("(c p) -> p c", p=P), allow_slow_non_contiguous=True).then_inc(loads["bq"], 16)
            split = math.gcd(E, 11 * 15 * 2)
            sp.dma_start(edge_in[0:E, :].rearrange("(a b) r -> a (b r)", a=split),
                         A["edge_attr_8"].rearrange("(a b) r -> a (b r)", a=split)).then_inc(loads["edge_in"], 16)
            sp.wait_ge(padding_ready, 2)
            zero_row = zeros16[0:1, :].bitcast(F32)
            for e0 in range(E, EPAD, D // 2 // R):
                n = min(D // 2 // R, EPAD - e0)
                sp.dma_start(edge_in[e0:e0 + n, :].rearrange("(a b) r -> a (b r)", a=1), zero_row[:, 0:n * R])\
                    .then_inc(loads["edge_in"], 16)
            sp.wait_ge(padding_ready, 3)
            for j in range(J):
                sp.dma_start(w_mlp1[R * j:R * j + R, j // 2, HID * (j % 2):HID * (j % 2) + HID], A["L0_gnn_W_mlp1"])\
                    .then_inc(loads["mlp"], 16)
            for j in range(2):
                half = slice(HID * j, HID * j + HID)
                sp.dma_start(w_mlp2[half, half], A["L0_gnn_W_mlp2"]).then_inc(loads["mlp"], 16)
                sp.dma_start(w_mlp3[half, half], A["L0_gnn_W_mlp3"]).then_inc(loads["mlp"], 16)
                sp.dma_start(w_mlp4[half, :], A["L0_gnn_W_mlp4"]).then_inc(loads["mlp"], 16)
            for k in range(2):
                sp.dma_start(w_out[:, k, :, :], A[f"L0_gnn_W_out{k}"].rearrange("(c p) v -> p c v", p=P))\
                    .then_inc(loads["w_out"], 16)
            for t in range(NT):
                drained(sp, ("xT", t))
            sp.dma_start(w_rows["Wq"], A["L0_mix_Wq"].rearrange("(c p) d -> p c d", p=P)).then_inc(loads["Wq"], 16)
            for t in range(NT):
                drained(sp, ("sender", t))
            sp.dma_start(sender_table.rearrange("(t p) d -> p t d", p=P), sender_rows).then_inc(sender_stored, 16)
            for h in range(2):
                sp.dma_start(tokens_sorted.rearrange("(t p) d -> p t d", p=P)[:, :, h * (D // 2):(h + 1) * (D // 2)],
                             zeros16[:, :].bitcast(F32).unsqueeze(1).to_broadcast([P, TILES + 2, D // 2])).then_inc(tokens_zeroed, 16)
            sure = -(-TOP * N // P)
            for h in range(2):
                sp.dma_start(mixed_sorted[sure * P:, :].rearrange("(t p) d -> p t d", p=P)[:, :, h * (D // 2):(h + 1) * (D // 2)],
                             zeros16[:, :].bitcast(F32).unsqueeze(1).to_broadcast([P, TILES - sure, D // 2])).then_inc(mixed_zeroed, 16)
            for t in range(NT):
                drained(sp, ("mix", t))
            sp.dma_start(router_rows[0:EX, :], A["L0_ffn_w_r"]).then_inc(loads["routers"], 16)
            sp.dma_start(router_rows[EX:EX + PARTS, :], A["L1_ffn_router_w"]).then_inc(loads["routers"], 16)
            for i, n in enumerate(("L0_ffn_ln_g", "L0_ffn_ln_b")):
                r = EX + PARTS + i
                sp.dma_start(router_rows[r:r + 1, :], A[n].rearrange("(a d) -> a d", a=1)).then_inc(loads["routers"], 16)
            sp.dma_start(expert_bias_rows, A["L0_ffn_b1"].rearrange("e (c f) -> (e c) f", f=P)).then_inc(loads["expert_bias"], 16)

            def spread(dst, name, what):
                sp.dma_start(dst, A[name].rearrange("(a d) -> a d", a=1).to_broadcast([P, A[name].shape[0]]))\
                    .then_inc(loads[what], 16)

            spread(router_bias[:, :], "L0_ffn_b_r", "router_bias")
            spread(b_row["bl"][:, :], "L1_gnn_b2", "gnn_b2")
            for a in range(PAIRS):
                sp.sem_inc(h3_out_free[a], 1)
            with sp.Fori(0, TURNS) as i:
                for a in range(PAIRS):
                    sp.wait_ge(h3_split[a], i + 2)
                    for part, h3 in enumerate((h3_hi[a], h3_lo[a])):
                        sp.dma_start(edge_hidden[part, bass.ds(i * (2 * PAIRS) + 2 * a, 2), :, :, :].rearrange("u q p n -> p (u q) n"),
                                       h3[:, :, :, :].bitcast(F32).rearrange("p u q n -> p (u q) n")).then_inc(h3_stored[a], 16)
                for a in range(PAIRS):
                    sp.wait_ge(h3_stored[a], i * 32 + 32)
                    sp.sem_inc(h3_out_free[a], 1)
            sp.wait_ge(h3_out_free[0], 1 + TURNS)
            sp.wait_ge(h3_out_free[1], 1 + TURNS)
            sp.wait_ge(span_ready, 1)

            def hidden_load(q, unit):
                for part in range(2):
                    sp.dma_start(h3_slot[q][part * HID:(part + 1) * HID, :, :].bitcast(F32),
                                 edge_hidden[part, unit, q, :, :].rearrange("u (j c) n -> c (u j) n", c=HID))\
                        .then_inc(h3_loaded[q], 16)

            step = step_counter(sp, "sp_step")
            with sp.Fori(0, NT) as b:
                lo, hi = block_span(sp, b)
                with sp.Fori(lo, hi) as u:
                    s = next_step(sp, step)
                    for q in range(2):
                        sp.wait_ge(weights_done, s * J + 2 * q + 2)
                        hidden_load(q, bass.ds(u, 1))
            s = next_step(sp, step)
            sp.wait_ge(weights_done, s * J + 2)
            hidden_load(0, slice(0, 1))

            filled(sp, ("routersT",))
            sp.dma_start(expert_b2[:, :], A["L0_ffn_b2"]).then_inc(loads["expert_b2"], 16)
            sp.wait_ge(padding_ready, 4)
            sp.dma_start(bias_rows[0:HC, :], A["L1_gnn_b1"].rearrange("(c f) -> c f", f=P)).then_inc(loads["biases"], 16)
            flat_b1 = A["L1_ffn_b1"].rearrange("e f -> (e f)")
            sp.dma_start(bias_rows[HC:HC + SC - 1, :], flat_b1[0:(SC - 1) * P].rearrange("(c f) -> c f", f=P))\
                .then_inc(loads["biases"], 16)
            sp.dma_start(bias_rows[HC + SC - 1:HC + SC, 0:hidden_rows(SC - 1)],
                         flat_b1[(SC - 1) * P:SE * SF].rearrange("(c f) -> c f", c=1)).then_inc(loads["biases"], 16)

            def expert_weights(a, e, part):
                if part == 1:
                    src = A["L0_ffn_W1"][bass.ds(e, 1), :, :] if not isinstance(e, int) else A["L0_ffn_W1"][e:e + 1, :, :]
                    sp.dma_start(ew1[a], src.rearrange("e (c p) f -> p (e c) f", p=P)).then_inc(ew1_loaded[a], 16)
                else:
                    src = A["L0_ffn_W2"][bass.ds(e, 1), :, :] if not isinstance(e, int) else A["L0_ffn_W2"][e:e + 1, :, :]
                    src = src.rearrange("e (c p) d -> p (e c) d", p=P)
                    if part != "hi":
                        sp.dma_start(ew2_lo[a], src[:, 0:HALF, :]).then_inc(ew2_loaded[a], 16)
                    if part != "lo":
                        sp.dma_start(ew2_hi[a], src[:, HALF:FC, :]).then_inc(ew2_loaded[a], 16)

            for t in range(NT):
                filled(sp, ("conv", t))
            expert_weights(0, 0, "hi")
            for s in range(NT):
                for g in range(len(GROUPS)):
                    drained(sp, ("adjT", s, g))
            sp.wait_ge(stats_ready, 2)
            expert_weights(0, 0, 1)
            sp.wait_ge(rows_scattered, 16 * TOP * NT)
            sp.wait_ge(tile_loaded, 16)
            expert_weights(0, 0, "lo")
            sp.dma_start(adj_dram, adj_T).then_inc(adj_stored, 16)
            sp.wait_ge(adj_stored, 16)
            expert_weights(1, 1, 1)
            expert_weights(1, 1, 2)
            with sp.Fori(0, EX // 2 - 1) as i:
                for a in range(2):
                    end = sp.value_load(first_tile_int[0:1, bass.ds(2 * i + a + 1, 1)], min_val=1, max_val=TILES)
                    sp.wait_ge(down_done, end + 1)
                    expert_weights(a, 2 * i + a + 2, 1)
                    expert_weights(a, 2 * i + a + 2, 2)
            end = sp.value_load(first_tile_int[0:1, EX - 1:EX], min_val=EX - 1, max_val=TILES - 1)
            sp.wait_ge(down_done, end + 1)
            sp.dma_start(adj_in, adj_dram).then_inc(loads["adj_T"], 16)
            sp.wait_ge(second_loaded[-1], 32)
            gw2_rows = A["L1_gnn_W2"].rearrange("(c p) d -> p c d", p=P)
            a0 = (NT + 2) * D + C * H1
            sp.dma_start(grid(big_b, a0, GW2_FIRST, D), gw2_rows[:, 0:GW2_FIRST, :]).then_inc(loads["gw2_first"], 16)
            sp.dma_start(gw1, A["L1_gnn_W1"].rearrange("(c p) f -> p c f", p=P)).then_inc(loads["gw1"], 16)
            filled(sp, ("b2", NT - 1))
            sp.dma_start(expert_b2[0:SE, :], A["L1_ffn_b2"]).then_inc(loads["shared_b2"], 16)
            spread(b_row["bk"][:, :], "L1_mix_b_out", "b_out")
            spread(b_row["bv"][:, :], "L1_mix_ln_scale", "ln_scale")
            for g in range(len(GROUPS)):
                filled(sp, ("h1T", HC - 1, g))
            sp.dma_start(grid(big_b, 0, HC - GW2_FIRST, D), gw2_rows[:, GW2_FIRST:, :]).then_inc(loads["gw2_last"], 16)
            filled(sp, ("y2", NT - 1))
            sp.dma_start(w_qkv, A["L1_mix_w_qkv"].rearrange("(c p) f -> p c f", p=P)).then_inc(loads["w_qkv"], 16)
            sp.dma_start(w_att, A["L1_mix_w_out"].rearrange("(c p) f -> p c f", p=P)).then_inc(loads["w_att"], 16)
            filled(sp, ("m5", C - 1))
            for e in range(SE):
                sp.dma_start(sw1[:, :, e, :], A["L1_ffn_W1"][e].rearrange("(c p) f -> p c f", p=P)).then_inc(loads["sw1"], 16)
            flat_w2 = A["L1_ffn_W2"].rearrange("e f d -> (e f) d")
            sp.dma_start(grid(big_b, 0, SW2_FIRST, D), flat_w2[0:SW2_FIRST * P, :].rearrange("(j p) d -> p j d", p=P))\
                .then_inc(loads["sw2"], 16)
            for j in range(SW2_FIRST, SC):
                r = hidden_rows(j)
                sp.dma_start(sw2[j][0:r, :], flat_w2[j * P:j * P + r, :]).then_inc(loads["sw2"], 16)
            for t in range(NT):
                drained(sp, ("down", t))
                sp.dma_start(out[t * P:t * P + rows(t), :], x_rows[0:rows(t), t, :]).then_inc(out_stored, 16)
            sp.wait_ge(out_stored, 16 * NT)

        @block.gpsimd
        def _(pool):
            nc.gpsimd.memset(x_rows[:, NT - 1, :], 0.0).then_inc(padding_ready, 1)
            nc.gpsimd.memset(zeros16[:, :], 0.0).then_inc(padding_ready, 1)
            nc.gpsimd.memset(w_mlp1[:, :, :], 0.0)
            nc.gpsimd.memset(w_mlp2[:, :], 0.0)
            nc.gpsimd.memset(w_mlp3[:, :], 0.0).then_inc(padding_ready, 1)
            nc.gpsimd.memset(ident[:, :], 0.0).then_inc(ident_zeroed, 1)
            nc.gpsimd.iota(iota_nodes[:, :], [[1, NP]], base=0, channel_multiplier=0,
                           allow_small_or_imprecise_dtypes=True)
            nc.gpsimd.iota(block_lo[:, :], [[P, NT]], base=0, channel_multiplier=0,
                           allow_small_or_imprecise_dtypes=True)
            nc.gpsimd.iota(unit_id[:, :], [[0, 1]], base=0, channel_multiplier=1,
                           allow_small_or_imprecise_dtypes=True)
            pool.wait_ge(ident_zeroed, 1)
            nc.gpsimd.affine_select(out=ident[:, :], in_=ident[:, :], compare_op=ALU.not_equal, fill=1.0, base=0,
                                    pattern=[[-1, P]], channel_multiplier=1).then_inc(consts_ready, 1)
            nc.gpsimd.memset(kv_T[:, :, :], 0.0)
            nc.gpsimd.memset(dst_int[:, :, :], -1)
            nc.gpsimd.memset(src_int[:, :, :], 0)
            nc.gpsimd.memset(edges[:, :, :], 0.0).then_inc(consts_ready, 1)
            pool.wait_ge(consts_ready, 2)
            tail = E - FULL * U
            q = tail // J
            for tab, a, w in ((dst_int[:, :, :], A["dst"], 1), (src_int[:, :, :], A["src"], 1),
                              (edges[:, :, J:J + J * Y], A["edge_attr_4"].rearrange("e y -> (e y)"), Y)):
                pool.dma_start(tab[:, 0:FULL, :], a[0:FULL * U * w].rearrange("(u p k) -> p u k", p=P, k=J * w))\
                    .then_inc(loads["edge_tables"], 16)
                if q:
                    pool.dma_start(tab[0:q, FULL, :], a[FULL * U * w:(FULL * U + q * J) * w]
                                   .rearrange("(p k) -> p k", k=J * w)).then_inc(loads["edge_tables"], 16)
                if tail % J:
                    pool.dma_start(tab[q:q + 1, FULL, 0:tail % J * w], a[(FULL * U + q * J) * w:E * w]
                                   .rearrange("(p k) -> p k", p=1)).then_inc(loads["edge_tables"], 16)
            pool.dma_start(dst_units[0:UNITS - 1, :], A["dst"][0:(UNITS - 1) * U].rearrange("(u k) -> u k", k=U))\
                .then_inc(loads["dst_units"], 16)
            pool.dma_start(dst_units[UNITS - 1:UNITS, :], A["dst"][E - U:E].rearrange("(u k) -> u k", k=U))\
                .then_inc(loads["dst_units"], 16)
            nc.gpsimd.memset(ones_col[:, :], 1.0)
            nc.gpsimd.iota(hidden_id[:, :], [[P, SC]], base=0, channel_multiplier=1, allow_small_or_imprecise_dtypes=True)
            nc.gpsimd.tensor_scalar(real_row[:, :], unit_id[:, :], float(rows(NT - 1)), None, ALU.is_lt)
            nc.gpsimd.tensor_copy(ident16[:, :], ident[:, :]).then_inc(consts_ready, 1)
            pool.wait_ge(reach_ready, 1)
            nc.gpsimd.partition_all_reduce(reach_all[:, :], reach[:, :], UNITS, RMAX).then_inc(reach_max_ready, 1)
            pool.wait_ge(loads["edge_in"], 16 * (1 + PAD_DMAS))
            with pool.Fori(0, TURNS) as i:
                for a in range(PAIRS):
                    pool.wait_ge(ea_transposed[a], i + 1)
                    pool.dma_start(ea_slot[a][:, :, :], edge_in.rearrange("(u p j) r -> u p (j r)", p=P, j=J)
                                 [bass.ds(i * (2 * PAIRS) + 2 * a, 2), :, :].rearrange("u p k -> p u k"))\
                        .then_inc(ea_loaded[a], 16)
            pool.wait_ge(sender_stored, 16)
            pool.wait_ge(loads["edge_tables"], 16 * TABLE_DMAS)
            pool.wait_ge(span_ready, 1)
            pool.sem_inc(idx_ready, J)
            step = step_counter(pool, "pool_step")
            with pool.Fori(0, NT) as b:
                lo, hi = block_span(pool, b)
                with pool.Fori(lo, hi) as u:
                    s = next_step(pool, step)
                    for j in range(J):
                        pool.wait_ge(products_done, s * J + j + 1)
                        nc.gpsimd.tensor_copy(idx_slot[j][:, :], src_int[:, bass.ds(u, 1), j]).then_inc(idx_ready, 1)
                        pool.wait_ge(idx_ready, s * J + j + 1)
                        pool.sem_inc(gathers_started, 1)
                        nc.gpsimd.indirect_dma_start(
                            out=sent[j][:, :], out_offset=None, in_=sender_table,
                            in_offset=bass.IndirectOffsetOnAxis(ap=idx_slot[j][:, 0:1], axis=0),
                            bounds_check=NP - 1, oob_is_err=False).then_inc(gathered[j], 16)

            nc.gpsimd.memset(bias_rows, 0.0).then_inc(padding_ready, 1)
            nc.gpsimd.memset(part_weights, 0.0)
            nc.gpsimd.memset(before_me, 0.0).then_inc(ident_zeroed, 1)
            pool.wait_ge(ident_zeroed, 2)
            for i, parts in enumerate(partitions(SE, SE)):
                for j, part in enumerate(parts):
                    nc.gpsimd.memset(part_weights[:, j, i:i + 1], part / SE)
            nc.gpsimd.affine_select(out=before_me, in_=before_me, compare_op=ALU.is_ge, fill=1.0, base=0,
                                    pattern=[[-1, P]], channel_multiplier=1).then_inc(consts_ready, 1)
            pool.wait_ge(slots_ready, 1)
            pool.wait_ge(ln_ready[2], NT)
            pool.wait_ge(tokens_zeroed, 32)
            for t in range(NT):
                for k in range(TOP):
                    r = rows(t)
                    nc.gpsimd.indirect_dma_start(
                        out=tokens_sorted, out_offset=bass.IndirectOffsetOnAxis(ap=slot_int[0:r, k, t:t + 1], axis=0),
                        in_=hx_rows[0:r, t, :], in_offset=None,
                        bounds_check=(TILES + 2) * P - 1, oob_is_err=False).then_inc(rows_scattered, 16)
            pool.wait_ge(rows_scattered, 16 * TOP * NT)
            pool.dma_start(tile_rows, tokens_sorted[0:P, :]).then_inc(tile_loaded, 16)
            pool.wait_ge(tile_transposed, 1)
            pool.dma_start(tile_rows, tokens_sorted[P:2 * P, :]).then_inc(tile_loaded, 16)
            pool.wait_ge(mixed_zeroed, 32)
            count = pool.value_load(first_tile_int[0:1, EX:EX + 1], min_val=EX, max_val=TILES)
            last = pool.value_load(first_tile_int[0:1, EX - 1:EX], min_val=EX - 1, max_val=TILES - 1)

            def tiles(start, end):
                with pool.Fori(start, end) as t:
                    pool.wait_ge(tile_transposed, t + 2)
                    pool.sem_inc(gathers_started, 1)
                    pool.dma_start(tile_rows, tokens_sorted[bass.ds(t * P + 2 * P, P), :]).then_inc(tile_loaded, 16)
                    pool.wait_ge(tile_out_ready, t + 2)
                    pool.sem_inc(gathers_started, 1)
                    pool.dma_start(mixed_sorted[bass.ds(t * P, P), :], tile_out).then_inc(tile_stored, 16)
                    pool.wait_ge(tile_stored, t * 16 + 16)
                    pool.sem_inc(tile_out_free, 1)

            def results(k):
                for t in range(NT):
                    r = rows(t)
                    nc.gpsimd.indirect_dma_start(
                        out=(second_rows if k else first_rows)[t][0:r, :], out_offset=None, in_=mixed_sorted,
                        in_offset=bass.IndirectOffsetOnAxis(ap=slot_int[0:r, k, t:t + 1], axis=0),
                        bounds_check=TILES * P - 1, oob_is_err=False).then_inc(second_loaded[t // 2] if k else first_loaded, 16)

            tiles(0, last)
            results(0)
            tiles(last, count)
            results(1)

        @block.scalar
        def _(act):
            def deviations(n, dst=rstd):
                act.wait_ge(stats_ready, n + 1)
                nc.scalar.activation(dst[:, :], meanvar[:, :, 1], ACT.Sqrt).then_inc(std_ready, 1)

            deviations(0)
            for w in ("Wk", "Wv", "Wl"):
                for c in range(C):
                    full, free = filled(act, ("wT", w, c))
                    nc.scalar.activation(w_T[w][:, c, :], full, ACT.Copy).then_inc(free, 1)
            for t in range(NT):
                full, free = filled(act, ("xT", t))
                nc.scalar.activation(xn_T[:, :, tile_cols[t]], full.rearrange("p (c n) -> p c n", c=C), ACT.Copy)\
                    .then_inc(free, 1)
            for t in range(NT):
                full, free = filled(act, ("sender", t))
                nc.scalar.activation(sender_rows[:, t, :], full, ACT.Copy, scale=MUL ** -0.5).then_inc(free, 1)
            full, free = filled(act, ("kvT",))
            act.wait_ge(consts_ready, 2)
            full = full.rearrange("p (c n) -> p c n", c=C)
            nc.scalar.activation(kv_T[0:HD, :, 0:HD], full[0:HD, :, 0:HD], ACT.Copy, scale=N ** -0.5)
            nc.scalar.activation(kv_T[HD:P, :, HD:P], full[HD:P, :, HD:P], ACT.Copy, scale=N ** -0.5).then_inc(free, 1)
            for c in range(C):
                full, free = filled(act, ("m2", c))
                nc.scalar.activation(m2[:, c, :], full, ACT.Copy).then_inc(free, 1)
            for c in range(C):
                full, free = filled(act, ("m3", c))
                nc.scalar.activation(m3[:, c, :], full, ACT.Copy).then_inc(free, 1)
            for a in range(PAIRS):
                act.sem_inc(silu_done[a], 3)
            with act.Fori(0, TURNS) as i:
                for layer in range(3):
                    for a in range(PAIRS):
                        act.wait_ge(layer_done[a], i * 3 + layer + 4)
                        dst = h_slot[a][:, :]
                        src = psum[:, 2 * a + 1, :]
                        if layer == 2:
                            act.wait_ge(h3_split[a], i + 1)
                            dst = h3_out[a][:, :, :, :].rearrange("p u q n -> p q u n")
                            src = src.rearrange("p (q u n) -> p q u n", q=2, u=2)
                        scale = R ** -0.5 if layer == 0 else SILU_2MOM * HID ** -0.5
                        nc.scalar.activation(dst, src, ACT.Silu, scale=scale).then_inc(silu_done[a], 1)
            for a in range(PAIRS):
                act.wait_ge(h3_out_free[a], 1 + TURNS)
            act.wait_ge(span_ready, 1)
            act.sem_inc(adj_flushed, 1)
            act.sem_inc(hot_y_ready, J)
            act.sem_inc(scaled_ready, J)
            step = step_counter(act, "act_step")
            with act.Fori(0, NT) as b:
                lo, hi = block_span(act, b)
                with act.Fori(lo, hi) as u:
                    s = next_step(act, step)
                    act.wait_ge(edge_slot_ready, s)
                    for j in range(J):
                        k = j % 2
                        y = [edge_slot[:, J + Y * j + y:J + Y * j + y + 1] for y in range(Y)]
                        act.wait_ge(gathered[j], s * 16)
                        act.wait_ge(products_done, s * J + J + j - 1)
                        for m in range(3):
                            last = nc.scalar.activation(scaled[:, k, m, :], sent[j][:, MUL + m * MUL:2 * MUL + m * MUL], ACT.Copy, scale=y[1 + m])
                        last.then_inc(scaled_ready, 1)
                        act.wait_ge(hot_ready, s * J + j + 1)
                        act.wait_ge(scatter_done, s * J + J + j - 1)
                        for i in range(Y):
                            last = nc.scalar.activation(hot_y[:, k, i, :], hot_f[:, k, :], ACT.Copy, scale=y[i])
                        last.then_inc(hot_y_ready, 1)
                act.wait_ge(scatter_done, s * J + 2 * J)
                nc.scalar.activation(adj_rows[:, bass.ds(b, 1), :].rearrange("p b n -> p (b n)"),
                                     adj_psum[:, 0:NP], ACT.Copy).then_inc(adj_flushed, 1)
            act.wait_ge(stats_ready, 2)
            nc.scalar.activation(dinv[:, :], degree, ACT.Sqrt).then_inc(std_ready, 1)
            roots = [2]

            def root(t, n=1):
                roots[0] += 1
                act.wait_ge(stats_ready, roots[0])
                nc.scalar.activation(ln_root[:, t, 0:n], ln_pair[:, t, 0:n], ACT.Sqrt).then_inc(std_ready, 1)

            alpha = SILU_2MOM * HID ** -0.5 * (2 * MUL) ** -0.5 / AVG_NUM_NEIGHBORS

            def messages(t):
                if t >= 2:
                    filled(act, ("conv", t - 2))
                full, free = filled(act, ("msgT0", t))
                nc.scalar.activation(msg_T[:, t % 2, 0:D], full, ACT.Copy, scale=alpha).then_inc(free, 1)
                full, free = filled(act, ("msgT1", t))
                nc.scalar.activation(msg_T[:, t % 2, D:2 * D - P], full[:, 0:D - P], ACT.Copy, scale=alpha)
                nc.scalar.activation(msg_T[:, t % 2, 2 * D - P:], full[:, D - P:], ACT.Copy, scale=alpha * 3 ** -0.5)\
                    .then_inc(free, 1)

            def expert_inputs(t):
                full, free = filled(act, ("hT", t))
                nc.scalar.activation(xn_T[:, :, tile_cols[t]], full.rearrange("p (c n) -> p c n", c=C), ACT.Copy)\
                    .then_inc(free, 1)

            full, free = filled(act, ("routersT",))
            nc.scalar.activation(routers_T[:, :, :], full[:, 0:C * (EX + PARTS + 2)].rearrange("p (c e) -> p c e", c=C), ACT.Copy)\
                .then_inc(free, 1)
            full, free = filled(act, ("expert_biasT",))
            nc.scalar.activation(expert_bias_T[:, :], full[:, 0:P], ACT.Copy).then_inc(free, 1)
            messages(0)
            for t in range(NT):
                if t + 1 < NT:
                    messages(t + 1)
                root(t, 2)
                if t >= 2:
                    expert_inputs(t - 2)
            for t in range(NT - 2, NT):
                expert_inputs(t)

            def adjacency(s0, s1):
                for s in range(s0, s1):
                    for g, (g0, w) in enumerate(GROUPS):
                        full, free = filled(act, ("adjT", s, g))
                        nc.scalar.activation(adj_T[:, s, g0:g0 + w], full[:, 0:w], ACT.Copy).then_inc(free, 1)

            adjacency(0, ADJ_FIRST)
            act.wait_ge(gap_ready, 1)
            nc.scalar.activation(gap[:, :], gap[:, :], ACT.Exp).then_inc(gap_exp, 1)
            adjacency(ADJ_FIRST, NT)
            for g, (g0, w) in enumerate(GROUPS):
                full, free = filled(act, ("gateT", g))
                nc.scalar.activation(gates_T[:, g0:g0 + w], full[0:EX, 0:w], ACT.Copy).then_inc(free, 1)
            full, free = filled(act, ("biasT",))
            nc.scalar.activation(bias_T[:, :], full[:, 0:HC + SC], ACT.Copy).then_inc(free, 1)
            act.wait_ge(tiles_ready, 1)
            act.sem_inc(gelu_done, UP_BANKS)
            with act.Fori(0, EX // 2) as i:
                bounds = expert_bounds(act, i)
                for a in range(2):
                    lo, hi = bounds[a:a + 2]
                    with act.Fori(lo, hi) as t:
                        for f in range(FC):
                            act.wait_ge(up_done, t * FC + f + 1)
                            nc.scalar.activation(hid[:, f, :], psum[:, f % UP_BANKS, 0:P], ACT.Gelu,
                                                 bias=expert_bias_T[:, bass.ds(i * (2 * FC) + a * FC + f, 1)]).then_inc(gelu_done, 1)
            act.wait_ge(dinv_ready, 1)
            for t in range(NT + 1):
                if t < NT:
                    root(t)
                if t:
                    act.wait_ge(ln_ready[3], t)
                    nc.scalar.activation(z_rows[:, t - 1, :], xn2_rows[:, t - 1, :], ACT.Copy, scale=dinv[:, t - 1:t]).then_inc(z_ready, 1)

            def transposed(key, dst, t, n=None):
                full, free = filled(act, (key, t))
                n = P if n is None else n
                nc.scalar.activation(dst[:, :, t * P:t * P + n], full.rearrange("p (c n) -> p c n", c=C)[:, :, 0:n], ACT.Copy)\
                    .then_inc(free, 1)

            def sums(t):
                if t >= 2:
                    filled(act, ("ahT", t - 2))
                full, free = filled(act, ("agg1", t))
                nc.scalar.activation(ah_rows[:, t % 2, :], full, ACT.Copy, scale=dinv[:, t:t + 1]).then_inc(free, 1)

            sums(0)
            sums(1)
            for key in agg_order():
                if key[0] == "ahT":
                    transposed("ahT", ah_T, key[1])
                    if key[1] + 2 < NT:
                        sums(key[1] + 2)
                elif key[0] == "xn2T":
                    transposed("xn2T", xn_T, key[1])
            for f in range(HC):
                for g, (g0, w) in enumerate(GROUPS):
                    full, free = filled(act, ("h1T", f, g))
                    nc.scalar.activation(h1_T[:, f, g0:g0 + w], full[:, 0:w], ACT.Relu, bias=bias_T[:, f:f + 1]).then_inc(free, 1)
            for t in range(NT):
                full, free = filled(act, ("y2", t))
                nc.scalar.activation(z2_rows[:, t, :], full, ACT.Copy, scale=dinv[:, t:t + 1]).then_inc(free, 1)
            for m in range(C):
                act.wait_ge(k_max_ready, m + 1)
                for g, (g0, w) in enumerate(GROUPS):
                    full, free = filled(act, ("kT", m, g))
                    n = KEY_COLS[g]
                    nc.scalar.activation(ek_T[:, m, g0:g0 + n], full[:, 0:n], ACT.Exp, bias=k_max[:, m:m + 1]).then_inc(free, 1)
            for t in range(NT):
                drained(act, ("q", t))
                nc.scalar.activation(q_rows[:, t, :], q_rows[:, t, :], ACT.Exp).then_inc(q_exp, 1)
            for t in range(NT):
                full, free = filled(act, ("v", t))
                nc.scalar.activation(vx_rows[:, t, :], full, ACT.Copy).then_inc(free, 1)
            for t in range(NT):
                full, free = filled(act, ("ek", t))
                r = rows(t)
                nc.scalar.activation(ek_rows[0:r, t, :], full[0:r, :], ACT.Copy).then_inc(free, 1)
            full, free = filled(act, ("ctxT",))
            full = full.rearrange("p (c n) -> p c n", c=C)
            nc.scalar.activation(kv_T[0:HD, :, 0:HD], full[0:HD, :, 0:HD], ACT.Copy)
            nc.scalar.activation(kv_T[HD:P, :, HD:P], full[HD:P, :, HD:P], ACT.Copy).then_inc(free, 1)
            act.wait_ge(k_scale_ready, 1)
            for c in range(C):
                full, free = filled(act, ("m5", c))
                nc.scalar.activation(m5[:, c, :], full, ACT.Copy, scale=k_scale[:, c:c + 1]).then_inc(free, 1)
            for t in range(NT):
                transposed("qT", q_T, t)
            LAG = 4
            for t in range(NT + 1):
                if t < NT:
                    root(t)
                if t:
                    root(t - 1)
                if t >= LAG:
                    transposed("lastT", xn_T, t - LAG)
            for t in range(NT + 1 - LAG, NT):
                transposed("lastT", xn_T, t)
            for key in ffn_order():
                if key == ("route",):
                    drained(act, key)
                    nc.scalar.activation(route[:, :], route[:, :], ACT.Exp).then_inc(route_exp, 1)
                if key[0] == "up":
                    _, g, j = key
                    n, r = len(TURN_TILES[g]) * P, hidden_rows(j)
                    if g >= 2:
                        filled(act, ("down", TURN_TILES[g - 2][-1]))
                    full, free = filled(act, key)
                    nc.scalar.activation(shid[g % 2][0:r, j, 0:n], full[0:r, 0:n], ACT.Gelu,
                                         bias=bias_T[0:r, HC + j:HC + j + 1]).then_inc(free, 1)

        @block.vector
        def _(dve):
            steps = [0]

            def settle(ins):
                steps[0] += 1
                ins.then_inc(dve_step, 1)
                dve.wait_ge(dve_step, steps[0])

            def layer_norm(src, dst, n):
                for t in range(NT):
                    if t == 0:
                        dve.wait_ge(loads["x"], 16)
                    if t == NT // 2:
                        dve.wait_ge(loads["x_rest"], 32)
                    last = nc.vector.bn_stats(stats[:, t, :], src[:, t, :])
                settle(last)
                for t in range(NT):
                    last = nc.vector.bn_aggr(meanvar[:, t, :], stats[:, t, :])
                settle(last)
                nc.vector.tensor_scalar(meanvar[:, :, 1], meanvar[:, :, 1], LN_EPS, None, ALU.add).then_inc(stats_ready, 1)
                dve.wait_ge(std_ready, n + 1)
                settle(nc.vector.reciprocal(rstd[:, :], rstd[:, :]))
                for t in range(NT):
                    nc.vector.tensor_scalar(dst[:, t, :], src[:, t, :], meanvar[:, t, 0:1], rstd[:, t:t + 1],
                                            ALU.subtract, ALU.mult).then_inc(ln_ready[n], 1)

            layer_norm(x_rows, ln_rows, 0)
            dve.wait_ge(loads["dst_units"], 32)
            dve.wait_ge(consts_ready, 1)
            settle(nc.vector.tensor_copy(dst_unitf[:, :], dst_units[:, :]))
            nc.vector.tensor_reduce(unit_max[:, :], dst_unitf[:, :], AX_X, ALU.max)
            settle(nc.vector.tensor_reduce(unit_min[:, :], dst_unitf[:, :], AX_X, ALU.min))
            lo_u = block_lo[0:UNITS, :]
            nc.vector.tensor_scalar(touch[:, 0, :], lo_u, unit_max[:, :], None, ALU.is_le)
            nc.vector.tensor_scalar(touch[:, 1, :], lo_u, float(P - 1), unit_min[:, :], ALU.add, ALU.is_ge)
            nc.vector.tensor_scalar(touch[:, 3, 0:1], unit_id[0:UNITS, :], -1.0, float(UNITS), ALU.mult, ALU.add)
            settle(nc.vector.tensor_scalar(touch[:, 3, 1:2], unit_id[0:UNITS, :], 1.0, None, ALU.add))
            settle(nc.vector.tensor_tensor(touch[:, 2, :], touch[:, 0, :], touch[:, 1, :], ALU.mult))
            nc.vector.tensor_scalar(reach[:, 0:NT], touch[:, 2, :], touch[:, 3, 0:1], None, ALU.mult)
            nc.vector.tensor_scalar(reach[:, NT:], touch[:, 2, :], touch[:, 3, 1:2], None, ALU.mult).then_inc(reach_ready, 1)
            dve.wait_ge(reach_max_ready, 1)
            settle(nc.vector.tensor_scalar(span_f[:, 0, :], reach_all[0:1, 0:NT], -1.0, float(UNITS), ALU.mult, ALU.add))
            settle(nc.vector.tensor_scalar(span_f[:, 0, :], span_f[:, 0, :], float(UNITS - 1), None, ALU.min))
            settle(nc.vector.tensor_scalar(span_f[:, 1, :], span_f[:, 0, :], 1.0, None, ALU.add))
            settle(nc.vector.tensor_tensor(span_f[:, 1, :], span_f[:, 1, :], reach_all[0:1, NT:], ALU.max))
            nc.vector.tensor_copy(span[:, :, :], span_f[:, :, :]).then_inc(span_ready, 1)
            dve.wait_ge(loads["edge_tables"], 16 * TABLE_DMAS)
            nc.vector.tensor_copy(edges[:, :, 0:J], dst_int[:, :, :])
            settle(nc.vector.tensor_copy(edges[:, :, J + J * Y:], src_int[:, :, :]))
            dve.wait_ge(loads["bk"], 16)
            dve.wait_ge(loads["bv"], 16)
            for t in range(NT):
                for w, b, dst in (("Wk", "bk", k_rows), ("Wv", "bv", v_rows)):
                    full, free = filled(dve, (w, t))
                    nc.vector.tensor_tensor(dst[:, t, :], full, b_row[b][:, :], ALU.add).then_inc(free, 1)
            dve.wait_ge(loads["bl"], 16)
            full, free = filled(dve, ("mix_bias",))
            nc.vector.tensor_tensor(mix_bias[:, :], full, b_row["bl"][:, :], ALU.add).then_inc(free, 1)
            drained(dve, ("mix_bias",))
            for t in range(NT):
                settle(nc.vector.tensor_tensor(x_rows[:, t, :], x_rows[:, t, :], mix_bias[:, :], ALU.add))
                full, free = filled(dve, ("mix", t))
                nc.vector.tensor_tensor(x_rows[:, t, :], full, x_rows[:, t, :], ALU.add).then_inc(free, 1)
            dve.wait_ge(loads["mlp"], 16 * (J + 6))
            settle(nc.vector.tensor_copy(w4_hi[:, :], w_mlp4[:, :]))
            nc.vector.tensor_tensor(w4_lo[:, :], w_mlp4[:, :], w4_hi[:, :].bitcast(F32), ALU.subtract).then_inc(w4_ready, 1)
            def edge_inputs(a, turn, layers):
                dve.wait_ge(ea_transposed[a], turn + 2)
                dve.wait_ge(layer_done[a], layers)
                nc.vector.tensor_copy(ea_T[a][:, :], psum[0:J * R, 2 * a, 0:2 * P]).then_inc(ea_T_ready[a], 1)

            def split_hidden(a, turn, layers):
                dve.wait_ge(silu_done[a], layers)
                dve.wait_ge(h3_out_free[a], turn + 1)
                settle_turn(nc.vector.tensor_copy(h3_hi[a][:, :, :, :], h3_out[a][:, :, :, :]), a, turn)
                nc.vector.tensor_tensor(h3_lo[a][:, :, :, :], h3_out[a][:, :, :, :], h3_hi[a][:, :, :, :].bitcast(F32),
                                        ALU.subtract).then_inc(h3_split[a], 1)

            def settle_turn(ins, a, turn):
                ins.then_inc(hi_ready[a], 1)
                dve.wait_ge(hi_ready[a], turn + 1)

            for a in range(PAIRS):
                dve.sem_inc(h3_split[a], 1)
                edge_inputs(a, 0, 1)
            with dve.Fori(0, TURNS - 1) as i:
                for a in range(PAIRS):
                    edge_inputs(a, i + 1, i * 3 + 4)
                for a in range(PAIRS):
                    split_hidden(a, i, i * 3 + 6)
            for a in range(PAIRS):
                split_hidden(a, TURNS - 1, (TURNS - 1) * 3 + 6)
            dve.sem_inc(products_done, 2 * J)
            for a in range(PAIRS):
                dve.wait_ge(h3_out_free[a], 1 + TURNS)
            nc.vector.memset(hot_src[:, :, N:NP - 1], 0.0)
            settle(nc.vector.memset(hot_src[:, :, NP - 1:NP], 1.0))
            dve.sem_inc(hot_ready, J)
            dve.sem_inc(dot_ready, J)
            dve.sem_inc(msg_flushed, 1)
            step = step_counter(dve, "dve_step_no")
            with dve.Fori(0, NT) as b:
                lo, hi = block_span(dve, b)
                with dve.Fori(lo, hi) as u:
                    s = next_step(dve, step)
                    dve.wait_ge(hot_y_ready, s * J)
                    dve.wait_ge(products_done, s * J + J)
                    nc.vector.tensor_copy(edge_slot[:, :], edges[:, bass.ds(u, 1), :].rearrange("p u k -> p (u k)"))\
                        .then_inc(edge_slot_ready, 1)
                    dve.wait_ge(edge_slot_ready, s)
                    nodes = iota_nodes[:, bass.ds(b * P, P)]
                    for j in range(J):
                        k = j % 2
                        dst = edge_slot[:, j:j + 1]
                        dve.wait_ge(scatter_done, s * J + J + j - 1)
                        nc.vector.tensor_scalar(hot_f[:, k, :], nodes, dst, None, ALU.is_equal).then_inc(hot_ready, 1)
                        nc.vector.tensor_scalar(hot_dst[:, k, :], nodes, dst, None, ALU.is_equal)
                        src = edge_slot[:, J + J * Y + j:J + J * Y + j + 1]
                        nc.vector.tensor_scalar(hot_src[:, k, 0:N], iota_nodes[:, 0:N], src, None, ALU.is_equal)
                        dve.wait_ge(scaled_ready, s * J + j + 1)
                        nc.vector.tensor_reduce(dot[:, k, :], scaled[:, k, :, :].rearrange("p m u -> p u m"), AX_X, ALU.add)\
                            .then_inc(dot_ready, 1)
                        dve.wait_ge(weights_done, s * J + J + j + 1)
                        w = tile_w[k].rearrange("p (q u) -> p q u", q=4)
                        o = prod[:, k, :].rearrange("p (c u) -> p c u", u=MUL)
                        s0 = sent[j][:, 0:MUL].rearrange("p (a u) -> p a u", a=1)
                        s1 = sent[j][:, MUL:].rearrange("p (m u) -> p m u", u=MUL)
                        nc.vector.tensor_tensor(o[:, 0:5:4, :], w[:, 0:2, :], s0.to_broadcast([P, 2, MUL]), ALU.mult)
                        nc.vector.tensor_tensor(o[:, 1:4, :], s1, w[:, 2:3, :].to_broadcast([P, 3, MUL]), ALU.mult)
                        dve.wait_ge(dot_ready, s * J + j + 1)
                        nc.vector.tensor_tensor(o[:, 5, :], w[:, 3, :], dot[:, k, :], ALU.mult).then_inc(products_done, 1)
                dve.wait_ge(scatter_done, s * J + 2 * J)
                nc.vector.tensor_copy(msg_rows[:, bass.ds(b, 1), :].rearrange("p b n -> p (b n)"), msg_psum[:, :])\
                    .then_inc(msg_flushed, 1)
            dve.wait_ge(adj_flushed, NT + 1)
            nc.vector.tensor_scalar(degree, adj_rows[:, :, NP - 1], 1.0, None, ALU.add).then_inc(stats_ready, 1)
            nc.vector.memset(members_before[:, 0, :], 0.0)
            settle(nc.vector.memset(first_tile[:, 0:1], 0.0))
            drained(dve, ("routersT",))
            ln_g, ln_b = routers_T[:, :, EX + PARTS:EX + PARTS + 1], routers_T[:, :, EX + PARTS + 1:EX + PARTS + 2]
            nc.vector.tensor_tensor(routers_scaled[:, :, :], routers_T[:, :, 0:EX], ln_g.to_broadcast([P, C, EX]), ALU.mult)\
                .then_inc(routers_ready, 1)
            roots = [2]

            def moments(row, t, twice=False):
                settle(nc.vector.bn_stats(stats[:, t, :], row))
                settle(nc.vector.bn_aggr(meanvar[:, t, :], stats[:, t, :]))
                last = nc.vector.tensor_scalar(ln_pair[:, t, 0:1], meanvar[:, t, 1:2], LN_EPS, None, ALU.add)
                if twice:
                    settle(last)
                    last = nc.vector.scalar_tensor_tensor(ln_pair[:, t, 1:2], ln_pair[:, t, 0:1], LN_EPS, meanvar[:, t, 1:2],
                                                          ALU.mult, ALU.add)
                last.then_inc(stats_ready, 1)
                roots[0] += 1
                return roots[0]

            def inverse_roots(t, number, n=1):
                dve.wait_ge(std_ready, number)
                settle(nc.vector.reciprocal(ln_root[:, t, 0:n], ln_root[:, t, 0:n]))

            dve.wait_ge(loads["router_bias"], 16)
            full, free = filled(dve, ("router_bias",))
            nc.vector.tensor_tensor(router_bias[:, :], full[:, 0:EX], router_bias[:, :], ALU.add).then_inc(free, 1)
            drained(dve, ("router_bias",))

            def add_router_bias(t):
                full, free = filled(dve, ("logits", t))
                nc.vector.tensor_tensor(logits[:, t, :], full[:, 0:EX], router_bias[:, :], ALU.add).then_inc(free, 1)

            numbers = {}
            for t in range(NT + 1):
                if t >= 4:
                    add_router_bias(t - 4)
                if t < NT:
                    full, free = filled(dve, ("conv", t))
                    nc.vector.tensor_tensor(x_rows[:, t, 0:MUL], full[:, 0:MUL], x_rows[:, t, 0:MUL], ALU.add)
                    v = x_rows[:, t, MUL:].rearrange("p (u m) -> p m u", m=3)
                    nc.vector.tensor_tensor(v, full[:, MUL:].rearrange("p (m u) -> p m u", m=3), v, ALU.add).then_inc(free, 1)
                    drained(dve, ("conv", t))
                    numbers[t] = moments(x_rows[:, t, :], t, True)
                if t:
                    inverse_roots(t - 1, numbers[t - 1], 2)
                    nc.vector.tensor_scalar(hx_rows[:, t - 1, :], x_rows[:, t - 1, :], meanvar[:, t - 1, 0:1], ln_root[:, t - 1, 1:2],
                                            ALU.subtract, ALU.mult).then_inc(ln_ready[2], 1)
            for t in range(NT - 3, NT):
                add_router_bias(t)
            for t in range(NT):
                drained(dve, ("logits", t))
                last = nc.vector.max(top_val[:, t, :], logits[:, t, :])
            settle(last)
            nc.vector.tensor_tensor(gap[:, :], top_val[:, :, 1], top_val[:, :, 0], ALU.subtract).then_inc(gap_ready, 1)
            for t in range(NT):
                last = nc.vector.max_index(top_idx[:, t, :], top_val[:, t, :], logits[:, t, :])
            settle(last)
            settle(nc.vector.tensor_copy(choice_f[:, :, :], top_idx[:, :, 0:TOP].rearrange("p t k -> p k t")))
            ids = iota_nodes[:, 0:EX].unsqueeze(1).to_broadcast([P, NT, EX])
            for k in range(TOP):
                last = nc.vector.tensor_tensor(chosen[:, k, :, :], ids, choice_f[:, k, :].unsqueeze(2).to_broadcast([P, NT, EX]),
                                               ALU.is_equal)
            settle(last)
            settle(nc.vector.tensor_tensor(member[:, :, :], chosen[:, 0, :, :], chosen[:, 1, :, :], ALU.add))
            settle(nc.vector.tensor_scalar(member[:, NT - 1, :], member[:, NT - 1, :], real_row[:, :], None, ALU.mult))
            for t in range(NT):
                last = nc.vector.tensor_tensor(members_before[:, t + 1, :], members_before[:, t, :], member[:, t, :], ALU.add)
                if t + 1 < NT:
                    settle(last)
            last.then_inc(members_ready, 1)
            full, free = filled(dve, ("rank",))
            counts = full[:, NT * EX:(NT + 1) * EX]
            settle(nc.vector.tensor_tensor(tile_tests[:, :, :], counts.unsqueeze(2).to_broadcast([P, EX, NT]),
                                           block_lo[:, :].unsqueeze(1).to_broadcast([P, EX, NT]), ALU.is_gt))
            settle(nc.vector.tensor_reduce(expert_tiles[:, :], tile_tests[:, :, :], AX_X, ALU.add))
            settle(nc.vector.tensor_scalar(expert_tiles[:, :], expert_tiles[:, :], 1.0, None, ALU.max))
            for e in range(EX):
                settle(nc.vector.tensor_tensor(first_tile[:, e + 1:e + 2], first_tile[:, e:e + 1], expert_tiles[:, e:e + 1], ALU.add))
            nc.vector.tensor_copy(first_tile_int[:, :], first_tile[0:1, :]).then_inc(tiles_ready, 1)
            settle(nc.vector.tensor_scalar(place_base[:, :], first_tile[:, 0:EX], float(P), None, ALU.mult))
            nc.vector.tensor_tensor(place[:, :, :], full[:, 0:NT * EX].rearrange("p (t e) -> p t e", e=EX),
                                    place_base[:, :].unsqueeze(1).to_broadcast([P, NT, EX]), ALU.add).then_inc(free, 1)
            drained(dve, ("rank",))
            for k in range(TOP):
                settle(nc.vector.tensor_tensor(member[:, :, :], chosen[:, k, :, :], place[:, :, :], ALU.mult))
                settle(nc.vector.tensor_reduce(slot_f[:, k, :], member[:, :, :], AX_X, ALU.add))
            nc.vector.tensor_tensor(slot_sorted[:, 0, :], slot_f[:, 0, :], slot_f[:, 1, :], ALU.min)
            settle(nc.vector.tensor_tensor(slot_sorted[:, 1, :], slot_f[:, 0, :], slot_f[:, 1, :], ALU.max))
            nc.vector.tensor_copy(slot_int[:, :, :], slot_sorted[:, :, :]).then_inc(slots_ready, 1)
            dve.wait_ge(gap_exp, 1)
            settle(nc.vector.tensor_scalar(gate[:, 0, :], gap[:, :], 1.0, None, ALU.add))
            settle(nc.vector.reciprocal(gate[:, 0, :], gate[:, 0, :]))
            settle(nc.vector.tensor_tensor(gate[:, 1, :], gap[:, :], gate[:, 0, :], ALU.mult))
            settle(nc.vector.tensor_tensor(slot_order[:, :], slot_f[:, 0, :], slot_f[:, 1, :], ALU.is_lt))
            for k in range(TOP):
                settle(nc.vector.tensor_tensor(gate_by_slot[:, k, :], gate[:, k, :], slot_order[:, :], ALU.mult))
                settle(nc.vector.tensor_tensor(slot_sorted[:, 0, :], gate[:, 1 - k, :], slot_order[:, :], ALU.mult))
                settle(nc.vector.tensor_tensor(slot_sorted[:, 0, :], gate[:, 1 - k, :], slot_sorted[:, 0, :], ALU.subtract))
                settle(nc.vector.tensor_tensor(gate_by_slot[:, k, :], gate_by_slot[:, k, :], slot_sorted[:, 0, :], ALU.add))
            for k in range(TOP):
                settle(nc.vector.tensor_tensor(chosen[:, k, :, :], chosen[:, k, :, :],
                                               gate[:, k, :].unsqueeze(2).to_broadcast([P, NT, EX]), ALU.mult))
            nc.vector.tensor_tensor(token_gates[:, :, :], chosen[:, 0, :, :], chosen[:, 1, :, :], ALU.add).then_inc(gates_ready, 1)
            nc.vector.tensor_scalar(x_scale[:, :], ln_root[:, :, 0], 1.0, None, ALU.add)
            settle(nc.vector.tensor_tensor(x_shift[:, :], ln_root[:, :, 0], meanvar[:, :, 0], ALU.mult))
            for t in range(NT):
                last = nc.vector.tensor_scalar(x_rows[:, t, :], x_rows[:, t, :], x_scale[:, t:t + 1], x_shift[:, t:t + 1],
                                               ALU.mult, ALU.subtract)
            settle(last)
            for t in range(NT):
                full, free = filled(dve, ("b2", t))
                nc.vector.tensor_tensor(x_rows[:, t, :], full, x_rows[:, t, :], ALU.add).then_inc(free, 1)
            dve.wait_ge(std_ready, 2)
            nc.vector.reciprocal(dinv[:, :], dinv[:, :]).then_inc(dinv_ready, 1)
            def tile_transposed_out(n):
                dve.wait_ge(tile_transposed, n)
                for c in range(C):
                    last = nc.vector.tensor_scalar(tile_T[:, c, :], psum[:, T_BANK, c * P:c * P + P], ln_g[:, c, :], ln_b[:, c, :],
                                                   ALU.mult, ALU.add)
                last.then_inc(tile_T_ready, 1)

            def tiles(start, end):
                with dve.Fori(start, end) as t:
                    tile_transposed_out(t + 2)
                    dve.wait_ge(down_done, t + 2)
                    dve.wait_ge(tile_out_free, t + 1)
                    nc.vector.tensor_copy(tile_out, psum[:, Y_BANK, :]).then_inc(tile_out_ready, 1)

            def add_results(t, k):
                r = rows(t)
                if k:
                    dve.wait_ge(second_loaded[t // 2], 32)
                else:
                    dve.wait_ge(first_loaded, 16 * NT)
                settle(nc.vector.scalar_tensor_tensor(x_rows[0:r, t, :], (second_rows if k else first_rows)[t][0:r, :], gate_by_slot[0:r, k, t:t + 1],
                                                      x_rows[0:r, t, :], ALU.mult, ALU.add))

            dve.sem_inc(tile_out_ready, 1)
            tile_transposed_out(1)
            last = dve.value_load(first_tile_int[0:1, EX - 1:EX], min_val=EX - 1, max_val=TILES - 1)
            count = dve.value_load(first_tile_int[0:1, EX:EX + 1], min_val=EX, max_val=TILES)
            dve.sem_inc(tile_out_free, 1)
            tiles(0, last)
            for t in range(NT):
                add_results(t, 0)
            tiles(last, count)
            for t in range(NT + 1):
                if t < NT:
                    add_results(t, 1)
                    numbers[t] = moments(x_rows[:, t, :], t)
                if t:
                    u = t - 1
                    inverse_roots(u, numbers[u])
                    nc.vector.tensor_scalar(xn2_rows[:, u, :], x_rows[:, u, :], meanvar[:, u, 0:1], ln_root[:, u, 0:1],
                                            ALU.subtract, ALU.mult).then_inc(ln_ready[3], 1)
            dve.wait_ge(loads["gnn_b2"], 16)
            for t in range(NT):
                full, free = filled(dve, ("agg2", t))
                nc.vector.scalar_tensor_tensor(conv_out[:, t % 2, :], full, dinv[:, t:t + 1], b_row["bl"][:, :], ALU.mult, ALU.add)\
                    .then_inc(free, 1)
                drained(dve, ("agg2", t))
                settle(nc.vector.scalar_tensor_tensor(x_rows[:, t, :], conv_out[:, t % 2, :], 0.0, x_rows[:, t, :], ALU.max, ALU.add))
            for m in range(C):
                for g, n in enumerate(KEY_COLS):
                    b, uses = ring.at[("kT", m, g)]
                    dve.wait_ge(bank_full[b], uses + 1)
                    last = nc.vector.tensor_reduce(k_max3[:, m, g:g + 1], psum[:, b, 0:n], AX_X, ALU.max)
                settle(last)
                settle(nc.vector.tensor_reduce(k_max[:, m:m + 1], k_max3[:, m, :], AX_X, ALU.max))
                nc.vector.tensor_scalar(k_max[:, m:m + 1], k_max[:, m:m + 1], -1.0, None, ALU.mult).then_inc(k_max_ready, 1)

            def heads(rows_ap):
                return rows_ap.rearrange("p (h d) -> p h d", h=HEADS)

            def queries(t):
                full, free = filled(dve, ("q", t))
                settle(nc.vector.tensor_reduce(q_max[:, :], heads(full), AX_X, ALU.max))
                nc.vector.tensor_tensor(heads(q_rows[:, t, :]), heads(full), q_max[:, :].unsqueeze(2).to_broadcast([P, HEADS, HD]),
                                        ALU.subtract).then_inc(free, 1)
                drained(dve, ("q", t))

            def normalised_queries(t):
                dve.wait_ge(q_exp, t + 1)
                settle(nc.vector.tensor_reduce(q_sum[:, t % 2, :], heads(q_rows[:, t, :]), AX_X, ALU.add))
                settle(nc.vector.reciprocal(q_sum[:, t % 2, :], q_sum[:, t % 2, :]))
                nc.vector.tensor_tensor(heads(q_rows[:, t, :]), heads(q_rows[:, t, :]),
                                        q_sum[:, t % 2, :].unsqueeze(2).to_broadcast([P, HEADS, HD]), ALU.mult).then_inc(q_ready, 1)

            queries(0)
            for t in range(1, NT):
                queries(t)
                normalised_queries(t - 1)
            normalised_queries(NT - 1)
            for m in range(C):
                for g in range(len(GROUPS)):
                    drained(dve, ("kT", m, g))
            settle(nc.vector.tensor_reduce(k_sum[:, :], ek_T[:, :, 0:N], AX_X, ALU.add))
            settle(nc.vector.tensor_scalar(k_sum[:, :], k_sum[:, :], float(N) * HD ** 0.5, None, ALU.mult))
            nc.vector.reciprocal(k_scale[:, :], k_sum[:, :]).then_inc(k_scale_ready, 1)
            dve.wait_ge(loads["b_out"], 16)
            dve.wait_ge(loads["ln_scale"], 16)
            last_numbers = {}
            for t in range(NT + 2):
                if t < NT:
                    full, free = filled(dve, ("att", t))
                    nc.vector.tensor_tensor(att_rows[:, t, :], full, b_row["bk"][:, :], ALU.add).then_inc(free, 1)
                    drained(dve, ("att", t))
                    numbers[t] = moments(att_rows[:, t, :], t)
                if 1 <= t <= NT:
                    u = t - 1
                    inverse_roots(u, numbers[u])
                    settle(nc.vector.scalar_tensor_tensor(att_rows[:, u, :], att_rows[:, u, :], meanvar[:, u, 0:1], b_row["bv"][:, :],
                                                          ALU.subtract, ALU.mult))
                    settle(nc.vector.scalar_tensor_tensor(x_rows[:, u, :], att_rows[:, u, :], ln_root[:, u, 0:1], x_rows[:, u, :],
                                                          ALU.mult, ALU.add))
                    last_numbers[u] = moments(x_rows[:, u, :], u)
                if t >= 2:
                    u = t - 2
                    inverse_roots(u, last_numbers[u])
                    nc.vector.tensor_scalar(last_rows[:, u, :], x_rows[:, u, :], meanvar[:, u, 0:1], ln_root[:, u, 0:1],
                                            ALU.subtract, ALU.mult).then_inc(ln_ready[5], 1)
            for t in range(NT):
                drained(dve, ("lastT", t))
            settle(nc.vector.tensor_reduce(mean_col[:, :], xn_T[:, :, 0:N], AX_X, ALU.add))
            nc.vector.tensor_scalar(mean_col[:, :], mean_col[:, :], 1.0 / N, None, ALU.mult).then_inc(mean_ready, 1)
            full, free = filled(dve, ("route",))
            settle(nc.vector.tensor_reduce(route_f[:, 0:1], full[0:1, 0:PARTS], AX_X, ALU.max))
            nc.vector.tensor_scalar(route[:, :], full[0:1, 0:PARTS], route_f[:, 0:1], None, ALU.subtract).then_inc(free, 1)
            drained(dve, ("route",))
            dve.wait_ge(route_exp, 1)
            settle(nc.vector.tensor_reduce(route_f[:, 1:2], route[:, :], AX_X, ALU.add))
            settle(nc.vector.reciprocal(route_f[:, 1:2], route_f[:, 1:2]))
            settle(nc.vector.tensor_scalar(route[:, :], route[:, :], route_f[:, 1:2], None, ALU.mult))
            settle(nc.vector.max(route_top[:, :], route[:, :]))
            settle(nc.vector.max_index(route_idx[:, :], route_top[:, :], route[:, :]))
            settle(nc.vector.tensor_copy(route_f[:, 2:4], route_idx[:, 0:2]))
            settle(nc.vector.tensor_reduce(route_f[:, 4:5], route_top[:, 0:2], AX_X, ALU.add))
            settle(nc.vector.reciprocal(route_f[:, 4:5], route_f[:, 4:5]))
            settle(nc.vector.tensor_scalar(route_f[:, 6:8], route_top[:, 0:2], route_f[:, 4:5], None, ALU.mult))
            for k in range(2):
                last = nc.vector.tensor_scalar(route_coef[:, k, :], iota_nodes[0:1, 0:PARTS], route_f[:, 2 + k:3 + k],
                                               route_f[:, 6 + k:7 + k], ALU.is_equal, ALU.mult)
            settle(last)
            settle(nc.vector.tensor_tensor(route_coef[:, 0, :], route_coef[:, 0, :], route_coef[:, 1, :], ALU.add))
            settle(nc.vector.tensor_tensor(part_prod[:, :, :], part_weights[:, :, :],
                                           route_coef[:, 0, :].unsqueeze(1).to_broadcast([1, SE, PARTS]), ALU.mult))
            settle(nc.vector.tensor_reduce(expert_w[:, 0, :], part_prod[:, :, :], AX_X, ALU.add))
            settle(nc.vector.tensor_scalar(expert_w[:, 1, :], expert_w[:, 0, :], 1e-6, None, ALU.is_gt))
            nc.vector.tensor_tensor(expert_w[:, 0, :], expert_w[:, 0, :], expert_w[:, 1, :], ALU.mult).then_inc(route_weighted, 1)
            full, free = filled(dve, ("expert_w",))
            nc.vector.tensor_copy(expert_w_col[:, :], full[0:SE, SE:SE + 1])
            nc.vector.tensor_copy(expert_w_all[:, :], full[:, 0:SE]).then_inc(free, 1)
            drained(dve, ("expert_w",))
            for e in range(SE + 1):
                last = nc.vector.tensor_scalar(past[:, e, :], hidden_id[:, :], float(e * SF), None, ALU.is_ge)
            settle(last)
            settle(nc.vector.tensor_tensor(past[:, 0:SE, :], past[:, 0:SE, :], past[:, 1:, :], ALU.subtract))
            settle(nc.vector.tensor_tensor(past[:, 0:SE, :], past[:, 0:SE, :],
                                           expert_w_all[:, :].unsqueeze(2).to_broadcast([P, SE, SC]), ALU.mult))
            nc.vector.tensor_reduce(hidden_w[:, :], past[:, 0:SE, :].rearrange("p e j -> p j e"), AX_X, ALU.add)\
                .then_inc(hidden_w_ready, 1)
            dve.wait_ge(hidden_w_ready, 1)
            dve.wait_ge(loads["sw2"], 16 * (1 + SC - SW2_FIRST))
            for j in range(SC):
                r = hidden_rows(j)
                nc.vector.tensor_scalar(sw2[j][0:r, :], sw2[j][0:r, :], hidden_w[0:r, j:j + 1], None, ALU.mult).then_inc(sw2_ready, 1)
            full, free = filled(dve, ("b2_mix",))
            nc.vector.tensor_copy(mix_bias[:, :], full).then_inc(free, 1)
            drained(dve, ("b2_mix",))
            for t in range(NT):
                settle(nc.vector.tensor_tensor(x_rows[:, t, :], x_rows[:, t, :], mix_bias[:, :], ALU.add))
            for t in range(NT):
                full, free = filled(dve, ("down", t))
                nc.vector.tensor_tensor(x_rows[:, t, :], full, x_rows[:, t, :], ALU.add).then_inc(free, 1)

        @block.tensor
        def _(pe):
            pe.wait_ge(consts_ready, 1)
            for w in ("Wk", "Wv", "Wl"):
                pe.wait_ge(loads[w], 16)
                for c in range(C):
                    out_b, full = claim(pe, ("wT", w, c))
                    for o in range(C):
                        cols = slice(c * P, c * P + P) if w == "Wl" else comp[c]
                        last = nc.tensor.transpose(out_b[:, o * P:o * P + P], w_rows[w][:, o, cols], ident[:, :])
                    last.then_inc(full, 1)
            for t in range(NT):
                pe.wait_ge(ln_ready[0], t + 1)
                out_b, full = claim(pe, ("xT", t))
                for c in range(C):
                    last = nc.tensor.transpose(out_b[:, c * P:c * P + P], ln_rows[:, t, comp[c]], ident[:, :])
                last.then_inc(full, 1)
            pe.wait_ge(loads["w_up"], 32)
            for t in range(NT):
                drained(pe, ("xT", t))
                out_b, full = claim(pe, ("sender", t))
                for c in range(C):
                    last = nc.tensor.matmul(out_b[:, c * P:c * P + P], xn_T[:, c, tile_cols[t]], w_up[:, min(c, 1), :],
                                            start=True, stop=True)
                last.then_inc(full, 1)
            for w in ("Wk", "Wv", "Wl"):
                for c in range(C):
                    drained(pe, ("wT", w, c))
            for t in range(NT):
                for w in ("Wk", "Wv"):
                    out_b, full = claim(pe, (w, t))
                    for c in range(C):
                        last = nc.tensor.matmul(out_b, xn_T[:, c, tile_cols[t]], w_T[w][:, c, :], start=(c == 0), stop=(c == C - 1))
                    last.then_inc(full, 1)
            out_b, full = claim(pe, ("kvT",))
            for t in range(NT):
                drained(pe, ("Wk", t))
                drained(pe, ("Wv", t))
            for c in range(C):
                for t in range(NT):
                    r = slice(0, rows(t))
                    last = nc.tensor.matmul(out_b[:, c * P:c * P + P], v_rows[r, t, c * P:c * P + P],
                                            k_rows[r, t, c * P:c * P + P], start=(t == 0), stop=(t == NT - 1))
            last.then_inc(full, 1)
            drained(pe, ("kvT",))
            for c in range(C):
                out_b, full = claim(pe, ("m2", c))
                nc.tensor.matmul(out_b, kv_T[:, c, :], w_T["Wl"][:, c, :], start=True, stop=True).then_inc(full, 1)
            for c in range(C):
                drained(pe, ("m2", c))
            pe.wait_ge(loads["Wq"], 16)
            for i in range(C):
                out_b, full = claim(pe, ("m3", i))
                for c in range(C):
                    last = nc.tensor.matmul(out_b, w_rows["Wq"][:, c, comp[i]], m2[:, c, :], start=(c == 0), stop=(c == C - 1))
                last.then_inc(full, 1)
            pe.wait_ge(loads["bq"], 16)
            out_b, full = claim(pe, ("mix_bias",))
            for c in range(C):
                last = nc.tensor.matmul(out_b, bq_col[:, c:c + 1].to_broadcast([P, P]), m2[:, c, :],
                                        start=(c == 0), stop=(c == C - 1))
            last.then_inc(full, 1)
            for c in range(C):
                drained(pe, ("m3", c))
            for t in range(NT):
                out_b, full = claim(pe, ("mix", t))
                for c in range(C):
                    last = nc.tensor.matmul(out_b, xn_T[:, c, tile_cols[t]], m3[:, c, :], start=(c == 0), stop=(c == C - 1))
                last.then_inc(full, 1)
            for b in range(8):
                pe.wait_ge(bank_free[b], before_edges[b])
            pe.wait_ge(loads["mlp"], 16 * (J + 6))
            for a in range(PAIRS):
                pe.sem_inc(ea_transposed[a], 1)
                pe.sem_inc(layer_done[a], 3)
            with pe.Fori(0, TURNS) as i:
                for a in range(PAIRS):
                    pe.wait_ge(ea_loaded[a], i * 16 + 16)
                    pe.wait_ge(silu_done[a], i * 3 + 3)
                    for h in range(2):
                        last = nc.tensor.transpose(psum[0:J * R, 2 * a, h * P:h * P + P], ea_slot[a][:, h, :], ident[:, :])
                    last.then_inc(ea_transposed[a], 1)
                for a in range(PAIRS):
                    pe.wait_ge(ea_T_ready[a], i + 1)
                    for q in range(2):
                        last = nc.tensor.matmul(psum[:, 2 * a + 1, q * 2 * P:(q + 1) * 2 * P], w_mlp1[:, q, :], ea_T[a][:, :],
                                                start=True, stop=True)
                    last.then_inc(layer_done[a], 1)
                for layer, w in ((1, w_mlp2), (2, w_mlp3)):
                    for a in range(PAIRS):
                        pe.wait_ge(silu_done[a], i * 3 + 3 + layer)
                        nc.tensor.matmul(psum[:, 2 * a + 1, :], w[:, :], h_slot[a][:, :], start=True, stop=True)\
                            .then_inc(layer_done[a], 1)
            for a in range(PAIRS):
                pe.wait_ge(silu_done[a], 3 + 3 * TURNS)

            def tile_weights(j):
                lhs = h3_slot[j // 2][:, j % 2, :]
                nc.tensor.matmul(tile_w[j % 2], lhs, w4_hi[:, :], start=True, stop=False)
                nc.tensor.matmul(tile_w[j % 2], lhs, w4_lo[:, :], start=False, stop=True).then_inc(weights_done, 1)

            pe.sem_inc(weights_done, 2 * J)
            pe.sem_inc(scatter_done, 2 * J)
            pe.wait_ge(padding_ready, 2)
            pe.wait_ge(consts_ready, 3)
            pe.wait_ge(span_ready, 1)
            pe.wait_ge(w4_ready, 1)
            pe.wait_ge(h3_loaded[0], 32)
            tile_weights(0)
            step = step_counter(pe, "pe_step")
            with pe.Fori(0, NT) as b:
                lo, hi = block_span(pe, b)
                pe.wait_ge(msg_flushed, b + 1)
                pe.wait_ge(adj_flushed, b + 1)
                for k in range(5):
                    nc.tensor.matmul(psum[:, k, :], zeros16[:, 0:P], zeros16[:, :], start=True, stop=False, skip_group_check=True)
                nc.tensor.matmul(adj_psum[:, bass.ds(b * P, P)], ident16[:, :], ident16[:, :], start=False, stop=True, skip_group_check=True)
                with pe.Fori(lo, hi) as u:
                    s = next_step(pe, step)
                    for j in range(J):
                        k = j % 2
                        if j == 1:
                            pe.wait_ge(h3_loaded[1], s * 32)
                        if j == J - 1:
                            pe.wait_ge(h3_loaded[0], s * 32 + 32)
                        tile_weights((j + 1) % J)
                        pe.wait_ge(products_done, s * J + J + j + 1)
                        pe.wait_ge(hot_y_ready, s * J + j + 1)
                        nc.tensor.matmul(psum[:, 0, :], hot_y[:, k, 0, :], prod[:, k, 0:D], start=False, stop=True, skip_group_check=True)
                        for m in range(3):
                            nc.tensor.matmul(psum[:, 1, m * MUL:m * MUL + MUL], hot_y[:, k, 1 + m, :],
                                             prod[:, k, D:D + MUL], start=False, stop=True, skip_group_check=True)
                        nc.tensor.matmul(psum[:, 1, 3 * MUL:], hot_f[:, k, :], prod[:, k, D + MUL:], start=False, stop=True,
                                         skip_group_check=True)
                        for a0 in range(0, NP, 512):
                            n = min(512, NP - a0)
                            last = nc.tensor.matmul(adj_psum[:, a0:a0 + n], hot_dst[:, k, :], hot_src[:, k, a0:a0 + n],
                                                    start=False, stop=True, skip_group_check=True)
                        last.then_inc(scatter_done, 1)
            def transposes(key, pieces):
                out_b, full = claim(pe, key)
                at = 0
                for piece in pieces:
                    r, n = piece.shape
                    last = nc.tensor.transpose(out_b[0:n, at:at + r], piece, ident[0:r, 0:r])
                    at += r
                last.then_inc(full, 1)

            def chunks(row):
                return [row[:, c * P:c * P + P] for c in range(row.shape[1] // P)]

            pe.wait_ge(msg_flushed, NT + 1)
            pe.wait_ge(adj_flushed, NT + 1)
            pe.wait_ge(loads["w_out"], 32)
            pe.wait_ge(loads["routers"], 64)
            pe.wait_ge(loads["expert_bias"], 16)
            for key in chain_order():
                if key[0] == "routersT":
                    transposes(key, chunks(router_rows))
                elif key[0] == "expert_biasT":
                    transposes(key, [expert_bias_rows])
                elif key[0] in ("msgT0", "msgT1"):
                    h0 = D * (key[0] == "msgT1")
                    transposes(key, chunks(msg_rows[:, key[1], h0:h0 + D]))
                elif key[0] == "hT":
                    pe.wait_ge(ln_ready[2], key[1] + 1)
                    transposes(key, chunks(hx_rows[:, key[1], :]))
                elif key[0] == "router_bias":
                    pe.wait_ge(routers_ready, 1)
                    out_b, full = claim(pe, key)
                    for c in range(C):
                        last = nc.tensor.matmul(out_b[:, 0:EX], routers_T[:, c, EX + PARTS + 1:EX + PARTS + 2].to_broadcast([P, P]),
                                                routers_T[:, c, 0:EX], start=(c == 0), stop=(c == C - 1))
                    last.then_inc(full, 1)
                elif key[0] == "logits":
                    drained(pe, ("hT", key[1]))
                    out_b, full = claim(pe, key)
                    for c in range(C):
                        last = nc.tensor.matmul(out_b[:, 0:EX], xn_T[:, c, tile_cols[key[1]]], routers_scaled[:, c, :],
                                                start=(c == 0), stop=(c == C - 1))
                    last.then_inc(full, 1)
                else:
                    t = key[1]
                    drained(pe, ("msgT0", t))
                    drained(pe, ("msgT1", t))
                    out_b, full = claim(pe, key)

                    def chunk(i):
                        return msg_T[:, t % 2, i * P:i * P + P]

                    for c, (i0, i1) in enumerate(((0, 7), (4, 1), (5, 2), (6, 3))):
                        w = w_out[:, min(c, 1), :, :]
                        nc.tensor.matmul(out_b[:, c * P:c * P + P], chunk(i0), w[:, 0, :], start=True, stop=False)
                        last = nc.tensor.matmul(out_b[:, c * P:c * P + P], chunk(i1), w[:, 1, :], start=False, stop=True)
                    last.then_inc(full, 1)

            def adjacency(s0, s1):
                for s in range(s0, s1):
                    for g, (g0, w) in enumerate(GROUPS):
                        transposes(("adjT", s, g), [adj_rows[:, b, tile_cols[s]] for b in range(g0 // P, (g0 + w) // P)])

            adjacency(0, ADJ_FIRST)
            pe.wait_ge(members_ready, 1)
            pe.wait_ge(consts_ready, 4)
            out_b, full = claim(pe, ("rank",))
            nc.tensor.matmul(out_b[:, 0:(NT + 1) * EX], ones_col[:, :].to_broadcast([P, P]),
                             members_before[:, :, :].rearrange("p t e -> p (t e)"), start=True, stop=False, skip_group_check=True)
            nc.tensor.matmul(out_b[:, 0:NT * EX], before_me[:, :], member[:, :, :].rearrange("p t e -> p (t e)"),
                             start=False, stop=True, skip_group_check=True).then_inc(full, 1)
            adjacency(ADJ_FIRST, NT)
            pe.wait_ge(gates_ready, 1)
            for g, (g0, w) in enumerate(GROUPS):
                transposes(("gateT", g), [token_gates[:, t, :] for t in range(g0 // P, (g0 + w) // P)])
            pe.wait_ge(loads["expert_b2"], 16)
            for t in range(NT):
                drained(pe, ("gateT", min(t * P // 512, len(GROUPS) - 1)))
                out_b, full = claim(pe, ("b2", t))
                nc.tensor.matmul(out_b, gates_T[:, tile_cols[t]], expert_b2[:, :], start=True, stop=True).then_inc(full, 1)
            pe.wait_ge(loads["biases"], 48)
            transposes(("biasT",), [bias_rows[:, :]])
            for b in range(8):
                pe.wait_ge(bank_free[b], before_experts[b])

            def tile_transposes(n, loaded):
                pe.wait_ge(tile_loaded, loaded)
                pe.wait_ge(tile_T_ready, n)
                for c in range(C):
                    last = nc.tensor.transpose(psum[:, T_BANK, c * P:c * P + P], tile_rows[:, c * P:c * P + P], ident[:, :])
                last.then_inc(tile_transposed, 1)

            pe.wait_ge(tile_loaded, 16)
            for c in range(C):
                last = nc.tensor.transpose(psum[:, T_BANK, c * P:c * P + P], tile_rows[:, c * P:c * P + P], ident[:, :])
            last.then_inc(tile_transposed, 1)
            pe.sem_inc(down_done, 1)
            with pe.Fori(0, EX // 2) as i:
                bounds = expert_bounds(pe, i)
                for a in range(2):
                    lo, hi = bounds[a:a + 2]
                    pe.wait_ge(ew1_loaded[a], i * 16 + 16)
                    pe.sem_inc(experts_started, 1)
                    with pe.Fori(lo, hi) as t:
                        def down(f):
                            if f == 0:
                                pe.wait_ge(ew2_loaded[a], i * 32 + 32)
                                pe.wait_ge(tile_out_ready, t + 1)
                            pe.wait_ge(gelu_done, t * FC + UP_BANKS + f + 1)
                            w2 = ew2_lo[a][:, f, :] if f < HALF else ew2_hi[a][:, f - HALF, :]
                            last = nc.tensor.matmul(psum[:, Y_BANK, :], hid[:, f, :], w2, start=(f == 0), stop=(f == FC - 1))
                            if f == FC - 1:
                                last.then_inc(down_done, 1)

                        pe.wait_ge(tile_T_ready, t + 1)
                        for f in range(FC):
                            pe.wait_ge(gelu_done, t * FC + f + 1)
                            for c in range(C):
                                last = nc.tensor.matmul(psum[:, f % UP_BANKS, 0:P], ew1[a][:, c, f * P:f * P + P], tile_T[:, c, :],
                                                        start=(c == 0), stop=(c == C - 1))
                            last.then_inc(up_done, 1)
                            if f >= 2:
                                down(f - 2)
                        pe.wait_ge(tile_loaded, t * 16 + 32)
                        for c in range(C):
                            last = nc.tensor.transpose(psum[:, T_BANK, c * P:c * P + P], tile_rows[:, c * P:c * P + P], ident[:, :])
                        last.then_inc(tile_transposed, 1)
                        down(FC - 2)
                        down(FC - 1)
            count = pe.value_load(first_tile_int[0:1, EX:EX + 1], min_val=EX, max_val=TILES)
            pe.wait_ge(tile_out_ready, count + 1)
            pe.wait_ge(tile_T_ready, count + 1)
            pe.wait_ge(loads["adj_T"], 16)
            open_banks = [claim(pe, ("agg1", t)) for t in range(AGG_OPEN)]
            for s in range(NT):
                pe.wait_ge(z_ready, s + 1)
                r = rows(s)
                for t, (out_b, full) in enumerate(open_banks):
                    last = nc.tensor.matmul(out_b, adj_in[0:r, s, tile_cols[t]], z_rows[0:r, s, :], start=(s == 0), stop=(s == NT - 1))
                    if s == NT - 1:
                        last.then_inc(full, 1)

            def aggregate(key, rows_ap, t):
                out_b, full = claim(pe, (key, t))
                for s in range(NT):
                    r = rows(s)
                    last = nc.tensor.matmul(out_b, adj_in[0:r, s, tile_cols[t]], rows_ap[0:r, s, :], start=(s == 0), stop=(s == NT - 1))
                last.then_inc(full, 1)

            def project(key, t, lhs, rhs):
                out_b, full = claim(pe, (key, t))
                for c in range(len(rhs)):
                    last = nc.tensor.matmul(out_b[:, 0:rhs[c].shape[1]], lhs[:, c, tile_cols[t]], rhs[c], start=(c == 0), stop=(c == len(rhs) - 1))
                last.then_inc(full, 1)

            for key in agg_order():
                if key[0] == "agg1":
                    aggregate("agg1", z_rows, key[1])
                elif key[0] == "xn2T":
                    transposes(key, chunks(xn2_rows[:, key[1], :]))
                else:
                    drained(pe, ("agg1", key[1]))
                    transposes(key, chunks(ah_rows[:, key[1] % 2, :]))
            pe.wait_ge(loads["gw1"], 16)
            for t in range(NT):
                drained(pe, ("ahT", t))
            for f in range(HC):
                for g, (g0, w) in enumerate(GROUPS):
                    out_b, full = claim(pe, ("h1T", f, g))
                    for c in range(C):
                        last = nc.tensor.matmul(out_b[:, 0:w], gw1[:, c, f * P:f * P + P], ah_T[:, c, g0:g0 + w], start=(c == 0), stop=(c == C - 1))
                    last.then_inc(full, 1)
            for f in range(HC):
                for g in range(len(GROUPS)):
                    drained(pe, ("h1T", f, g))
            pe.wait_ge(loads["gw2_first"], 16)
            pe.wait_ge(loads["gw2_last"], 16)
            for t in range(NT):
                project("y2", t, h1_T, gw2)
            for t in range(NT):
                drained(pe, ("y2", t))
            for t in range(NT):
                aggregate("agg2", z2_rows, t)
            pe.wait_ge(loads["w_qkv"], 16)
            for m in range(C):
                for g, (g0, w) in enumerate(GROUPS):
                    out_b, full = claim(pe, ("kT", m, g))
                    for c in range(C):
                        last = nc.tensor.matmul(out_b[:, 0:w], w_qkv[:, c, D + m * P:D + m * P + P], xn_T[:, c, g0:g0 + w],
                                                start=(c == 0), stop=(c == C - 1))
                    last.then_inc(full, 1)
            for t in range(NT):
                project("q", t, xn_T, [w_qkv[:, c, 0:D] for c in range(C)])
            for t in range(NT):
                project("v", t, xn_T, [w_qkv[:, c, 2 * D:3 * D] for c in range(C)])
            for m in range(C):
                for g in range(len(GROUPS)):
                    drained(pe, ("kT", m, g))
            for t in range(NT):
                out_b, full = claim(pe, ("ek", t))
                r = rows(t)
                for c in range(C):
                    last = nc.tensor.transpose(out_b[0:r, c * P:c * P + P], ek_T[:, c, t * P:t * P + r], ident[:, :])
                last.then_inc(full, 1)
            for t in range(NT):
                drained(pe, ("v", t))
                drained(pe, ("ek", t))
            out_b, full = claim(pe, ("ctxT",))
            for c in range(C):
                for t in range(NT):
                    r = slice(0, rows(t))
                    last = nc.tensor.matmul(out_b[:, c * P:c * P + P], vx_rows[r, t, c * P:c * P + P],
                                            ek_rows[r, t, c * P:c * P + P], start=(t == 0), stop=(t == NT - 1))
            last.then_inc(full, 1)
            drained(pe, ("ctxT",))
            pe.wait_ge(loads["w_att"], 16)
            for c in range(C):
                out_b, full = claim(pe, ("m5", c))
                nc.tensor.matmul(out_b, kv_T[:, c, :], w_att[:, c, :], start=True, stop=True).then_inc(full, 1)
            pe.wait_ge(k_scale_ready, 1)
            for t in range(NT):
                pe.wait_ge(q_ready, t + 1)
                transposes(("qT", t), chunks(q_rows[:, t, :]))
            for c in range(C):
                drained(pe, ("m5", c))
            for t in range(NT):
                drained(pe, ("qT", t))
                project("att", t, q_T, [m5[:, c, :] for c in range(C)])
            for t in range(NT):
                pe.wait_ge(ln_ready[5], t + 1)
                transposes(("lastT", t), chunks(last_rows[:, t, :]))
            pe.wait_ge(loads["sw1"], 16 * SE)
            for t in range(NT):
                drained(pe, ("lastT", t))
            for key in ffn_order():
                if key == ("route",):
                    pe.wait_ge(mean_ready, 1)
                elif key == ("expert_w",):
                    pe.wait_ge(route_weighted, 1)
                elif key == ("b2_mix",):
                    drained(pe, ("expert_w",))
                    pe.wait_ge(loads["shared_b2"], 16)
                out_b, full = claim(pe, key)
                if key == ("route",):
                    for c in range(C):
                        last = nc.tensor.matmul(out_b[0:1, 0:PARTS], mean_col[:, c:c + 1], routers_T[:, c, EX:EX + PARTS],
                                                start=(c == 0), stop=(c == C - 1))
                elif key == ("expert_w",):
                    nc.tensor.matmul(out_b[:, 0:SE], ones_col[0:1, :].to_broadcast([1, P]), expert_w[:, 0, :], start=True, stop=True)
                    last = nc.tensor.matmul(out_b[0:SE, SE:SE + 1], expert_w[:, 0, :], ones_col[0:1, :], start=True, stop=True)
                elif key == ("b2_mix",):
                    last = nc.tensor.matmul(out_b, expert_w_col[:, :].to_broadcast([SE, P]), expert_b2[0:SE, :], start=True, stop=True)
                elif key[0] == "up":
                    _, g, j = key
                    n, r, n0 = len(TURN_TILES[g]) * P, hidden_rows(j), TURN_TILES[g][0] * P
                    for c in range(C):
                        last = nc.tensor.matmul(out_b[0:r, 0:n], sw1_cols[:, c, j * P:j * P + r], xn_T[:, c, n0:n0 + n],
                                                start=(c == 0), stop=(c == C - 1))
                else:
                    t = key[1]
                    g, off = t * P // TG, t * P % TG
                    if off == 0:
                        for j in range(SC):
                            drained(pe, ("up", g, j))
                    if t == 0:
                        pe.wait_ge(sw2_ready, SC)
                    for j in range(SC):
                        r = hidden_rows(j)
                        last = nc.tensor.matmul(out_b, shid[g % 2][0:r, j, off:off + P], sw2[j][0:r, :], start=(j == 0), stop=(j == SC - 1))
                last.then_inc(full, 1)


def kernel(**inputs):
    import numpy as _np
    import concourse.bacc as _bacc
    from concourse import mybir as _mybir
    from concourse.bass_utils import run_bass_kernel_spmd as _run

    nc = _bacc.Bacc("TRN2", target_bir_lowering=False, num_devices=1)
    arrays, aps = {}, {}
    for name, value in inputs.items():
        a = _np.ascontiguousarray(value)
        arrays[f"in_{name}"] = a
        aps[name] = nc.dram_tensor(f"in_{name}", a.shape, _mybir.dt.from_np(a.dtype), kind="ExternalInput").ap()
    out = nc.dram_tensor("out_x", aps["x"].shape, F32, kind="ExternalOutput").ap()
    graph_block_kernel(nc, aps, out)
    r = _run(nc, [arrays], core_ids=[0])
    return r.results[0]["out_x"]
```

```python
import math
from contextlib import ExitStack

import concourse.bass as bass
from concourse import mybir

P = 128
F32 = mybir.dt.float32
BF16 = mybir.dt.bfloat16
F16 = mybir.dt.float16
F32R = mybir.dt.float32r
I32 = mybir.dt.int32
ALU = mybir.AluOpType
ACT = mybir.ActivationFunctionType
AX_X = mybir.AxisListType.X
RMAX = bass.bass_isa.ReduceOp.max

SILU_2MOM = 1.679177
AVG_NUM_NEIGHBORS = 10.0
LN_EPS = 1e-5


class BankRing:

    def __init__(self, banks):
        self.turn, self.used, self.at = 0, [0] * banks, {}

    def plan(self, keys, banks=None):
        for i, key in enumerate(keys):
            if banks is None:
                b = self.turn % len(self.used)
                self.turn += 1
            else:
                b = banks[i % len(banks)]
            self.at[key] = (b, self.used[b])
            self.used[b] += 1

    def uses(self, bank):
        return self.used[bank]


def graph_block_kernel(nc, A, out):
    N, D = A["x"].shape
    E = A["src"].shape[0]
    NT = -(-N // P)
    NP = NT * P
    C = D // P
    MUL = A["L0_gnn_W_up0"].shape[0]
    HID = A["L0_gnn_W_mlp2"].shape[0]
    R = A["edge_attr_8"].shape[1]
    Y = A["edge_attr_4"].shape[1]
    J = 4
    U = J * P
    UNITS = -(-E // U)
    FULL = E // U
    PAIRS = 3
    TURNS = -(-UNITS // (2 * PAIRS))
    EPAD = TURNS * 2 * PAIRS * U
    HEADS, HD = 8, D // 8

    def rows(t):
        return min(P, N - t * P)

    ctx = ExitStack()
    with ctx:
        def sb(name, shape, dt=F32):
            return ctx.enter_context(nc.sbuf_tensor(name, shape, dt))

        def sem(name):
            return ctx.enter_context(nc.semaphore(name))

        def dram(name, shape, dt=F32):
            return nc.dram_tensor(name, shape, dt).ap()

        sender_table = dram("sender_table", (NP, D))
        edge_in = dram("edge_in", (EPAD, R))
        edge_hidden = dram("edge_hidden", (2, TURNS * 2 * PAIRS, 2, P, P))

        ident = sb("ident", [P, P])
        table = sb("table", [P, NP])
        iota_nodes = table[:, 0:NP // 2].bitcast(F16)
        assert NP <= 2048
        block_lo = sb("block_lo", [P, NT])
        unit_id = sb("unit_id", [P, 1])
        zeros16 = sb("zeros16", [P, D], BF16)
        x_rows = sb("x_rows", [P, NT, D])
        HID_SLOTS = 4
        with ExitStack() as overlay:
            hid_hi, hid_lo = [overlay.enter_context(nc.sbuf_tensor(f"hid_{part}", [P, HID_SLOTS, P], F32R)) for part in ("hi", "lo")]
        xn_T = sb("xn_T", [P, C, NP])
        stats = sb("stats", [P, NT, 6])
        meanvar = sb("meanvar", [P, NT, 2])
        rstd = sb("rstd", [P, NT])
        SE, SF = A["L1_ffn_b1"].shape
        SC = -(-SE * SF // P)
        TG = 2 * P
        with ExitStack() as overlay:
            shid_hi = overlay.enter_context(nc.sbuf_tensor("shid_hi", [P, 2, SC, TG], F32R))
        big_a = sb("big_a", [P, NT * NP])
        with ExitStack() as overlay:
            shid_lo = overlay.enter_context(nc.sbuf_tensor("shid_lo", [P, 2, SC, TG], F32R))
        big_b = sb("big_b", [P, NT * NP])
        ln_rows = big_a[:, 0:NT * D].rearrange("p (t d) -> p t d", d=D)
        sender_rows = big_a[:, NT * D:2 * NT * D].rearrange("p (t d) -> p t d", d=D)
        k_rows = big_b[:, 0:NT * D].rearrange("p (t d) -> p t d", d=D)
        v_rows = big_b[:, NT * D:2 * NT * D].rearrange("p (t d) -> p t d", d=D)
        adj_rows = big_a[:, :].rearrange("p (t n) -> p t n", n=NP)
        msg_rows = big_b[:, 0:NT * 2 * D].rearrange("p (t d) -> p t d", d=2 * D)

        with ExitStack() as overlay:
            def sb_r(name, shape):
                return overlay.enter_context(nc.sbuf_tensor(name, shape, F32R))

            h3_hi = [sb_r(f"h3_hi{a}", [P, 2, 2, P]) for a in range(PAIRS)]
            h3_lo = [sb_r(f"h3_lo{a}", [P, 2, 2, P]) for a in range(PAIRS)]
            h3_slot = [sb_r(f"h3_slot{q}", [P, 2, P]) for q in range(2)]
            w4_hi = sb_r("w4_hi", [P, 4 * MUL])
            w4_lo = sb_r("w4_lo", [P, 4 * MUL])
            OVERLAY = 2 * PAIRS * 4 * P + 2 * 2 * P + 2 * 4 * MUL
            W2_HI = A["L0_ffn_W1"].shape[2] // P // 2 * D
            sb_r("ahead_of_w2", [P, 2 * W2_HI - OVERLAY])
            w2_hi = sb_r("w2_hi", [P, 2, D])
            w2_lo = sb_r("w2_lo", [P, 2, D])
        wide = sb("wide", [P, 5 * C * D])

        def weight(region, i):
            return region[:, i * C * D:(i + 1) * C * D].rearrange("p (c d) -> p c d", d=D)

        spare_a, spare_b = big_a[:, 2 * NT * D:], big_b[:, 2 * NT * D:]
        w_rows = {"Wk": weight(wide, 0), "Wv": weight(wide, 1), "Wl": weight(wide, 2), "Wq": weight(big_a, 0)}
        w_T = {"Wk": weight(wide, 3), "Wv": weight(wide, 4), "Wl": weight(spare_a, 0)}
        m2, m3 = weight(wide, 0), weight(wide, 1)
        mix_bias = sb("mix_bias", [P, D])
        w_up = sb("w_up", [P, 2, MUL])
        bq_col = sb("bq_col", [P, C])
        b_row = {n: sb(f"{n}_row", [P, D]) for n in ("bk", "bv", "bl")}
        kv_T = sb("kv_T", [P, C, P])
        w_mlp1 = sb("w_mlp1", [J * R, 2, 2 * HID])
        w_mlp2 = sb("w_mlp2", [P, P])
        w_mlp3 = sb("w_mlp3", [P, P])
        w_mlp4 = sb("w_mlp4", [P, 4 * MUL])
        w_out = sb("w_out", [P, 2, 2, MUL])

        dst_units = big_b[0:UNITS, 0:U].bitcast(I32)
        dst_unitf = big_b[0:UNITS, U:2 * U]
        unit_max = sb("unit_max", [UNITS, 1])
        unit_min = sb("unit_min", [UNITS, 1])
        touch = sb("touch", [UNITS, 4, NT])
        reach = sb("reach", [UNITS, 2 * NT])
        reach_all = sb("reach_all", [UNITS, 2 * NT])
        span_f = sb("span_f", [1, 2, NT])
        span = sb("span", [1, 2, NT], I32)
        dst_int = sb("dst_int", [P, UNITS, J], I32)
        src_int = sb("src_int", [P, UNITS, J], I32)
        edges = spare_b[:, 0:UNITS * J * (Y + 2)].rearrange("p (u k) -> p u k", u=UNITS)
        class Space:
            def __init__(self, region):
                self.region, self.used = region, 0

            def take(self, n):
                self.used += n
                assert self.used <= self.region.shape[-1]
                return self.region[:, self.used - n:self.used]

        mlp_space = Space(wide[:, OVERLAY:])
        ea_slot = [mlp_space.take(2 * J * R).rearrange("p (h k) -> p h k", h=2) for a in range(PAIRS)]
        ea_T = [mlp_space.take(2 * P)[0:J * R, :] for a in range(PAIRS)]
        h_slot = [mlp_space.take(4 * P) for a in range(PAIRS)]
        h3_out = [mlp_space.take(4 * P).rearrange("p (u q n) -> p u q n", u=2, q=2) for a in range(PAIRS)]
        edge_space = Space(xn_T[:, :, :].rearrange("p c n -> p (c n)")[:, 2 * D:])
        edge_slot = edge_space.take(J * (Y + 2))
        idx_slot = [sb(f"idx_slot{j}", [P, 1], I32) for j in range(J)]
        sent = [edge_space.take(D) for j in range(J)]
        hot_f = edge_space.take(2 * P).rearrange("p (k n) -> p k n", k=2)
        hot_y = edge_space.take(2 * Y * P).rearrange("p (k y n) -> p k y n", k=2, y=Y)
        dot = edge_space.take(2 * MUL).rearrange("p (k n) -> p k n", k=2)
        edge_space2 = Space(wide[:, OVERLAY:])
        scaled = edge_space2.take(2 * 3 * MUL).rearrange("p (k m u) -> p k m u", k=2, m=3)
        prod = edge_space2.take(2 * 6 * MUL).rearrange("p (k n) -> p k n", k=2)
        hot_dst = edge_space2.take(P).bitcast(BF16).rearrange("p (k n) -> p k n", k=2)
        hot_src = edge_space2.take(NP).bitcast(BF16).rearrange("p (k n) -> p k n", k=2)
        msg_T = wide[:, 0:4 * D].rearrange("p (k n) -> p k n", k=2)
        assert edge_space.used <= C * NP - 2 * D and max(mlp_space.used, edge_space2.used) <= 5 * C * D - OVERLAY

        psum = ctx.enter_context(nc.psum_tensor("psum", [P, 8, 512], F32))
        msg_psum = psum[:, 0:2, :].rearrange("p k n -> p (k n)")
        adj_psum = psum[:, 2:5, :].rearrange("p k n -> p (k n)")
        tile_w = [psum[:, 5 + k, :] for k in range(2)]
        ring = BankRing(8)

        ring.plan([("wT", w, c) for w in ("Wk", "Wv", "Wl") for c in range(C)])
        ring.plan([("xT", t) for t in range(NT)])
        ring.plan([("sender", t) for t in range(NT)])
        ring.plan([(w, t) for t in range(NT) for w in ("Wk", "Wv")])
        ring.plan([("kvT",)])
        ring.plan([("m2", c) for c in range(C)])
        ring.plan([("m3", c) for c in range(C)] + [("mix_bias",)])
        ring.plan([("mix", t) for t in range(NT)])
        before_edges = [ring.uses(b) for b in range(8)]
        def chain_order():
            yield from [("routersT",), ("expert_biasT",), ("msgT0", 0), ("msgT1", 0), ("router_bias",)]
            for t in range(NT):
                if t + 1 < NT:
                    yield from [("msgT0", t + 1), ("msgT1", t + 1)]
                yield ("conv", t)
                if t >= 3:
                    yield ("logits", t - 3)
                if t >= 2:
                    yield ("hT", t - 2)
            for t in range(NT - 2, NT):
                yield from [("logits", t - 1), ("hT", t)]
            yield ("logits", NT - 1)
        ring.plan(list(chain_order()))

        bank_full = [sem(f"bank_full{b}") for b in range(8)]
        bank_free = [sem(f"bank_free{b}") for b in range(8)]
        loads = {}

        def load_sem(name):
            loads[name] = sem(f"{name}_loaded")
            return loads[name]

        for n in ("x", "x_rest", "w_up", "Wk", "Wv", "Wl", "Wq", "bq", "mix_b", "mlp", "w_out", "dst_units",
                  "edge_tables", "edge_in"):
            load_sem(n)
        consts_ready = sem("consts_ready")
        ident_zeroed = sem("ident_zeroed")
        padding_ready = sem("padding_ready")
        dve_step = sem("dve_step")
        stats_ready = sem("stats_ready")
        std_ready = sem("std_ready")
        ln_ready = {n: sem(f"ln_ready{n}") for n in (0, 2, 3, 5)}
        loop_entered = sem("loop_entered")
        sender_stored = sem("sender_stored")
        reach_ready = sem("reach_ready")
        reach_max_ready = sem("reach_max_ready")
        span_ready = sem("span_ready")
        ea_loaded = [sem(f"ea_loaded{a}") for a in range(PAIRS)]
        ea_transposed = [sem(f"ea_transposed{a}") for a in range(PAIRS)]
        ea_T_ready = [sem(f"ea_T_ready{a}") for a in range(PAIRS)]
        layer_done = [sem(f"layer_done{a}") for a in range(PAIRS)]
        silu_done = [sem(f"silu_done{a}") for a in range(PAIRS)]
        h3_stored = [sem(f"h3_stored{a}") for a in range(PAIRS)]
        h3_out_free = [sem(f"h3_out_free{a}") for a in range(PAIRS)]
        h3_split = [sem(f"h3_split{a}") for a in range(PAIRS)]
        h3_loaded = [sem(f"h3_loaded{q}") for q in range(2)]
        w4_ready = sem("w4_ready")
        hi_ready = [sem(f"hi_ready{a}") for a in range(PAIRS)]
        dot_ready = sem("dot_ready")
        hot_ready = sem("hot_ready")
        hot_y_ready = sem("hot_y_ready")
        scaled_ready = sem("scaled_ready")
        weights_done = sem("weights_done")
        scatter_done = sem("scatter_done")
        products_done = sem("products_done")
        edge_slot_ready = sem("edge_slot_ready")
        gathered = [sem(f"gathered{j}") for j in range(J)]
        idx_ready = sem("idx_ready")
        msg_flushed = sem("msg_flushed")
        adj_flushed = sem("adj_flushed")
        out_stored = sem("out_stored")

        EX = A["L0_ffn_w_r"].shape[0]
        TOP = 2
        FH = A["L0_ffn_W1"].shape[2]
        FC = FH // P
        TILES = (TOP * N + EX * P) // P
        H1 = A["L1_gnn_b1"].shape[0]
        HC = H1 // P
        PARTS = A["L1_ffn_router_w"].shape[0]
        GROUPS = [(g, min(512, NP - g)) for g in range(0, NP, 512)]
        KEY_COLS = [min(w, N - g) for g, w in GROUPS]

        adj_dram = dram("adj_dram", (P, NT, NP))
        tokens_sorted = dram("tokens_sorted", ((TILES + 2) * P, D))
        mixed_sorted = dram("mixed_sorted", (TILES * P, D))

        late = Space(table[:, 16:])
        late_dst = Space(dst_int[:, :, :].rearrange("p u j -> p (u j)").bitcast(F32))
        late_src = Space(src_int[:, :, :].rearrange("p u j -> p (u j)").bitcast(F32))
        ident16 = sb("ident16", [P, P], BF16)
        before_me = late_src.take(P)
        ones_col = sb("ones_col", [P, 1])
        real_row = sb("real_row", [P, 1])
        dinv = sb("dinv", [P, NT])
        bias_rows = late_src.take(P)[0:HC + SC, :]
        bias_T = late.take(HC + SC)
        expert_bias_T = late.take(EX * FC)
        expert_b2 = w_mlp4[0:EX, :]
        routers_T = late.take(C * (EX + PARTS + 2)).rearrange("p (a b) -> p a b", b=(EX + PARTS + 2))
        ln_g, ln_b = routers_T[:, :, EX + PARTS:EX + PARTS + 1], routers_T[:, :, EX + PARTS + 1:EX + PARTS + 2]
        router_bias = sb("router_bias", [P, EX])
        logits = late.take(NT * EX).rearrange("p (a b) -> p a b", b=EX)
        top_val = late.take(NT * 8).rearrange("p (a b) -> p a b", b=8)
        top_idx = late.take(NT * 8).bitcast(mybir.dt.uint32).rearrange("p (a b) -> p a b", b=8)
        choice_f = late.take(TOP * NT).rearrange("p (a b) -> p a b", b=NT)
        chosen = late.take(TOP * NT * EX).rearrange("p (k a b) -> p k a b", k=TOP, b=EX)
        routers_scaled = late_dst.take(C * EX).rearrange("p (c e) -> p c e", c=C)
        member = late.take(NT * EX).rearrange("p (a b) -> p a b", b=EX)
        members_before = late.take((NT + 1) * EX).rearrange("p (a b) -> p a b", b=EX)
        place = late_dst.take(NT * EX).rearrange("p (a b) -> p a b", b=EX)
        tile_tests = late_dst.take(EX * NT).rearrange("p (a b) -> p a b", b=NT)
        first_tile = late.take(EX + 1)
        expert_tiles = late.take(EX)
        place_base = late.take(EX)
        first_tile_int = late.take(EX + 1)[0:1, :].bitcast(I32)
        slot_f = late.take(TOP * NT).rearrange("p (a b) -> p a b", b=NT)
        slot_int = late.take(TOP * NT).bitcast(I32).rearrange("p (a b) -> p a b", b=NT)
        gate = late.take(TOP * NT).rearrange("p (a b) -> p a b", b=NT)
        gap = late.take(NT)
        ln_pair = late.take(2 * NT).rearrange("p (t k) -> p t k", k=2)
        ln_root = late.take(2 * NT).rearrange("p (t k) -> p t k", k=2)
        x_scale = late.take(NT)
        x_shift = late.take(NT)
        gate_by_slot = late.take(TOP * NT).rearrange("p (k t) -> p k t", k=TOP)
        slot_order = late.take(NT)
        slot_sorted = late.take(TOP * NT).rearrange("p (k t) -> p k t", k=TOP)

        xn_flat = xn_T[:, :, :].rearrange("p c n -> p (c n)")
        router_rows = xn_flat[0:EX + PARTS + 2, 0:D]
        expert_bias_rows = xn_flat[:, D:D + P]
        def grid(region, a, b, k):
            return region[:, a:a + b * k].rearrange("p (a k) -> p a k", k=k)

        adj_T = grid(big_b, 0, NT, NP)
        hx_rows = grid(wide, NT * D, NT, D)
        spare_x = FC * P + 3 * D
        gates_T = xn_flat[0:EX, spare_x:spare_x + NP]
        token_gates = grid(xn_flat, spare_x + NP, NT, EX)
        HALF = FC // 2
        ew1 = [grid(r, 0, C, FH) for r in (big_a, big_b)]
        ew2_lo = [grid(r, C * FH, HALF, D) for r in (big_a, big_b)]
        ew2_hi = [grid(wide, a * HALF * D, HALF, D) for a in range(2)]
        def w2_chunk(a, f):
            return ew2_lo[a][:, f, :] if f < HALF else ew2_hi[a][:, f - HALF, :]

        hid = grid(xn_flat, 2 * HID_SLOTS * P, HID_SLOTS, P)
        tile_rows = xn_flat[:, FC * P:FC * P + D]
        tile_T = grid(xn_flat, FC * P + D, C, P)
        tile_out = xn_flat[:, FC * P + 2 * D:FC * P + 3 * D]
        first_rows = [wide[:, t * D:(t + 1) * D] if t < HALF else xn_flat[:, spare_x + (t - HALF) * D:spare_x + (t - HALF + 1) * D]
                      for t in range(NT)]
        second_rows = [big_b[:, t * D:(t + 1) * D] for t in range(NT)]
        degree = late.take(NT)
        adj_in = grid(big_a, 0, NT, NP)
        xn2_rows = grid(wide, 0, NT, D)
        z_rows = grid(wide, NT * D, NT, D)
        ah_T = grid(big_b, 0, C, NP)
        ah_rows = grid(big_b, NT * D, 2, D)
        gw1 = grid(big_b, (NT + 2) * D, C, H1)
        h1_T = grid(wide, 0, HC, NP)
        GW2_FIRST = 5
        gw2 = [big_b[:, (NT + 2) * D + C * H1 + i * D:(NT + 2) * D + C * H1 + (i + 1) * D] for i in range(GW2_FIRST)]
        gw2 += [big_b[:, i * D:(i + 1) * D] for i in range(HC - GW2_FIRST)]
        z2_rows = grid(big_b, (HC - GW2_FIRST) * D, NT, D)
        conv_out = grid(big_b, (HC - GW2_FIRST + NT) * D, 2, D)
        w_qkv = grid(wide, 0, C, 3 * D)
        w_att = grid(wide, 3 * C * D, C, D)
        m5 = grid(wide, 4 * C * D, C, D)
        EK = (HC - GW2_FIRST + NT) * D
        ek_T = grid(big_b, EK, C, NP)
        q_T = ek_T
        ek_rows = grid(big_b, 0, NT, D)
        q_rows = grid(big_a, 0, NT, D)
        att_rows = q_rows
        vx_rows = grid(big_a, NT * D, NT, D)
        k_max3 = late.take(C * len(GROUPS)).rearrange("p (a b) -> p a b", b=len(GROUPS))
        k_max = late.take(C)
        k_sum = late.take(C)
        k_scale = late.take(C)
        q_max = late.take(HEADS)
        q_sum = late.take(2 * HEADS).rearrange("p (a h) -> p a h", a=2)
        last_rows = vx_rows
        sw1 = wide[:, 0:C * SE * SF].rearrange("p (c e f) -> p c e f", c=C, e=SE)
        sw1_cols = wide[:, 0:C * SE * SF].rearrange("p (c h) -> p c h", c=C)
        SHID_END = 2 * SC * TG
        SW2_FIRST = (NT * NP - SHID_END) // D
        sw2 = [big_a[:, SHID_END + j * D:SHID_END + (j + 1) * D] for j in range(SW2_FIRST)]
        sw2 += [big_b[:, SHID_END + j * D:SHID_END + (j + 1) * D] for j in range(SC - SW2_FIRST)]
        SHID_SLOTS = 4
        shid_full = grid(big_b, SHID_END + (SC - SW2_FIRST) * D, SHID_SLOTS, TG)
        UP_BANKS, Y_BANK = 4, 4

        def tile_psum(c):
            return psum[:, 5 + 2 * c // C, (c % (C // 2)) * P:(c % (C // 2) + 1) * P]

        last_shift = rstd
        mean_col = late.take(C)
        route = late.take(PARTS)[0:1, :]
        route_top = late.take(8)[0:1, :]
        route_idx = late.take(8)[0:1, :].bitcast(mybir.dt.uint32)
        route_f = late.take(8)[0:1, :]
        route_coef = late.take(2 * PARTS)[0:1, :].rearrange("p (a b) -> p a b", b=PARTS)
        part_weights = late_src.take(SE * PARTS)[0:1, :].rearrange("p (a b) -> p a b", b=PARTS)
        part_prod = late.take(SE * PARTS)[0:1, :].rearrange("p (a b) -> p a b", b=PARTS)
        expert_w = late.take(2 * SE)[0:1, :].rearrange("p (a b) -> p a b", b=SE)
        expert_w_all = late.take(SE)
        expert_w_col = late.take(1)[0:SE, :]
        hidden_id = sb("hidden_id", [P, SC])
        past = late_dst.take((SE + 1) * SC).rearrange("p (a b) -> p a b", b=SC)
        hidden_w = late.take(SC)

        def hidden_rows(j):
            return min(P, SE * SF - j * P)

        ADJ_FIRST = NT // 3
        ring.plan([("adjT", s, g) for s in range(ADJ_FIRST) for g in range(len(GROUPS))] + [("rank",)])
        ring.plan([("adjT", s, g) for s in range(ADJ_FIRST, NT) for g in range(len(GROUPS))])
        ring.plan([("gateT", g) for g in range(len(GROUPS))] + [("b2", t) for t in range(NT)] + [("biasT",)])
        before_experts = [ring.uses(b) for b in range(8)]
        AGG_OPEN = 6
        ring.plan([("agg1", t) for t in range(AGG_OPEN)])

        def agg_order():
            for t in range(AGG_OPEN, NT):
                yield ("agg1", t)
                u = 2 * (t - AGG_OPEN)
                yield from [("ahT", u), ("ahT", u + 1)]
            late_tiles = range(2 * (NT - AGG_OPEN), NT)
            for t in late_tiles:
                yield from [("xn2T", t - late_tiles[0]), ("ahT", t)]
            for t in range(len(late_tiles), NT):
                yield ("xn2T", t)
        ring.plan(list(agg_order()))
        ring.plan([("h1T", f, g) for f in range(HC) for g in range(len(GROUPS))])
        ring.plan([(k, t) for k in ("y2", "agg2") for t in range(NT)])
        ring.plan([("kT", m, g) for m in range(C) for g in range(len(GROUPS))])
        ring.plan([("q", t) for t in range(NT)] + [("v", t) for t in range(NT)] + [("ek", t) for t in range(NT)])
        ring.plan([("ctxT",)] + [("m5", c) for c in range(C)])
        ring.plan([("qT", t) for t in range(NT)] + [("att", t) for t in range(NT)])
        first_free = ring.at[("att", NT - 8)][0]
        result_banks, hidden_banks = ([(first_free + h + i) % 8 for i in range(4)] for h in (0, 4))
        ring.plan([("lastT", t) for t in range(NT)], result_banks)
        UP_AHEAD = 4
        TURN_TILES = [[t for t in range(g, min(g + TG // P, NT))] for g in range(0, NT, TG // P)]
        TG_N = len(TURN_TILES)

        def ffn_order():
            for j in range(SC):
                yield ("up", 0, j)
                if j == SC // 4:
                    yield ("route",)
                if j == 3 * SC // 4:
                    yield from [("expert_w",), ("b2_mix",)]
            for g in range(1, TG_N + 1):
                for j in range(SC):
                    if g < TG_N:
                        yield ("up", g, j)
                    yield ("down", g - 1, j)

        def next_chunk(g, j):
            return (g, j + 1) if j + 1 < SC else (g + 1, 0) if g + 1 < TG_N else None

        ring.plan([key for key in ffn_order() if key[0] != "down"], hidden_banks)
        for g, turn in enumerate(TURN_TILES):
            ring.plan([("down", t) for t in turn], result_banks[2 * (g % 2):2 * (g % 2) + 2])

        for n in ("routers", "router_bias", "expert_bias", "biases", "expert_b2", "adj_T",
                  "gw1", "gw2_first", "gw2_last", "w_qkv", "w_att", "b_out", "shared_b2", "sw1", "sw2"):
            load_sem(n)
        adj_stored = sem("adj_stored")
        tokens_zeroed = sem("tokens_zeroed")
        members_ready = sem("members_ready")
        gap_ready = sem("gap_ready")
        gap_exp = sem("gap_exp")
        gates_ready = sem("gates_ready")
        tiles_ready = sem("tiles_ready")
        slots_ready = sem("slots_ready")
        dinv_ready = sem("dinv_ready")
        z_ready = sem("z_ready")
        routers_ready = sem("routers_ready")
        rows_scattered = sem("rows_scattered")
        ew1_loaded = [sem(f"ew1_loaded{a}") for a in range(2)]
        ew2_loaded = [sem(f"ew2_loaded{a}") for a in range(2)]
        tile_loaded = sem("tile_loaded")
        tile_transposed = sem("tile_transposed")
        tile_T_ready = sem("tile_T_ready")
        tile_T_half_ready = sem("tile_T_half_ready")
        up_done = sem("up_done")
        gelu_done = sem("gelu_done")
        chunk_used = sem("chunk_used")
        w2_hi_ready = sem("w2_hi_ready")
        w2_split = sem("w2_split")
        hid_split = sem("hid_split")
        tile_out_ready = sem("tile_out_ready")
        tile_stored = sem("tile_stored")
        mixed_zeroed = sem("mixed_zeroed")
        tile_out_free = sem("tile_out_free")
        first_loaded = sem("first_loaded")
        second_loaded = [sem(f"second_loaded{g}") for g in range(NT // 2)]
        k_max_ready = sem("k_max_ready")
        k_scale_ready = sem("k_scale_ready")
        q_exp = sem("q_exp")
        q_ready = sem("q_ready")
        mean_ready = sem("mean_ready")
        last_scale_ready = sem("last_scale_ready")
        route_exp = sem("route_exp")
        route_weighted = sem("route_weighted")
        sw2_ready = sem("sw2_ready")
        shid_split = sem("shid_split")
        sw2_hi_ready = sem("sw2_hi_ready")
        sw2_split = sem("sw2_split")
        sw2_used = sem("sw2_used")

        def partitions(n, largest):
            if n == 0:
                yield ()
            for part in range(min(n, largest), 0, -1):
                for rest in partitions(n - part, part):
                    yield (part, *rest)

        block = ctx.enter_context(nc.Block())

        def bank(key):
            return psum[:, ring.at[key][0], :]

        def claim(pe, key):
            b, n = ring.at[key]
            if n:
                pe.wait_ge(bank_free[b], n)
            return psum[:, b, :], bank_full[b]

        def filled(eng, key):
            b, n = ring.at[key]
            eng.wait_ge(bank_full[b], n + 1)
            return psum[:, b, :], bank_free[b]

        def drained(eng, key):
            b, n = ring.at[key]
            eng.wait_ge(bank_free[b], n + 1)

        def block_span(eng, b):
            lo = eng.value_load(span[0:1, 0, bass.ds(b, 1)], min_val=0, max_val=UNITS - 1)
            hi = eng.value_load(span[0:1, 1, bass.ds(b, 1)], min_val=1, max_val=UNITS)
            return lo, hi

        def expert_bounds(eng, i):
            return [eng.value_load(first_tile_int[0:1, bass.ds(2 * i + k, 1)], min_val=min(k, 1), max_val=TILES - (k < 2))
                    for k in range(3)]

        def step_counter(eng, name):
            step = eng.alloc_register(name)
            eng.reg_mov(step, 0)
            return step

        def next_step(eng, step):
            eng.reg_add(step, step, 1)
            return eng.snap(step, min_val=1, max_val=NT * UNITS)

        tile_cols = [slice(t * P, t * P + P) for t in range(NT)]
        comp = [slice(0, MUL)] + [slice(MUL + m, D, 3) for m in range(3)]
        PAD_DMAS = -(-(EPAD - E) // (D // 2 // R))
        TABLE_DMAS = 3 * (1 + ((E - FULL * U) // J > 0) + ((E - FULL * U) % J > 0))

        @block.sync
        def _(sp):
            sp.wait_ge(padding_ready, 1)
            for name, t0, t1 in (("x", 0, NT // 2), ("x_rest", NT // 2, NT - 1)):
                sp.dma_start(x_rows[:, t0:t1, :], A["x"][t0 * P:t1 * P, :].rearrange("(t p) d -> p t d", p=P))\
                    .then_inc(loads[name], 16)
            sp.dma_start(x_rows[0:rows(NT - 1), NT - 1, :], A["x"][(NT - 1) * P:N, :]).then_inc(loads["x_rest"], 16)
            for w in ("Wk", "Wv", "Wl"):
                sp.dma_start(w_rows[w], A[f"L0_mix_{w}"].rearrange("(c p) d -> p c d", p=P)).then_inc(loads[w], 16)
            sp.dma_start(w_up[:, 0, :], A["L0_gnn_W_up0"]).then_inc(loads["w_up"], 16)
            sp.dma_start(w_up[:, 1, :], A["L0_gnn_W_up1"]).then_inc(loads["w_up"], 16)
            for b in ("bk", "bv", "bl"):
                sp.dma_start(b_row[b][:, :], A[f"L0_mix_{b}"].rearrange("(a d) -> a d", a=1).to_broadcast([P, D]))\
                    .then_inc(loads["mix_b"], 16)
            sp.dma_start(bq_col[:, :], A["L0_mix_bq"].rearrange("(c p) -> p c", p=P), allow_slow_non_contiguous=True).then_inc(loads["bq"], 16)
            split = math.gcd(E, 11 * 15 * 2)
            sp.dma_start(edge_in[0:E, :].rearrange("(a b) r -> a (b r)", a=split),
                         A["edge_attr_8"].rearrange("(a b) r -> a (b r)", a=split)).then_inc(loads["edge_in"], 16)
            sp.wait_ge(padding_ready, 2)
            zero_row = zeros16[0:1, :].bitcast(F32)
            for e0 in range(E, EPAD, D // 2 // R):
                n = min(D // 2 // R, EPAD - e0)
                sp.dma_start(edge_in[e0:e0 + n, :].rearrange("(a b) r -> a (b r)", a=1), zero_row[:, 0:n * R])\
                    .then_inc(loads["edge_in"], 16)
            sp.wait_ge(padding_ready, 3)
            for j in range(J):
                sp.dma_start(w_mlp1[R * j:R * j + R, j // 2, HID * (j % 2):HID * (j % 2) + HID], A["L0_gnn_W_mlp1"])\
                    .then_inc(loads["mlp"], 16)
            for j in range(2):
                half = slice(HID * j, HID * j + HID)
                sp.dma_start(w_mlp2[half, half], A["L0_gnn_W_mlp2"]).then_inc(loads["mlp"], 16)
                sp.dma_start(w_mlp3[half, half], A["L0_gnn_W_mlp3"]).then_inc(loads["mlp"], 16)
                sp.dma_start(w_mlp4[half, :], A["L0_gnn_W_mlp4"]).then_inc(loads["mlp"], 16)
            for k in range(2):
                sp.dma_start(w_out[:, k, :, :], A[f"L0_gnn_W_out{k}"].rearrange("(c p) v -> p c v", p=P))\
                    .then_inc(loads["w_out"], 16)
            for t in range(NT):
                drained(sp, ("xT", t))
            sp.dma_start(w_rows["Wq"], A["L0_mix_Wq"].rearrange("(c p) d -> p c d", p=P)).then_inc(loads["Wq"], 16)
            for t in range(NT):
                drained(sp, ("sender", t))
            sp.dma_start(sender_table.rearrange("(t p) d -> p t d", p=P), sender_rows).then_inc(sender_stored, 16)
            for h in range(2):
                sp.dma_start(tokens_sorted.rearrange("(t p) d -> p t d", p=P)[:, :, h * (D // 2):(h + 1) * (D // 2)],
                             zeros16[:, :].bitcast(F32).unsqueeze(1).to_broadcast([P, TILES + 2, D // 2])).then_inc(tokens_zeroed, 16)
            sure = -(-TOP * N // P)
            for h in range(2):
                sp.dma_start(mixed_sorted[sure * P:, :].rearrange("(t p) d -> p t d", p=P)[:, :, h * (D // 2):(h + 1) * (D // 2)],
                             zeros16[:, :].bitcast(F32).unsqueeze(1).to_broadcast([P, TILES - sure, D // 2])).then_inc(mixed_zeroed, 16)
            for a in range(PAIRS):
                sp.sem_inc(h3_out_free[a], 1)
            with sp.Fori(0, TURNS) as i:
                for a in range(PAIRS):
                    sp.wait_ge(h3_split[a], i + 2)
                    for part, h3 in enumerate((h3_hi[a], h3_lo[a])):
                        sp.dma_start(edge_hidden[part, bass.ds(i * (2 * PAIRS) + 2 * a, 2), :, :, :].rearrange("u q p n -> p (u q) n"),
                                       h3[:, :, :, :].bitcast(F32).rearrange("p u q n -> p (u q) n")).then_inc(h3_stored[a], 16)
                for a in range(PAIRS):
                    sp.wait_ge(h3_stored[a], i * 32 + 32)
                    sp.sem_inc(h3_out_free[a], 1)
            sp.wait_ge(span_ready, 1)

            def hidden_load(q, unit):
                for part in range(2):
                    sp.dma_start(h3_slot[q][part * HID:(part + 1) * HID, :, :].bitcast(F32),
                                 edge_hidden[part, unit, q, :, :].rearrange("u (j c) n -> c (u j) n", c=HID))\
                        .then_inc(h3_loaded[q], 16)

            step = step_counter(sp, "sp_step")
            with sp.Fori(0, NT) as b:
                lo, hi = block_span(sp, b)
                for a in range(PAIRS):
                    sp.wait_ge(h3_out_free[a], 1 + TURNS)
                with sp.Fori(lo, hi) as u:
                    s = next_step(sp, step)
                    for q in range(2):
                        sp.wait_ge(weights_done, s * J + 2 * q + 2)
                        hidden_load(q, bass.ds(u, 1))
            s = next_step(sp, step)
            sp.wait_ge(weights_done, s * J + 2)
            hidden_load(0, slice(0, 1))

            def spread(dst, name, what):
                sp.dma_start(dst, A[name].rearrange("(a d) -> a d", a=1).to_broadcast([P, A[name].shape[0]]))\
                    .then_inc(loads[what], 16)

            filled(sp, ("routersT",))
            sp.dma_start(expert_b2[:, :], A["L0_ffn_b2"]).then_inc(loads["expert_b2"], 16)
            sp.wait_ge(padding_ready, 4)
            sp.dma_start(bias_rows[0:HC, :], A["L1_gnn_b1"].rearrange("(c f) -> c f", f=P)).then_inc(loads["biases"], 16)
            flat_b1 = A["L1_ffn_b1"].rearrange("e f -> (e f)")
            sp.dma_start(bias_rows[HC:HC + SC - 1, :], flat_b1[0:(SC - 1) * P].rearrange("(c f) -> c f", f=P))\
                .then_inc(loads["biases"], 16)
            sp.dma_start(bias_rows[HC + SC - 1:HC + SC, 0:hidden_rows(SC - 1)],
                         flat_b1[(SC - 1) * P:SE * SF].rearrange("(c f) -> c f", c=1)).then_inc(loads["biases"], 16)

            def expert_weights(a, e, part):
                if part in (1, "1 first", "1 last"):
                    src = A["L0_ffn_W1"][bass.ds(e, 1), :, :] if not isinstance(e, int) else A["L0_ffn_W1"][e:e + 1, :, :]
                    src = src.rearrange("e (c p) f -> p (e c) f", p=P)
                    if part != "1 last":
                        sp.dma_start(ew1[a][:, 0:C // 2, :], src[:, 0:C // 2, :]).then_inc(ew1_loaded[a], 16)
                    if part != "1 first":
                        sp.dma_start(ew1[a][:, C // 2:, :], src[:, C // 2:, :]).then_inc(ew1_loaded[a], 16)
                else:
                    src = A["L0_ffn_W2"][bass.ds(e, 1), :, :] if not isinstance(e, int) else A["L0_ffn_W2"][e:e + 1, :, :]
                    src = src.rearrange("e (c p) d -> p (e c) d", p=P)
                    if part != "hi":
                        sp.dma_start(ew2_lo[a], src[:, 0:HALF, :]).then_inc(ew2_loaded[a], 16)
                    if part != "lo":
                        sp.dma_start(ew2_hi[a], src[:, HALF:FC, :]).then_inc(ew2_loaded[a], 16)

            for t in range(NT):
                filled(sp, ("conv", t))
            expert_weights(0, 0, "hi")
            for s in range(NT):
                for g in range(len(GROUPS)):
                    drained(sp, ("adjT", s, g))
            sp.wait_ge(stats_ready, 2)
            expert_weights(0, 0, "1 first")
            sp.wait_ge(rows_scattered, 16 * TOP * NT)
            expert_weights(0, 0, "1 last")
            sp.wait_ge(tile_loaded, 16)
            expert_weights(0, 0, "lo")
            sp.dma_start(adj_dram, adj_T).then_inc(adj_stored, 16)
            sp.wait_ge(adj_stored, 16)
            expert_weights(1, 1, 1)
            expert_weights(1, 1, 2)
            with sp.Fori(0, EX // 2 - 1) as i:
                for a in range(2):
                    end = sp.value_load(first_tile_int[0:1, bass.ds(2 * i + a + 1, 1)], min_val=1, max_val=TILES)
                    sp.wait_ge(chunk_used, end * FC + HID_SLOTS)
                    expert_weights(a, 2 * i + a + 2, 1)
                    expert_weights(a, 2 * i + a + 2, 2)
            end = sp.value_load(first_tile_int[0:1, EX - 1:EX], min_val=EX - 1, max_val=TILES - 1)
            sp.wait_ge(chunk_used, end * FC + HID_SLOTS)
            sp.wait_ge(first_loaded, 16 * NT)
            sp.dma_start(adj_in[:, 0:NT // 2, :], adj_dram[:, 0:NT // 2, :]).then_inc(loads["adj_T"], 16)
            sp.wait_ge(second_loaded[-1], 32)
            sp.wait_ge(loads["adj_T"], 16)
            sp.dma_start(adj_in[:, NT // 2:, :], adj_dram[:, NT // 2:, :]).then_inc(loads["adj_T"], 16)
            gw2_rows = A["L1_gnn_W2"].rearrange("(c p) d -> p c d", p=P)
            a0 = (NT + 2) * D + C * H1
            sp.dma_start(grid(big_b, a0, GW2_FIRST, D), gw2_rows[:, 0:GW2_FIRST, :]).then_inc(loads["gw2_first"], 16)
            sp.dma_start(gw1, A["L1_gnn_W1"].rearrange("(c p) f -> p c f", p=P)).then_inc(loads["gw1"], 16)
            filled(sp, ("b2", NT - 1))
            sp.dma_start(expert_b2[0:SE, :], A["L1_ffn_b2"]).then_inc(loads["shared_b2"], 16)
            spread(b_row["bk"][:, :], "L1_mix_b_out", "b_out")
            spread(b_row["bv"][:, :], "L1_mix_ln_scale", "b_out")
            for g in range(len(GROUPS)):
                filled(sp, ("h1T", HC - 1, g))
            sp.dma_start(grid(big_b, 0, HC - GW2_FIRST, D), gw2_rows[:, GW2_FIRST:, :]).then_inc(loads["gw2_last"], 16)
            filled(sp, ("y2", NT - 1))
            sp.dma_start(w_qkv, A["L1_mix_w_qkv"].rearrange("(c p) f -> p c f", p=P)).then_inc(loads["w_qkv"], 16)
            sp.dma_start(w_att, A["L1_mix_w_out"].rearrange("(c p) f -> p c f", p=P)).then_inc(loads["w_att"], 16)
            filled(sp, ("m5", C - 1))
            for e in range(SE):
                sp.dma_start(sw1[:, :, e, :], A["L1_ffn_W1"][e].rearrange("(c p) f -> p c f", p=P)).then_inc(loads["sw1"], 16)
            flat_w2 = A["L1_ffn_W2"].rearrange("e f d -> (e f) d")
            full_chunks = flat_w2[0:(SC - 1) * P, :].rearrange("(j p) d -> p j d", p=P)
            filled(sp, ("att", NT - 1))
            sp.dma_start(grid(big_b, SHID_END, SC - 1 - SW2_FIRST, D), full_chunks[:, SW2_FIRST:, :]).then_inc(loads["sw2"], 16)
            r = hidden_rows(SC - 1)
            sp.dma_start(sw2[SC - 1][0:r, :], flat_w2[(SC - 1) * P:(SC - 1) * P + r, :]).then_inc(loads["sw2"], 16)
            filled(sp, ("lastT", NT - 1))
            sp.dma_start(grid(big_a, SHID_END, SW2_FIRST, D), full_chunks[:, 0:SW2_FIRST, :]).then_inc(loads["sw2"], 16)
            for t in range(NT):
                drained(sp, ("down", t))
                sp.dma_start(out[t * P:t * P + rows(t), :], x_rows[0:rows(t), t, :]).then_inc(out_stored, 16)
            sp.wait_ge(out_stored, 16 * NT)

        @block.gpsimd
        def _(pool):
            nc.gpsimd.memset(x_rows[:, NT - 1, :], 0.0).then_inc(padding_ready, 1)
            nc.gpsimd.memset(zeros16[:, :], 0.0).then_inc(padding_ready, 1)
            nc.gpsimd.memset(w_mlp1[:, :, :], 0.0)
            nc.gpsimd.memset(w_mlp2[:, :], 0.0)
            nc.gpsimd.memset(w_mlp3[:, :], 0.0).then_inc(padding_ready, 1)
            nc.gpsimd.memset(ident[:, :], 0.0).then_inc(ident_zeroed, 1)
            nc.gpsimd.iota(iota_nodes[:, :], [[1, NP]], base=0, channel_multiplier=0,
                           allow_small_or_imprecise_dtypes=True)
            nc.gpsimd.iota(block_lo[:, :], [[P, NT]], base=0, channel_multiplier=0,
                           allow_small_or_imprecise_dtypes=True)
            nc.gpsimd.iota(unit_id[:, :], [[0, 1]], base=0, channel_multiplier=1,
                           allow_small_or_imprecise_dtypes=True)
            pool.wait_ge(ident_zeroed, 1)
            nc.gpsimd.affine_select(out=ident[:, :], in_=ident[:, :], compare_op=ALU.not_equal, fill=1.0, base=0,
                                    pattern=[[-1, P]], channel_multiplier=1).then_inc(consts_ready, 1)
            nc.gpsimd.memset(kv_T[:, :, :], 0.0)
            nc.gpsimd.memset(dst_int[:, :, :], -1)
            nc.gpsimd.memset(src_int[:, :, :], 0)
            nc.gpsimd.memset(edges[:, :, :], 0.0).then_inc(consts_ready, 1)
            pool.wait_ge(consts_ready, 2)
            tail = E - FULL * U
            q = tail // J
            for tab, a, w in ((dst_int[:, :, :], A["dst"], 1), (src_int[:, :, :], A["src"], 1),
                              (edges[:, :, J:J + J * Y], A["edge_attr_4"].rearrange("e y -> (e y)"), Y)):
                pool.dma_start(tab[:, 0:FULL, :], a[0:FULL * U * w].rearrange("(u p k) -> p u k", p=P, k=J * w))\
                    .then_inc(loads["edge_tables"], 16)
                if q:
                    pool.dma_start(tab[0:q, FULL, :], a[FULL * U * w:(FULL * U + q * J) * w]
                                   .rearrange("(p k) -> p k", k=J * w)).then_inc(loads["edge_tables"], 16)
                if tail % J:
                    pool.dma_start(tab[q:q + 1, FULL, 0:tail % J * w], a[(FULL * U + q * J) * w:E * w]
                                   .rearrange("(p k) -> p k", p=1)).then_inc(loads["edge_tables"], 16)
            pool.dma_start(dst_units[0:UNITS - 1, :], A["dst"][0:(UNITS - 1) * U].rearrange("(u k) -> u k", k=U))\
                .then_inc(loads["dst_units"], 16)
            pool.dma_start(dst_units[UNITS - 1:UNITS, :], A["dst"][E - U:E].rearrange("(u k) -> u k", k=U))\
                .then_inc(loads["dst_units"], 16)
            nc.gpsimd.memset(ones_col[:, :], 1.0)
            nc.gpsimd.iota(hidden_id[:, :], [[P, SC]], base=0, channel_multiplier=1, allow_small_or_imprecise_dtypes=True)
            nc.gpsimd.tensor_scalar(real_row[:, :], unit_id[:, :], float(rows(NT - 1)), None, ALU.is_lt)
            nc.gpsimd.tensor_copy(ident16[:, :], ident[:, :]).then_inc(consts_ready, 1)
            pool.wait_ge(reach_ready, 1)
            nc.gpsimd.partition_all_reduce(reach_all[:, :], reach[:, :], UNITS, RMAX).then_inc(reach_max_ready, 1)
            pool.wait_ge(loads["edge_in"], 16 * (1 + PAD_DMAS))
            with pool.Fori(0, TURNS) as i:
                for a in range(PAIRS):
                    pool.wait_ge(ea_transposed[a], i + 1)
                    pool.dma_start(ea_slot[a][:, :, :], edge_in.rearrange("(u p j) r -> u p (j r)", p=P, j=J)
                                 [bass.ds(i * (2 * PAIRS) + 2 * a, 2), :, :].rearrange("u p k -> p u k"))\
                        .then_inc(ea_loaded[a], 16)
            pool.wait_ge(sender_stored, 16)
            pool.wait_ge(loads["edge_tables"], 16 * TABLE_DMAS)
            pool.wait_ge(span_ready, 1)
            pool.sem_inc(idx_ready, J)
            step = step_counter(pool, "pool_step")
            with pool.Fori(0, NT) as b:
                lo, hi = block_span(pool, b)
                with pool.Fori(lo, hi) as u:
                    s = next_step(pool, step)
                    for j in range(J):
                        pool.wait_ge(products_done, s * J + j + 1)
                        nc.gpsimd.tensor_copy(idx_slot[j][:, :], src_int[:, bass.ds(u, 1), j]).then_inc(idx_ready, 1)
                        pool.wait_ge(idx_ready, s * J + j + 1)
                        pool.sem_inc(loop_entered, 1)
                        nc.gpsimd.indirect_dma_start(
                            out=sent[j][:, :], out_offset=None, in_=sender_table,
                            in_offset=bass.IndirectOffsetOnAxis(ap=idx_slot[j][:, 0:1], axis=0),
                            bounds_check=NP - 1, oob_is_err=False).then_inc(gathered[j], 16)

            nc.gpsimd.memset(bias_rows, 0.0).then_inc(padding_ready, 1)
            nc.gpsimd.memset(part_weights, 0.0)
            nc.gpsimd.memset(before_me, 0.0).then_inc(ident_zeroed, 1)
            pool.wait_ge(ident_zeroed, 2)
            for i, parts in enumerate(partitions(SE, SE)):
                for j, part in enumerate(parts):
                    nc.gpsimd.memset(part_weights[:, j, i:i + 1], part / SE)
            nc.gpsimd.affine_select(out=before_me, in_=before_me, compare_op=ALU.is_ge, fill=1.0, base=0,
                                    pattern=[[-1, P]], channel_multiplier=1).then_inc(consts_ready, 1)
            pool.wait_ge(slots_ready, 1)
            pool.wait_ge(ln_ready[2], NT)
            pool.wait_ge(tokens_zeroed, 32)
            for t in range(NT):
                for k in range(TOP):
                    r = rows(t)
                    nc.gpsimd.indirect_dma_start(
                        out=tokens_sorted, out_offset=bass.IndirectOffsetOnAxis(ap=slot_int[0:r, k, t:t + 1], axis=0),
                        in_=hx_rows[0:r, t, :], in_offset=None,
                        bounds_check=(TILES + 2) * P - 1, oob_is_err=False).then_inc(rows_scattered, 16)
            pool.wait_ge(rows_scattered, 16 * TOP * NT)
            pool.dma_start(tile_rows, tokens_sorted[0:P, :]).then_inc(tile_loaded, 16)
            pool.wait_ge(tile_transposed, 1)
            pool.dma_start(tile_rows, tokens_sorted[P:2 * P, :]).then_inc(tile_loaded, 16)
            pool.wait_ge(mixed_zeroed, 32)
            count = pool.value_load(first_tile_int[0:1, EX:EX + 1], min_val=EX, max_val=TILES)
            last = pool.value_load(first_tile_int[0:1, EX - 1:EX], min_val=EX - 1, max_val=TILES - 1)

            def tiles(start, end):
                with pool.Fori(start, end) as t:
                    pool.wait_ge(tile_transposed, t + 2)
                    pool.sem_inc(loop_entered, 1)
                    pool.dma_start(tile_rows, tokens_sorted[bass.ds(t * P + 2 * P, P), :]).then_inc(tile_loaded, 16)
                    pool.wait_ge(tile_out_ready, t + 2)
                    pool.sem_inc(loop_entered, 1)
                    pool.dma_start(mixed_sorted[bass.ds(t * P, P), :], tile_out).then_inc(tile_stored, 16)
                    pool.wait_ge(tile_stored, t * 16 + 16)
                    pool.sem_inc(tile_out_free, 1)

            def results(k):
                for t in range(NT):
                    r = rows(t)
                    nc.gpsimd.indirect_dma_start(
                        out=(second_rows if k else first_rows)[t][0:r, :], out_offset=None, in_=mixed_sorted,
                        in_offset=bass.IndirectOffsetOnAxis(ap=slot_int[0:r, k, t:t + 1], axis=0),
                        bounds_check=TILES * P - 1, oob_is_err=False).then_inc(second_loaded[t // 2] if k else first_loaded, 16)

            tiles(0, last)
            results(0)
            tiles(last, count)
            results(1)

        @block.scalar
        def _(act):
            def deviations(n, dst=rstd):
                act.wait_ge(stats_ready, n + 1)
                nc.scalar.activation(dst[:, :], meanvar[:, :, 1], ACT.Sqrt).then_inc(std_ready, 1)

            deviations(0)
            for w in ("Wk", "Wv", "Wl"):
                for c in range(C):
                    full, free = filled(act, ("wT", w, c))
                    nc.scalar.activation(w_T[w][:, c, :], full, ACT.Copy).then_inc(free, 1)
            for t in range(NT):
                full, free = filled(act, ("xT", t))
                nc.scalar.activation(xn_T[:, :, tile_cols[t]], full.rearrange("p (c n) -> p c n", c=C), ACT.Copy)\
                    .then_inc(free, 1)
            for t in range(NT):
                full, free = filled(act, ("sender", t))
                nc.scalar.activation(sender_rows[:, t, :], full, ACT.Copy, scale=MUL ** -0.5).then_inc(free, 1)
            full, free = filled(act, ("kvT",))
            act.wait_ge(consts_ready, 2)
            full = full.rearrange("p (c n) -> p c n", c=C)
            nc.scalar.activation(kv_T[0:HD, :, 0:HD], full[0:HD, :, 0:HD], ACT.Copy, scale=N ** -0.5)
            nc.scalar.activation(kv_T[HD:P, :, HD:P], full[HD:P, :, HD:P], ACT.Copy, scale=N ** -0.5).then_inc(free, 1)
            for c in range(C):
                full, free = filled(act, ("m2", c))
                nc.scalar.activation(m2[:, c, :], full, ACT.Copy).then_inc(free, 1)
            for c in range(C):
                full, free = filled(act, ("m3", c))
                nc.scalar.activation(m3[:, c, :], full, ACT.Copy).then_inc(free, 1)
            for t in range(NT):
                drained(act, ("mix", t))
            act.dma_start(router_rows[0:EX, :], A["L0_ffn_w_r"]).then_inc(loads["routers"], 16)
            act.dma_start(router_rows[EX:EX + PARTS, :], A["L1_ffn_router_w"]).then_inc(loads["routers"], 16)
            for i, n in enumerate(("L0_ffn_ln_g", "L0_ffn_ln_b")):
                r = EX + PARTS + i
                act.dma_start(router_rows[r:r + 1, :], A[n].rearrange("(a d) -> a d", a=1)).then_inc(loads["routers"], 16)
            act.dma_start(expert_bias_rows, A["L0_ffn_b1"].rearrange("e (c f) -> (e c) f", f=P)).then_inc(loads["expert_bias"], 16)

            def spread(dst, name, what):
                act.dma_start(dst, A[name].rearrange("(a d) -> a d", a=1).to_broadcast([P, A[name].shape[0]]))\
                    .then_inc(loads[what], 16)

            spread(router_bias[:, :], "L0_ffn_b_r", "router_bias")
            spread(b_row["bl"][:, :], "L1_gnn_b2", "router_bias")
            for a in range(PAIRS):
                act.sem_inc(silu_done[a], 3)
            with act.Fori(0, TURNS) as i:
                for layer in range(3):
                    for a in range(PAIRS):
                        act.wait_ge(layer_done[a], i * 3 + layer + 4)
                        dst = h_slot[a][:, :]
                        src = psum[:, 2 * a + 1, :]
                        if layer == 2:
                            act.wait_ge(h3_split[a], i + 1)
                            dst = h3_out[a][:, :, :, :].rearrange("p u q n -> p q u n")
                            src = src.rearrange("p (q u n) -> p q u n", q=2, u=2)
                        scale = R ** -0.5 if layer == 0 else SILU_2MOM * HID ** -0.5
                        nc.scalar.activation(dst, src, ACT.Silu, scale=scale).then_inc(silu_done[a], 1)
            act.wait_ge(span_ready, 1)
            act.sem_inc(adj_flushed, 1)
            act.sem_inc(hot_y_ready, J)
            act.sem_inc(scaled_ready, J)
            step = step_counter(act, "act_step")
            with act.Fori(0, NT) as b:
                lo, hi = block_span(act, b)
                with act.Fori(lo, hi) as u:
                    s = next_step(act, step)
                    act.wait_ge(edge_slot_ready, s)
                    for j in range(J):
                        k = j % 2
                        y = [edge_slot[:, J + Y * j + y:J + Y * j + y + 1] for y in range(Y)]
                        act.wait_ge(gathered[j], s * 16)
                        act.wait_ge(products_done, s * J + J + j - 1)
                        for m in range(3):
                            last = nc.scalar.activation(scaled[:, k, m, :], sent[j][:, MUL + m * MUL:2 * MUL + m * MUL], ACT.Copy, scale=y[1 + m])
                        last.then_inc(scaled_ready, 1)
                        act.wait_ge(hot_ready, s * J + j + 1)
                        act.wait_ge(scatter_done, s * J + J + j - 1)
                        for i in range(Y):
                            last = nc.scalar.activation(hot_y[:, k, i, :], hot_f[:, k, :], ACT.Copy, scale=y[i])
                        last.then_inc(hot_y_ready, 1)
                act.wait_ge(scatter_done, s * J + 2 * J)
                nc.scalar.activation(adj_rows[:, bass.ds(b, 1), :].rearrange("p b n -> p (b n)"),
                                     adj_psum[:, 0:NP], ACT.Copy).then_inc(adj_flushed, 1)
            act.wait_ge(stats_ready, 2)
            nc.scalar.activation(dinv[:, :], degree, ACT.Sqrt).then_inc(std_ready, 1)
            roots = [2]

            def root(t, n=1):
                roots[0] += 1
                act.wait_ge(stats_ready, roots[0])
                nc.scalar.activation(ln_root[:, t, 0:n], ln_pair[:, t, 0:n], ACT.Sqrt).then_inc(std_ready, 1)

            alpha = SILU_2MOM * HID ** -0.5 * (2 * MUL) ** -0.5 / AVG_NUM_NEIGHBORS

            def messages(t):
                if t >= 2:
                    filled(act, ("conv", t - 2))
                full, free = filled(act, ("msgT0", t))
                nc.scalar.activation(msg_T[:, t % 2, 0:D], full, ACT.Copy, scale=alpha).then_inc(free, 1)
                full, free = filled(act, ("msgT1", t))
                nc.scalar.activation(msg_T[:, t % 2, D:2 * D - P], full[:, 0:D - P], ACT.Copy, scale=alpha)
                nc.scalar.activation(msg_T[:, t % 2, 2 * D - P:], full[:, D - P:], ACT.Copy, scale=alpha * 3 ** -0.5)\
                    .then_inc(free, 1)

            def expert_inputs(t):
                full, free = filled(act, ("hT", t))
                nc.scalar.activation(xn_T[:, :, tile_cols[t]], full.rearrange("p (c n) -> p c n", c=C), ACT.Copy)\
                    .then_inc(free, 1)

            full, free = filled(act, ("routersT",))
            nc.scalar.activation(routers_T[:, :, :], full[:, 0:C * (EX + PARTS + 2)].rearrange("p (c e) -> p c e", c=C), ACT.Copy)\
                .then_inc(free, 1)
            full, free = filled(act, ("expert_biasT",))
            nc.scalar.activation(expert_bias_T[:, :], full[:, 0:P], ACT.Copy).then_inc(free, 1)
            messages(0)
            for t in range(NT):
                if t + 1 < NT:
                    messages(t + 1)
                root(t, 2)
                if t >= 2:
                    expert_inputs(t - 2)
            for t in range(NT - 2, NT):
                expert_inputs(t)

            def adjacency(s0, s1):
                for s in range(s0, s1):
                    for g, (g0, w) in enumerate(GROUPS):
                        full, free = filled(act, ("adjT", s, g))
                        nc.scalar.activation(adj_T[:, s, g0:g0 + w], full[:, 0:w], ACT.Copy).then_inc(free, 1)

            adjacency(0, ADJ_FIRST)
            act.wait_ge(gap_ready, 1)
            nc.scalar.activation(gap[:, :], gap[:, :], ACT.Exp).then_inc(gap_exp, 1)
            adjacency(ADJ_FIRST, NT)
            for g, (g0, w) in enumerate(GROUPS):
                full, free = filled(act, ("gateT", g))
                nc.scalar.activation(gates_T[:, g0:g0 + w], full[0:EX, 0:w], ACT.Copy).then_inc(free, 1)
            full, free = filled(act, ("biasT",))
            nc.scalar.activation(bias_T[:, :], full[:, 0:HC + SC], ACT.Copy).then_inc(free, 1)
            def w2_leading(t, a, f):
                act.wait_ge(chunk_used, t * FC + f + HID_SLOTS - 1)
                nc.scalar.activation(w2_hi[:, f % 2, :], w2_chunk(a, f), ACT.Copy).then_inc(w2_hi_ready, 1)

            def tile_T_half(n):
                act.wait_ge(tile_transposed, n)
                for c in range(C // 2, C):
                    last = nc.scalar.activation(tile_T[:, c, :], tile_psum(c), ACT.Identity,
                                                scale=ln_g[:, c, :], bias=ln_b[:, c, :])
                last.then_inc(tile_T_half_ready, 1)

            act.wait_ge(rows_scattered, 16 * TOP * NT)
            act.wait_ge(tiles_ready, 1)
            act.sem_inc(gelu_done, UP_BANKS)
            tile_T_half(1)
            with act.Fori(0, EX // 2) as i:
                bounds = expert_bounds(act, i)
                for a in range(2):
                    lo, hi = bounds[a:a + 2]
                    with act.Fori(lo, hi) as t:
                        act.wait_ge(ew2_loaded[a], i * 32 + 32)
                        w2_leading(t, a, 0)
                        for f in range(FC):
                            act.wait_ge(up_done, t * FC + f + 1)
                            act.wait_ge(chunk_used, t * FC + f + 1)
                            for dst in (hid, hid_hi):
                                last = nc.scalar.activation(dst[:, f % HID_SLOTS, :], psum[:, f % UP_BANKS, 0:P], ACT.Gelu,
                                                            bias=expert_bias_T[:, bass.ds(i * (2 * FC) + a * FC + f, 1)])
                            last.then_inc(gelu_done, 1)
                            if f + 1 < FC - 1:
                                w2_leading(t, a, f + 1)
                            if f == FC - 1:
                                w2_leading(t, a, f)
                        tile_T_half(t + 2)
            act.wait_ge(dinv_ready, 1)
            for t in range(NT + 1):
                if t < NT:
                    root(t)
                if t:
                    act.wait_ge(ln_ready[3], t)
                    nc.scalar.activation(z_rows[:, t - 1, :], xn2_rows[:, t - 1, :], ACT.Copy, scale=dinv[:, t - 1:t]).then_inc(z_ready, 1)

            def transposed(key, dst, t, n=None):
                full, free = filled(act, (key, t))
                n = P if n is None else n
                nc.scalar.activation(dst[:, :, t * P:t * P + n], full.rearrange("p (c n) -> p c n", c=C)[:, :, 0:n], ACT.Copy)\
                    .then_inc(free, 1)

            def sums(t):
                if t >= 2:
                    filled(act, ("ahT", t - 2))
                full, free = filled(act, ("agg1", t))
                nc.scalar.activation(ah_rows[:, t % 2, :], full, ACT.Copy, scale=dinv[:, t:t + 1]).then_inc(free, 1)

            sums(0)
            sums(1)
            for key in agg_order():
                if key[0] == "ahT":
                    transposed("ahT", ah_T, key[1])
                    if key[1] + 2 < NT:
                        sums(key[1] + 2)
                elif key[0] == "xn2T":
                    transposed("xn2T", xn_T, key[1])
            for f in range(HC):
                for g, (g0, w) in enumerate(GROUPS):
                    full, free = filled(act, ("h1T", f, g))
                    nc.scalar.activation(h1_T[:, f, g0:g0 + w], full[:, 0:w], ACT.Relu, bias=bias_T[:, f:f + 1]).then_inc(free, 1)
            for t in range(NT):
                full, free = filled(act, ("y2", t))
                nc.scalar.activation(z2_rows[:, t, :], full, ACT.Copy, scale=dinv[:, t:t + 1]).then_inc(free, 1)
            for m in range(C):
                act.wait_ge(k_max_ready, m + 1)
                for g, (g0, w) in enumerate(GROUPS):
                    full, free = filled(act, ("kT", m, g))
                    n = KEY_COLS[g]
                    nc.scalar.activation(ek_T[:, m, g0:g0 + n], full[:, 0:n], ACT.Exp, bias=k_max[:, m:m + 1]).then_inc(free, 1)
            for t in range(NT):
                drained(act, ("q", t))
                nc.scalar.activation(q_rows[:, t, :], q_rows[:, t, :], ACT.Exp).then_inc(q_exp, 1)
            for t in range(NT):
                full, free = filled(act, ("v", t))
                nc.scalar.activation(vx_rows[:, t, :], full, ACT.Copy).then_inc(free, 1)
            for t in range(NT):
                full, free = filled(act, ("ek", t))
                r = rows(t)
                nc.scalar.activation(ek_rows[0:r, t, :], full[0:r, :], ACT.Copy).then_inc(free, 1)
            full, free = filled(act, ("ctxT",))
            full = full.rearrange("p (c n) -> p c n", c=C)
            nc.scalar.activation(kv_T[0:HD, :, 0:HD], full[0:HD, :, 0:HD], ACT.Copy)
            nc.scalar.activation(kv_T[HD:P, :, HD:P], full[HD:P, :, HD:P], ACT.Copy).then_inc(free, 1)
            act.wait_ge(k_scale_ready, 1)
            for c in range(C):
                full, free = filled(act, ("m5", c))
                nc.scalar.activation(m5[:, c, :], full, ACT.Copy, scale=k_scale[:, c:c + 1]).then_inc(free, 1)
            for t in range(NT):
                transposed("qT", q_T, t)
            LAG = 4
            for t in range(NT + 2):
                if t < NT:
                    root(t)
                if 1 <= t <= NT:
                    root(t - 1)
                if t >= 2:
                    u = t - 2
                    act.wait_ge(last_scale_ready, u + 1)
                    nc.scalar.activation(last_rows[:, u, :], x_rows[:, u, :], ACT.Identity, scale=ln_root[:, u, 0:1],
                                         bias=last_shift[:, u:u + 1]).then_inc(ln_ready[5], 1)
                if t >= LAG:
                    transposed("lastT", xn_T, t - LAG)
            for t in range(NT + 2 - LAG, NT):
                transposed("lastT", xn_T, t)
            def sw2_leading(g, j):
                r = hidden_rows(j)
                act.wait_ge(loads["sw2"], 48)
                act.wait_ge(sw2_ready, 1)
                if g * (SC - 1) + j >= 2 and j != 1:
                    act.wait_ge(sw2_used, g * (SC - 1) + max(j - 1, 0))
                if g and j == 1:
                    filled(act, ("down", TURN_TILES[g - 1][-1]))
                nc.scalar.activation(w2_hi[0:r, j % 2, :], sw2[j][0:r, :], ACT.Copy, scale=hidden_w[0:r, j:j + 1]).then_inc(sw2_hi_ready, 1)

            for key in ffn_order():
                if key == ("route",):
                    drained(act, key)
                    nc.scalar.activation(route[:, :], route[:, :], ACT.Exp).then_inc(route_exp, 1)
                if key[0] == "up":
                    _, g, j = key
                    n, r = len(TURN_TILES[g]) * P, hidden_rows(j)
                    if g >= 2:
                        filled(act, ("down", TURN_TILES[g - 2][-1]))
                    if g * SC + j >= SHID_SLOTS:
                        act.wait_ge(shid_split, g * SC + j - SHID_SLOTS + 1)
                    full, free = filled(act, key)
                    for dst in (shid_full[:, j % SHID_SLOTS, :], shid_hi[:, g % 2, j, :]):
                        last = nc.scalar.activation(dst[0:r, 0:n], full[0:r, 0:n], ACT.Gelu, bias=bias_T[0:r, HC + j:HC + j + 1])
                    last.then_inc(free, 1)
                if key == ("b2_mix",):
                    sw2_leading(0, 0)
                if key[0] == "down" and next_chunk(*key[1:]):
                    sw2_leading(*next_chunk(*key[1:]))

        @block.vector
        def _(dve):
            steps = [0]

            def settle(ins):
                steps[0] += 1
                ins.then_inc(dve_step, 1)
                dve.wait_ge(dve_step, steps[0])

            def layer_norm(src, dst, n):
                for t in range(NT):
                    if t == 0:
                        dve.wait_ge(loads["x"], 16)
                    if t == NT // 2:
                        dve.wait_ge(loads["x_rest"], 32)
                    last = nc.vector.bn_stats(stats[:, t, :], src[:, t, :])
                settle(last)
                for t in range(NT):
                    last = nc.vector.bn_aggr(meanvar[:, t, :], stats[:, t, :])
                settle(last)
                nc.vector.tensor_scalar(meanvar[:, :, 1], meanvar[:, :, 1], LN_EPS, None, ALU.add).then_inc(stats_ready, 1)
                dve.wait_ge(std_ready, n + 1)
                settle(nc.vector.reciprocal(rstd[:, :], rstd[:, :]))
                for t in range(NT):
                    nc.vector.tensor_scalar(dst[:, t, :], src[:, t, :], meanvar[:, t, 0:1], rstd[:, t:t + 1],
                                            ALU.subtract, ALU.mult).then_inc(ln_ready[n], 1)

            layer_norm(x_rows, ln_rows, 0)
            dve.wait_ge(loads["dst_units"], 32)
            dve.wait_ge(consts_ready, 1)
            settle(nc.vector.tensor_copy(dst_unitf[:, :], dst_units[:, :]))
            nc.vector.tensor_reduce(unit_max[:, :], dst_unitf[:, :], AX_X, ALU.max)
            settle(nc.vector.tensor_reduce(unit_min[:, :], dst_unitf[:, :], AX_X, ALU.min))
            lo_u = block_lo[0:UNITS, :]
            nc.vector.tensor_scalar(touch[:, 0, :], lo_u, unit_max[:, :], None, ALU.is_le)
            nc.vector.tensor_scalar(touch[:, 1, :], lo_u, float(P - 1), unit_min[:, :], ALU.add, ALU.is_ge)
            nc.vector.tensor_scalar(touch[:, 3, 0:1], unit_id[0:UNITS, :], -1.0, float(UNITS), ALU.mult, ALU.add)
            settle(nc.vector.tensor_scalar(touch[:, 3, 1:2], unit_id[0:UNITS, :], 1.0, None, ALU.add))
            settle(nc.vector.tensor_tensor(touch[:, 2, :], touch[:, 0, :], touch[:, 1, :], ALU.mult))
            nc.vector.tensor_scalar(reach[:, 0:NT], touch[:, 2, :], touch[:, 3, 0:1], None, ALU.mult)
            nc.vector.tensor_scalar(reach[:, NT:], touch[:, 2, :], touch[:, 3, 1:2], None, ALU.mult).then_inc(reach_ready, 1)
            dve.wait_ge(reach_max_ready, 1)
            settle(nc.vector.tensor_scalar(span_f[:, 0, :], reach_all[0:1, 0:NT], -1.0, float(UNITS), ALU.mult, ALU.add))
            settle(nc.vector.tensor_scalar(span_f[:, 0, :], span_f[:, 0, :], float(UNITS - 1), None, ALU.min))
            settle(nc.vector.tensor_scalar(span_f[:, 1, :], span_f[:, 0, :], 1.0, None, ALU.add))
            settle(nc.vector.tensor_tensor(span_f[:, 1, :], span_f[:, 1, :], reach_all[0:1, NT:], ALU.max))
            nc.vector.tensor_copy(span[:, :, :], span_f[:, :, :]).then_inc(span_ready, 1)
            dve.wait_ge(loads["edge_tables"], 16 * TABLE_DMAS)
            nc.vector.tensor_copy(edges[:, :, 0:J], dst_int[:, :, :])
            settle(nc.vector.tensor_copy(edges[:, :, J + J * Y:], src_int[:, :, :]))
            dve.wait_ge(loads["mix_b"], 48)
            for t in range(NT):
                for w, b, dst in (("Wk", "bk", k_rows), ("Wv", "bv", v_rows)):
                    full, free = filled(dve, (w, t))
                    nc.vector.tensor_tensor(dst[:, t, :], full, b_row[b][:, :], ALU.add).then_inc(free, 1)
            full, free = filled(dve, ("mix_bias",))
            nc.vector.tensor_tensor(mix_bias[:, :], full, b_row["bl"][:, :], ALU.add).then_inc(free, 1)
            drained(dve, ("mix_bias",))
            for t in range(NT):
                settle(nc.vector.tensor_tensor(x_rows[:, t, :], x_rows[:, t, :], mix_bias[:, :], ALU.add))
                full, free = filled(dve, ("mix", t))
                nc.vector.tensor_tensor(x_rows[:, t, :], full, x_rows[:, t, :], ALU.add).then_inc(free, 1)
            dve.wait_ge(loads["mlp"], 16 * (J + 6))
            settle(nc.vector.tensor_copy(w4_hi[:, :], w_mlp4[:, :]))
            nc.vector.tensor_tensor(w4_lo[:, :], w_mlp4[:, :], w4_hi[:, :].bitcast(F32), ALU.subtract).then_inc(w4_ready, 1)
            def edge_inputs(a, turn, layers):
                dve.wait_ge(ea_transposed[a], turn + 2)
                dve.wait_ge(layer_done[a], layers)
                nc.vector.tensor_copy(ea_T[a][:, :], psum[0:J * R, 2 * a, 0:2 * P]).then_inc(ea_T_ready[a], 1)

            def split_hidden(a, turn, layers):
                dve.wait_ge(silu_done[a], layers)
                dve.wait_ge(h3_out_free[a], turn + 1)
                settle_turn(nc.vector.tensor_copy(h3_hi[a][:, :, :, :], h3_out[a][:, :, :, :]), a, turn)
                nc.vector.tensor_tensor(h3_lo[a][:, :, :, :], h3_out[a][:, :, :, :], h3_hi[a][:, :, :, :].bitcast(F32),
                                        ALU.subtract).then_inc(h3_split[a], 1)

            def settle_turn(ins, a, turn):
                ins.then_inc(hi_ready[a], 1)
                dve.wait_ge(hi_ready[a], turn + 1)

            for a in range(PAIRS):
                dve.sem_inc(h3_split[a], 1)
                edge_inputs(a, 0, 1)
            with dve.Fori(0, TURNS - 1) as i:
                for a in range(PAIRS):
                    edge_inputs(a, i + 1, i * 3 + 4)
                for a in range(PAIRS):
                    split_hidden(a, i, i * 3 + 6)
            for a in range(PAIRS):
                split_hidden(a, TURNS - 1, (TURNS - 1) * 3 + 6)
            dve.sem_inc(products_done, 2 * J)
            for a in range(PAIRS):
                dve.wait_ge(h3_split[a], 1 + TURNS)
            nc.vector.memset(hot_src[:, :, N:NP - 1], 0.0)
            settle(nc.vector.memset(hot_src[:, :, NP - 1:NP], 1.0))
            dve.sem_inc(hot_ready, J)
            dve.sem_inc(dot_ready, J)
            dve.sem_inc(msg_flushed, 1)
            step = step_counter(dve, "dve_step_no")
            with dve.Fori(0, NT) as b:
                lo, hi = block_span(dve, b)
                with dve.Fori(lo, hi) as u:
                    s = next_step(dve, step)
                    dve.wait_ge(hot_y_ready, s * J)
                    dve.wait_ge(products_done, s * J + J)
                    nc.vector.tensor_copy(edge_slot[:, :], edges[:, bass.ds(u, 1), :].rearrange("p u k -> p (u k)"))\
                        .then_inc(edge_slot_ready, 1)
                    dve.wait_ge(edge_slot_ready, s)
                    nodes = iota_nodes[:, bass.ds(b * P, P)]
                    for j in range(J):
                        k = j % 2
                        dst = edge_slot[:, j:j + 1]
                        dve.wait_ge(scatter_done, s * J + J + j - 1)
                        nc.vector.tensor_scalar(hot_f[:, k, :], nodes, dst, None, ALU.is_equal).then_inc(hot_ready, 1)
                        nc.vector.tensor_scalar(hot_dst[:, k, :], nodes, dst, None, ALU.is_equal)
                        src = edge_slot[:, J + J * Y + j:J + J * Y + j + 1]
                        nc.vector.tensor_scalar(hot_src[:, k, 0:N], iota_nodes[:, 0:N], src, None, ALU.is_equal)
                        dve.wait_ge(scaled_ready, s * J + j + 1)
                        nc.vector.tensor_reduce(dot[:, k, :], scaled[:, k, :, :].rearrange("p m u -> p u m"), AX_X, ALU.add)\
                            .then_inc(dot_ready, 1)
                        dve.wait_ge(weights_done, s * J + J + j + 1)
                        w = tile_w[k].rearrange("p (q u) -> p q u", q=4)
                        o = prod[:, k, :].rearrange("p (c u) -> p c u", u=MUL)
                        s0 = sent[j][:, 0:MUL].rearrange("p (a u) -> p a u", a=1)
                        s1 = sent[j][:, MUL:].rearrange("p (m u) -> p m u", u=MUL)
                        nc.vector.tensor_tensor(o[:, 0:5:4, :], w[:, 0:2, :], s0.to_broadcast([P, 2, MUL]), ALU.mult)
                        nc.vector.tensor_tensor(o[:, 1:4, :], s1, w[:, 2:3, :].to_broadcast([P, 3, MUL]), ALU.mult)
                        dve.wait_ge(dot_ready, s * J + j + 1)
                        nc.vector.tensor_tensor(o[:, 5, :], w[:, 3, :], dot[:, k, :], ALU.mult).then_inc(products_done, 1)
                dve.wait_ge(scatter_done, s * J + 2 * J)
                nc.vector.tensor_copy(msg_rows[:, bass.ds(b, 1), :].rearrange("p b n -> p (b n)"), msg_psum[:, :])\
                    .then_inc(msg_flushed, 1)
            dve.wait_ge(adj_flushed, NT + 1)
            nc.vector.tensor_scalar(degree, adj_rows[:, :, NP - 1], 1.0, None, ALU.add).then_inc(stats_ready, 1)
            nc.vector.memset(members_before[:, 0, :], 0.0)
            settle(nc.vector.memset(first_tile[:, 0:1], 0.0))
            drained(dve, ("routersT",))
            nc.vector.tensor_tensor(routers_scaled[:, :, :], routers_T[:, :, 0:EX], ln_g.to_broadcast([P, C, EX]), ALU.mult)\
                .then_inc(routers_ready, 1)
            roots = [2]

            def moments(row, t, twice=False):
                settle(nc.vector.bn_stats(stats[:, t, :], row))
                settle(nc.vector.bn_aggr(meanvar[:, t, :], stats[:, t, :]))
                last = nc.vector.tensor_scalar(ln_pair[:, t, 0:1], meanvar[:, t, 1:2], LN_EPS, None, ALU.add)
                if twice:
                    settle(last)
                    last = nc.vector.scalar_tensor_tensor(ln_pair[:, t, 1:2], ln_pair[:, t, 0:1], LN_EPS, meanvar[:, t, 1:2],
                                                          ALU.mult, ALU.add)
                last.then_inc(stats_ready, 1)
                roots[0] += 1
                return roots[0]

            def inverse_roots(t, number, n=1):
                dve.wait_ge(std_ready, number)
                settle(nc.vector.reciprocal(ln_root[:, t, 0:n], ln_root[:, t, 0:n]))

            dve.wait_ge(loads["router_bias"], 32)
            full, free = filled(dve, ("router_bias",))
            nc.vector.tensor_tensor(router_bias[:, :], full[:, 0:EX], router_bias[:, :], ALU.add).then_inc(free, 1)
            drained(dve, ("router_bias",))

            def add_router_bias(t):
                full, free = filled(dve, ("logits", t))
                nc.vector.tensor_tensor(logits[:, t, :], full[:, 0:EX], router_bias[:, :], ALU.add).then_inc(free, 1)

            numbers = {}
            for t in range(NT + 1):
                if t >= 4:
                    add_router_bias(t - 4)
                if t < NT:
                    full, free = filled(dve, ("conv", t))
                    nc.vector.tensor_tensor(x_rows[:, t, 0:MUL], full[:, 0:MUL], x_rows[:, t, 0:MUL], ALU.add)
                    v = x_rows[:, t, MUL:].rearrange("p (u m) -> p m u", m=3)
                    nc.vector.tensor_tensor(v, full[:, MUL:].rearrange("p (m u) -> p m u", m=3), v, ALU.add).then_inc(free, 1)
                    drained(dve, ("conv", t))
                    numbers[t] = moments(x_rows[:, t, :], t, True)
                if t:
                    inverse_roots(t - 1, numbers[t - 1], 2)
                    nc.vector.tensor_scalar(hx_rows[:, t - 1, :], x_rows[:, t - 1, :], meanvar[:, t - 1, 0:1], ln_root[:, t - 1, 1:2],
                                            ALU.subtract, ALU.mult).then_inc(ln_ready[2], 1)
            for t in range(NT - 3, NT):
                add_router_bias(t)
            for t in range(NT):
                drained(dve, ("logits", t))
                last = nc.vector.max(top_val[:, t, :], logits[:, t, :])
            settle(last)
            nc.vector.tensor_tensor(gap[:, :], top_val[:, :, 1], top_val[:, :, 0], ALU.subtract).then_inc(gap_ready, 1)
            for t in range(NT):
                last = nc.vector.max_index(top_idx[:, t, :], top_val[:, t, :], logits[:, t, :])
            settle(last)
            settle(nc.vector.tensor_copy(choice_f[:, :, :], top_idx[:, :, 0:TOP].rearrange("p t k -> p k t")))
            ids = iota_nodes[:, 0:EX].unsqueeze(1).to_broadcast([P, NT, EX])
            for k in range(TOP):
                last = nc.vector.tensor_tensor(chosen[:, k, :, :], ids, choice_f[:, k, :].unsqueeze(2).to_broadcast([P, NT, EX]),
                                               ALU.is_equal)
            settle(last)
            settle(nc.vector.tensor_tensor(member[:, :, :], chosen[:, 0, :, :], chosen[:, 1, :, :], ALU.add))
            settle(nc.vector.tensor_scalar(member[:, NT - 1, :], member[:, NT - 1, :], real_row[:, :], None, ALU.mult))
            for t in range(NT):
                last = nc.vector.tensor_tensor(members_before[:, t + 1, :], members_before[:, t, :], member[:, t, :], ALU.add)
                if t + 1 < NT:
                    settle(last)
            last.then_inc(members_ready, 1)
            full, free = filled(dve, ("rank",))
            counts = full[:, NT * EX:(NT + 1) * EX]
            settle(nc.vector.tensor_tensor(tile_tests[:, :, :], counts.unsqueeze(2).to_broadcast([P, EX, NT]),
                                           block_lo[:, :].unsqueeze(1).to_broadcast([P, EX, NT]), ALU.is_gt))
            settle(nc.vector.tensor_reduce(expert_tiles[:, :], tile_tests[:, :, :], AX_X, ALU.add))
            settle(nc.vector.tensor_scalar(expert_tiles[:, :], expert_tiles[:, :], 1.0, None, ALU.max))
            for e in range(EX):
                settle(nc.vector.tensor_tensor(first_tile[:, e + 1:e + 2], first_tile[:, e:e + 1], expert_tiles[:, e:e + 1], ALU.add))
            nc.vector.tensor_copy(first_tile_int[:, :], first_tile[0:1, :]).then_inc(tiles_ready, 1)
            settle(nc.vector.tensor_scalar(place_base[:, :], first_tile[:, 0:EX], float(P), None, ALU.mult))
            nc.vector.tensor_tensor(place[:, :, :], full[:, 0:NT * EX].rearrange("p (t e) -> p t e", e=EX),
                                    place_base[:, :].unsqueeze(1).to_broadcast([P, NT, EX]), ALU.add).then_inc(free, 1)
            drained(dve, ("rank",))
            for k in range(TOP):
                settle(nc.vector.tensor_tensor(member[:, :, :], chosen[:, k, :, :], place[:, :, :], ALU.mult))
                settle(nc.vector.tensor_reduce(slot_f[:, k, :], member[:, :, :], AX_X, ALU.add))
            nc.vector.tensor_tensor(slot_sorted[:, 0, :], slot_f[:, 0, :], slot_f[:, 1, :], ALU.min)
            settle(nc.vector.tensor_tensor(slot_sorted[:, 1, :], slot_f[:, 0, :], slot_f[:, 1, :], ALU.max))
            nc.vector.tensor_copy(slot_int[:, :, :], slot_sorted[:, :, :]).then_inc(slots_ready, 1)
            dve.wait_ge(gap_exp, 1)
            settle(nc.vector.tensor_scalar(gate[:, 0, :], gap[:, :], 1.0, None, ALU.add))
            settle(nc.vector.reciprocal(gate[:, 0, :], gate[:, 0, :]))
            settle(nc.vector.tensor_tensor(gate[:, 1, :], gap[:, :], gate[:, 0, :], ALU.mult))
            settle(nc.vector.tensor_tensor(slot_order[:, :], slot_f[:, 0, :], slot_f[:, 1, :], ALU.is_lt))
            for k in range(TOP):
                settle(nc.vector.tensor_tensor(gate_by_slot[:, k, :], gate[:, k, :], slot_order[:, :], ALU.mult))
                settle(nc.vector.tensor_tensor(slot_sorted[:, 0, :], gate[:, 1 - k, :], slot_order[:, :], ALU.mult))
                settle(nc.vector.tensor_tensor(slot_sorted[:, 0, :], gate[:, 1 - k, :], slot_sorted[:, 0, :], ALU.subtract))
                settle(nc.vector.tensor_tensor(gate_by_slot[:, k, :], gate_by_slot[:, k, :], slot_sorted[:, 0, :], ALU.add))
            for k in range(TOP):
                settle(nc.vector.tensor_tensor(chosen[:, k, :, :], chosen[:, k, :, :],
                                               gate[:, k, :].unsqueeze(2).to_broadcast([P, NT, EX]), ALU.mult))
            nc.vector.tensor_tensor(token_gates[:, :, :], chosen[:, 0, :, :], chosen[:, 1, :, :], ALU.add).then_inc(gates_ready, 1)
            nc.vector.tensor_scalar(x_scale[:, :], ln_root[:, :, 0], 1.0, None, ALU.add)
            settle(nc.vector.tensor_tensor(x_shift[:, :], ln_root[:, :, 0], meanvar[:, :, 0], ALU.mult))
            for t in range(NT):
                last = nc.vector.tensor_scalar(x_rows[:, t, :], x_rows[:, t, :], x_scale[:, t:t + 1], x_shift[:, t:t + 1],
                                               ALU.mult, ALU.subtract)
            settle(last)
            for t in range(NT):
                full, free = filled(dve, ("b2", t))
                nc.vector.tensor_tensor(x_rows[:, t, :], full, x_rows[:, t, :], ALU.add).then_inc(free, 1)
            dve.wait_ge(std_ready, 2)
            nc.vector.reciprocal(dinv[:, :], dinv[:, :]).then_inc(dinv_ready, 1)
            def tile_transposed_out(n):
                dve.wait_ge(tile_transposed, n)
                for c in range(C // 2):
                    last = nc.vector.tensor_scalar(tile_T[:, c, :], tile_psum(c), ln_g[:, c, :], ln_b[:, c, :],
                                                   ALU.mult, ALU.add)
                last.then_inc(tile_T_ready, 1)

            def hidden_rest(t, f):
                dve.wait_ge(gelu_done, t * FC + f + UP_BANKS + 1)
                nc.vector.tensor_tensor(hid_lo[:, f % HID_SLOTS, :], hid[:, f % HID_SLOTS, :], hid_hi[:, f % HID_SLOTS, :].bitcast(F32),
                                        ALU.subtract).then_inc(hid_split, 1)

            def w2_rest(t, a, f):
                w2 = w2_chunk(a, f)
                dve.wait_ge(w2_hi_ready, t * FC + f + 1)
                nc.vector.tensor_tensor(w2_lo[:, f % 2, :], w2, w2_hi[:, f % 2, :].bitcast(F32), ALU.subtract).then_inc(w2_split, 1)

            def add_results(t, k):
                r = rows(t)
                if k:
                    dve.wait_ge(second_loaded[t // 2], 32)
                else:
                    dve.wait_ge(first_loaded, 16 * NT)
                settle(nc.vector.scalar_tensor_tensor(x_rows[0:r, t, :], (second_rows if k else first_rows)[t][0:r, :], gate_by_slot[0:r, k, t:t + 1],
                                                      x_rows[0:r, t, :], ALU.mult, ALU.add))

            dve.sem_inc(tile_out_ready, 1)
            tile_transposed_out(1)
            dve.sem_inc(tile_out_free, 1)
            with dve.Fori(0, EX // 2) as i:
                bounds = expert_bounds(dve, i)
                for a in range(2):
                    with dve.Fori(bounds[a], bounds[a + 1]) as t:
                        w2_rest(t, a, 0)
                        for f in range(FC):
                            hidden_rest(t, f)
                            if f + 1 < FC - 1:
                                w2_rest(t, a, f + 1)
                        w2_rest(t, a, FC - 1)
                        tile_transposed_out(t + 2)
                        dve.wait_ge(chunk_used, t * FC + FC + HID_SLOTS)
                        dve.wait_ge(tile_out_free, t + 1)
                        nc.vector.tensor_copy(tile_out, psum[:, Y_BANK, :]).then_inc(tile_out_ready, 1)
            for t in range(NT + 1):
                if t < NT:
                    add_results(t, 0)
                    add_results(t, 1)
                    numbers[t] = moments(x_rows[:, t, :], t)
                if t:
                    u = t - 1
                    inverse_roots(u, numbers[u])
                    nc.vector.tensor_scalar(xn2_rows[:, u, :], x_rows[:, u, :], meanvar[:, u, 0:1], ln_root[:, u, 0:1],
                                            ALU.subtract, ALU.mult).then_inc(ln_ready[3], 1)
            for t in range(NT):
                full, free = filled(dve, ("agg2", t))
                nc.vector.scalar_tensor_tensor(conv_out[:, t % 2, :], full, dinv[:, t:t + 1], b_row["bl"][:, :], ALU.mult, ALU.add)\
                    .then_inc(free, 1)
                drained(dve, ("agg2", t))
                settle(nc.vector.scalar_tensor_tensor(x_rows[:, t, :], conv_out[:, t % 2, :], 0.0, x_rows[:, t, :], ALU.max, ALU.add))
            for m in range(C):
                for g, n in enumerate(KEY_COLS):
                    b, uses = ring.at[("kT", m, g)]
                    dve.wait_ge(bank_full[b], uses + 1)
                    last = nc.vector.tensor_reduce(k_max3[:, m, g:g + 1], psum[:, b, 0:n], AX_X, ALU.max)
                settle(last)
                settle(nc.vector.tensor_reduce(k_max[:, m:m + 1], k_max3[:, m, :], AX_X, ALU.max))
                nc.vector.tensor_scalar(k_max[:, m:m + 1], k_max[:, m:m + 1], -1.0, None, ALU.mult).then_inc(k_max_ready, 1)

            def heads(rows_ap):
                return rows_ap.rearrange("p (h d) -> p h d", h=HEADS)

            def queries(t):
                full, free = filled(dve, ("q", t))
                settle(nc.vector.tensor_reduce(q_max[:, :], heads(full), AX_X, ALU.max))
                nc.vector.tensor_tensor(heads(q_rows[:, t, :]), heads(full), q_max[:, :].unsqueeze(2).to_broadcast([P, HEADS, HD]),
                                        ALU.subtract).then_inc(free, 1)
                drained(dve, ("q", t))

            def normalised_queries(t):
                dve.wait_ge(q_exp, t + 1)
                settle(nc.vector.tensor_reduce(q_sum[:, t % 2, :], heads(q_rows[:, t, :]), AX_X, ALU.add))
                settle(nc.vector.reciprocal(q_sum[:, t % 2, :], q_sum[:, t % 2, :]))
                nc.vector.tensor_tensor(heads(q_rows[:, t, :]), heads(q_rows[:, t, :]),
                                        q_sum[:, t % 2, :].unsqueeze(2).to_broadcast([P, HEADS, HD]), ALU.mult).then_inc(q_ready, 1)

            queries(0)
            for t in range(1, NT):
                queries(t)
                normalised_queries(t - 1)
            normalised_queries(NT - 1)
            for m in range(C):
                for g in range(len(GROUPS)):
                    drained(dve, ("kT", m, g))
            settle(nc.vector.tensor_reduce(k_sum[:, :], ek_T[:, :, 0:N], AX_X, ALU.add))
            settle(nc.vector.tensor_scalar(k_sum[:, :], k_sum[:, :], float(N) * HD ** 0.5, None, ALU.mult))
            nc.vector.reciprocal(k_scale[:, :], k_sum[:, :]).then_inc(k_scale_ready, 1)
            dve.wait_ge(loads["b_out"], 32)
            last_numbers = {}
            for t in range(NT + 2):
                if t < NT:
                    full, free = filled(dve, ("att", t))
                    nc.vector.tensor_tensor(att_rows[:, t, :], full, b_row["bk"][:, :], ALU.add).then_inc(free, 1)
                    drained(dve, ("att", t))
                    numbers[t] = moments(att_rows[:, t, :], t)
                if 1 <= t <= NT:
                    u = t - 1
                    inverse_roots(u, numbers[u])
                    settle(nc.vector.scalar_tensor_tensor(att_rows[:, u, :], att_rows[:, u, :], meanvar[:, u, 0:1], b_row["bv"][:, :],
                                                          ALU.subtract, ALU.mult))
                    settle(nc.vector.scalar_tensor_tensor(x_rows[:, u, :], att_rows[:, u, :], ln_root[:, u, 0:1], x_rows[:, u, :],
                                                          ALU.mult, ALU.add))
                    last_numbers[u] = moments(x_rows[:, u, :], u)
                if t >= 2:
                    u = t - 2
                    inverse_roots(u, last_numbers[u])
                    nc.vector.tensor_scalar(last_shift[:, u:u + 1], meanvar[:, u, 0:1], ln_root[:, u, 0:1], -1.0, ALU.mult, ALU.mult)\
                        .then_inc(last_scale_ready, 1)
            for t in range(NT):
                drained(dve, ("lastT", t))
            settle(nc.vector.tensor_reduce(mean_col[:, :], xn_T[:, :, 0:N], AX_X, ALU.add))
            nc.vector.tensor_scalar(mean_col[:, :], mean_col[:, :], 1.0 / N, None, ALU.mult).then_inc(mean_ready, 1)
            def routing():
                full, free = filled(dve, ("route",))
                settle(nc.vector.tensor_reduce(route_f[:, 0:1], full[0:1, 0:PARTS], AX_X, ALU.max))
                nc.vector.tensor_scalar(route[:, :], full[0:1, 0:PARTS], route_f[:, 0:1], None, ALU.subtract).then_inc(free, 1)
                drained(dve, ("route",))
                dve.wait_ge(route_exp, 1)
                settle(nc.vector.tensor_reduce(route_f[:, 1:2], route[:, :], AX_X, ALU.add))
                settle(nc.vector.reciprocal(route_f[:, 1:2], route_f[:, 1:2]))
                settle(nc.vector.tensor_scalar(route[:, :], route[:, :], route_f[:, 1:2], None, ALU.mult))
                settle(nc.vector.max(route_top[:, :], route[:, :]))
                settle(nc.vector.max_index(route_idx[:, :], route_top[:, :], route[:, :]))
                settle(nc.vector.tensor_copy(route_f[:, 2:4], route_idx[:, 0:2]))
                settle(nc.vector.tensor_reduce(route_f[:, 4:5], route_top[:, 0:2], AX_X, ALU.add))
                settle(nc.vector.reciprocal(route_f[:, 4:5], route_f[:, 4:5]))
                settle(nc.vector.tensor_scalar(route_f[:, 6:8], route_top[:, 0:2], route_f[:, 4:5], None, ALU.mult))
                for k in range(2):
                    last = nc.vector.tensor_scalar(route_coef[:, k, :], iota_nodes[0:1, 0:PARTS], route_f[:, 2 + k:3 + k],
                                                   route_f[:, 6 + k:7 + k], ALU.is_equal, ALU.mult)
                settle(last)
                settle(nc.vector.tensor_tensor(route_coef[:, 0, :], route_coef[:, 0, :], route_coef[:, 1, :], ALU.add))
                settle(nc.vector.tensor_tensor(part_prod[:, :, :], part_weights[:, :, :],
                                               route_coef[:, 0, :].unsqueeze(1).to_broadcast([1, SE, PARTS]), ALU.mult))
                settle(nc.vector.tensor_reduce(expert_w[:, 0, :], part_prod[:, :, :], AX_X, ALU.add))
                settle(nc.vector.tensor_scalar(expert_w[:, 1, :], expert_w[:, 0, :], 1e-6, None, ALU.is_gt))
                nc.vector.tensor_tensor(expert_w[:, 0, :], expert_w[:, 0, :], expert_w[:, 1, :], ALU.mult).then_inc(route_weighted, 1)

            def hidden_weights():
                full, free = filled(dve, ("expert_w",))
                nc.vector.tensor_copy(expert_w_col[:, :], full[0:SE, SE:SE + 1])
                nc.vector.tensor_copy(expert_w_all[:, :], full[:, 0:SE]).then_inc(free, 1)
                drained(dve, ("expert_w",))
                for e in range(SE + 1):
                    last = nc.vector.tensor_scalar(past[:, e, :], hidden_id[:, :], float(e * SF), None, ALU.is_ge)
                settle(last)
                settle(nc.vector.tensor_tensor(past[:, 0:SE, :], past[:, 0:SE, :], past[:, 1:, :], ALU.subtract))
                settle(nc.vector.tensor_tensor(past[:, 0:SE, :], past[:, 0:SE, :],
                                               expert_w_all[:, :].unsqueeze(2).to_broadcast([P, SE, SC]), ALU.mult))
                nc.vector.tensor_reduce(hidden_w[:, :], past[:, 0:SE, :].rearrange("p e j -> p j e"), AX_X, ALU.add)\
                    .then_inc(sw2_ready, 1)
                dve.wait_ge(sw2_ready, 1)

            def sw2_rest(g, j):
                r = hidden_rows(j)
                dve.wait_ge(sw2_hi_ready, g * SC + j + 1)
                nc.vector.scalar_tensor_tensor(w2_lo[0:r, j % 2, :], sw2[j][0:r, :], hidden_w[0:r, j:j + 1],
                                               w2_hi[0:r, j % 2, :].bitcast(F32), ALU.mult, ALU.subtract).then_inc(sw2_split, 1)

            for key in ffn_order():
                if key == ("route",):
                    routing()
                elif key == ("expert_w",):
                    hidden_weights()
                elif key == ("b2_mix",):
                    full, free = filled(dve, key)
                    nc.vector.tensor_copy(mix_bias[:, :], full).then_inc(free, 1)
                    drained(dve, key)
                    sw2_rest(0, 0)
                elif key[0] == "up":
                    _, g, j = key
                    n, r = len(TURN_TILES[g]) * P, hidden_rows(j)
                    drained(dve, key)
                    nc.vector.tensor_tensor(shid_lo[0:r, g % 2, j, 0:n], shid_full[0:r, j % SHID_SLOTS, 0:n],
                                            shid_hi[0:r, g % 2, j, 0:n].bitcast(F32), ALU.subtract).then_inc(shid_split, 1)
                else:
                    _, g, j = key
                    if next_chunk(g, j):
                        sw2_rest(*next_chunk(g, j))
                    if j == SC - 1:
                        for t in TURN_TILES[g]:
                            settle(nc.vector.tensor_tensor(x_rows[:, t, :], x_rows[:, t, :], mix_bias[:, :], ALU.add))
                        for t in TURN_TILES[g]:
                            full, free = filled(dve, ("down", t))
                            nc.vector.tensor_tensor(x_rows[:, t, :], full, x_rows[:, t, :], ALU.add).then_inc(free, 1)

        @block.tensor
        def _(pe):
            pe.wait_ge(consts_ready, 1)
            for w in ("Wk", "Wv", "Wl"):
                pe.wait_ge(loads[w], 16)
                for c in range(C):
                    out_b, full = claim(pe, ("wT", w, c))
                    for o in range(C):
                        cols = slice(c * P, c * P + P) if w == "Wl" else comp[c]
                        last = nc.tensor.transpose(out_b[:, o * P:o * P + P], w_rows[w][:, o, cols], ident[:, :])
                    last.then_inc(full, 1)
            for t in range(NT):
                pe.wait_ge(ln_ready[0], t + 1)
                out_b, full = claim(pe, ("xT", t))
                for c in range(C):
                    last = nc.tensor.transpose(out_b[:, c * P:c * P + P], ln_rows[:, t, comp[c]], ident[:, :])
                last.then_inc(full, 1)
            pe.wait_ge(loads["w_up"], 32)
            for t in range(NT):
                drained(pe, ("xT", t))
                out_b, full = claim(pe, ("sender", t))
                for c in range(C):
                    last = nc.tensor.matmul(out_b[:, c * P:c * P + P], xn_T[:, c, tile_cols[t]], w_up[:, min(c, 1), :],
                                            start=True, stop=True)
                last.then_inc(full, 1)
            for w in ("Wk", "Wv", "Wl"):
                for c in range(C):
                    drained(pe, ("wT", w, c))
            for t in range(NT):
                for w in ("Wk", "Wv"):
                    out_b, full = claim(pe, (w, t))
                    for c in range(C):
                        last = nc.tensor.matmul(out_b, xn_T[:, c, tile_cols[t]], w_T[w][:, c, :], start=(c == 0), stop=(c == C - 1))
                    last.then_inc(full, 1)
            out_b, full = claim(pe, ("kvT",))
            for t in range(NT):
                drained(pe, ("Wk", t))
                drained(pe, ("Wv", t))
            for c in range(C):
                for t in range(NT):
                    r = slice(0, rows(t))
                    last = nc.tensor.matmul(out_b[:, c * P:c * P + P], v_rows[r, t, c * P:c * P + P],
                                            k_rows[r, t, c * P:c * P + P], start=(t == 0), stop=(t == NT - 1))
            last.then_inc(full, 1)
            drained(pe, ("kvT",))
            for a in range(PAIRS):
                pe.sem_inc(ea_transposed[a], 1)
            for c in range(C):
                out_b, full = claim(pe, ("m2", c))
                nc.tensor.matmul(out_b, kv_T[:, c, :], w_T["Wl"][:, c, :], start=True, stop=True).then_inc(full, 1)
            for c in range(C):
                drained(pe, ("m2", c))
            pe.wait_ge(loads["Wq"], 16)
            for i in range(C):
                out_b, full = claim(pe, ("m3", i))
                for c in range(C):
                    last = nc.tensor.matmul(out_b, w_rows["Wq"][:, c, comp[i]], m2[:, c, :], start=(c == 0), stop=(c == C - 1))
                last.then_inc(full, 1)
            pe.wait_ge(loads["bq"], 16)
            out_b, full = claim(pe, ("mix_bias",))
            for c in range(C):
                last = nc.tensor.matmul(out_b, bq_col[:, c:c + 1].to_broadcast([P, P]), m2[:, c, :],
                                        start=(c == 0), stop=(c == C - 1))
            last.then_inc(full, 1)
            for c in range(C):
                drained(pe, ("m3", c))
            for t in range(NT):
                out_b, full = claim(pe, ("mix", t))
                for c in range(C):
                    last = nc.tensor.matmul(out_b, xn_T[:, c, tile_cols[t]], m3[:, c, :], start=(c == 0), stop=(c == C - 1))
                last.then_inc(full, 1)
            for b in range(8):
                pe.wait_ge(bank_free[b], before_edges[b])
            pe.wait_ge(loads["mlp"], 16 * (J + 6))
            for a in range(PAIRS):
                pe.sem_inc(layer_done[a], 3)
            with pe.Fori(0, TURNS) as i:
                for a in range(PAIRS):
                    pe.wait_ge(ea_loaded[a], i * 16 + 16)
                    pe.wait_ge(silu_done[a], i * 3 + 3)
                    for h in range(2):
                        last = nc.tensor.transpose(psum[0:J * R, 2 * a, h * P:h * P + P], ea_slot[a][:, h, :], ident[:, :])
                    last.then_inc(ea_transposed[a], 1)
                for a in range(PAIRS):
                    pe.wait_ge(ea_T_ready[a], i + 1)
                    for q in range(2):
                        last = nc.tensor.matmul(psum[:, 2 * a + 1, q * 2 * P:(q + 1) * 2 * P], w_mlp1[:, q, :], ea_T[a][:, :],
                                                start=True, stop=True)
                    last.then_inc(layer_done[a], 1)
                for layer, w in ((1, w_mlp2), (2, w_mlp3)):
                    for a in range(PAIRS):
                        pe.wait_ge(silu_done[a], i * 3 + 3 + layer)
                        nc.tensor.matmul(psum[:, 2 * a + 1, :], w[:, :], h_slot[a][:, :], start=True, stop=True)\
                            .then_inc(layer_done[a], 1)
            for a in range(PAIRS):
                pe.wait_ge(silu_done[a], 3 + 3 * TURNS)

            def tile_weights(j):
                lhs = h3_slot[j // 2][:, j % 2, :]
                nc.tensor.matmul(tile_w[j % 2], lhs, w4_hi[:, :], start=True, stop=False)
                nc.tensor.matmul(tile_w[j % 2], lhs, w4_lo[:, :], start=False, stop=True).then_inc(weights_done, 1)

            pe.sem_inc(weights_done, 2 * J)
            pe.sem_inc(scatter_done, 2 * J)
            pe.wait_ge(padding_ready, 2)
            pe.wait_ge(consts_ready, 3)
            pe.wait_ge(span_ready, 1)
            pe.wait_ge(w4_ready, 1)
            pe.wait_ge(h3_loaded[0], 32)
            tile_weights(0)
            step = step_counter(pe, "pe_step")
            with pe.Fori(0, NT) as b:
                lo, hi = block_span(pe, b)
                pe.wait_ge(msg_flushed, b + 1)
                pe.wait_ge(adj_flushed, b + 1)
                for k in range(5):
                    nc.tensor.matmul(psum[:, k, :], zeros16[:, 0:P], zeros16[:, :], start=True, stop=False, skip_group_check=True)
                nc.tensor.matmul(adj_psum[:, bass.ds(b * P, P)], ident16[:, :], ident16[:, :], start=False, stop=True, skip_group_check=True)
                with pe.Fori(lo, hi) as u:
                    s = next_step(pe, step)
                    for j in range(J):
                        k = j % 2
                        if j == 1:
                            pe.wait_ge(h3_loaded[1], s * 32)
                        if j == J - 1:
                            pe.wait_ge(h3_loaded[0], s * 32 + 32)
                        tile_weights((j + 1) % J)
                        pe.wait_ge(products_done, s * J + J + j + 1)
                        pe.wait_ge(hot_y_ready, s * J + j + 1)
                        nc.tensor.matmul(psum[:, 0, :], hot_y[:, k, 0, :], prod[:, k, 0:D], start=False, stop=True, skip_group_check=True)
                        for m in range(3):
                            nc.tensor.matmul(psum[:, 1, m * MUL:m * MUL + MUL], hot_y[:, k, 1 + m, :],
                                             prod[:, k, D:D + MUL], start=False, stop=True, skip_group_check=True)
                        nc.tensor.matmul(psum[:, 1, 3 * MUL:], hot_f[:, k, :], prod[:, k, D + MUL:], start=False, stop=True,
                                         skip_group_check=True)
                        for a0 in range(0, NP, 512):
                            n = min(512, NP - a0)
                            last = nc.tensor.matmul(adj_psum[:, a0:a0 + n], hot_dst[:, k, :], hot_src[:, k, a0:a0 + n],
                                                    start=False, stop=True, skip_group_check=True)
                        last.then_inc(scatter_done, 1)
            def transposes(key, pieces):
                out_b, full = claim(pe, key)
                at = 0
                for piece in pieces:
                    r, n = piece.shape
                    last = nc.tensor.transpose(out_b[0:n, at:at + r], piece, ident[0:r, 0:r])
                    at += r
                last.then_inc(full, 1)

            def chunks(row):
                return [row[:, c * P:c * P + P] for c in range(row.shape[1] // P)]

            pe.wait_ge(msg_flushed, NT + 1)
            pe.wait_ge(adj_flushed, NT + 1)
            pe.wait_ge(loads["w_out"], 32)
            pe.wait_ge(loads["routers"], 64)
            pe.wait_ge(loads["expert_bias"], 16)
            for key in chain_order():
                if key[0] == "routersT":
                    transposes(key, chunks(router_rows))
                elif key[0] == "expert_biasT":
                    transposes(key, [expert_bias_rows])
                elif key[0] in ("msgT0", "msgT1"):
                    h0 = D * (key[0] == "msgT1")
                    transposes(key, chunks(msg_rows[:, key[1], h0:h0 + D]))
                elif key[0] == "hT":
                    pe.wait_ge(ln_ready[2], key[1] + 1)
                    transposes(key, chunks(hx_rows[:, key[1], :]))
                elif key[0] == "router_bias":
                    pe.wait_ge(routers_ready, 1)
                    out_b, full = claim(pe, key)
                    for c in range(C):
                        last = nc.tensor.matmul(out_b[:, 0:EX], routers_T[:, c, EX + PARTS + 1:EX + PARTS + 2].to_broadcast([P, P]),
                                                routers_T[:, c, 0:EX], start=(c == 0), stop=(c == C - 1))
                    last.then_inc(full, 1)
                elif key[0] == "logits":
                    drained(pe, ("hT", key[1]))
                    out_b, full = claim(pe, key)
                    for c in range(C):
                        last = nc.tensor.matmul(out_b[:, 0:EX], xn_T[:, c, tile_cols[key[1]]], routers_scaled[:, c, :],
                                                start=(c == 0), stop=(c == C - 1))
                    last.then_inc(full, 1)
                else:
                    t = key[1]
                    drained(pe, ("msgT0", t))
                    drained(pe, ("msgT1", t))
                    out_b, full = claim(pe, key)

                    def chunk(i):
                        return msg_T[:, t % 2, i * P:i * P + P]

                    for c, (i0, i1) in enumerate(((0, 7), (4, 1), (5, 2), (6, 3))):
                        w = w_out[:, min(c, 1), :, :]
                        nc.tensor.matmul(out_b[:, c * P:c * P + P], chunk(i0), w[:, 0, :], start=True, stop=False)
                        last = nc.tensor.matmul(out_b[:, c * P:c * P + P], chunk(i1), w[:, 1, :], start=False, stop=True)
                    last.then_inc(full, 1)

            def adjacency(s0, s1):
                for s in range(s0, s1):
                    for g, (g0, w) in enumerate(GROUPS):
                        transposes(("adjT", s, g), [adj_rows[:, b, tile_cols[s]] for b in range(g0 // P, (g0 + w) // P)])

            adjacency(0, ADJ_FIRST)
            pe.wait_ge(members_ready, 1)
            pe.wait_ge(consts_ready, 4)
            out_b, full = claim(pe, ("rank",))
            nc.tensor.matmul(out_b[:, 0:(NT + 1) * EX], ones_col[:, :].to_broadcast([P, P]),
                             members_before[:, :, :].rearrange("p t e -> p (t e)"), start=True, stop=False, skip_group_check=True)
            nc.tensor.matmul(out_b[:, 0:NT * EX], before_me[:, :], member[:, :, :].rearrange("p t e -> p (t e)"),
                             start=False, stop=True, skip_group_check=True).then_inc(full, 1)
            adjacency(ADJ_FIRST, NT)
            pe.wait_ge(gates_ready, 1)
            for g, (g0, w) in enumerate(GROUPS):
                transposes(("gateT", g), [token_gates[:, t, :] for t in range(g0 // P, (g0 + w) // P)])
            pe.wait_ge(loads["expert_b2"], 16)
            for t in range(NT):
                drained(pe, ("gateT", min(t * P // 512, len(GROUPS) - 1)))
                out_b, full = claim(pe, ("b2", t))
                nc.tensor.matmul(out_b, gates_T[:, tile_cols[t]], expert_b2[:, :], start=True, stop=True).then_inc(full, 1)
            pe.wait_ge(loads["biases"], 48)
            transposes(("biasT",), [bias_rows[:, :]])
            for b in range(8):
                pe.wait_ge(bank_free[b], before_experts[b])

            def tile_transposes():
                for c in range(C):
                    last = nc.tensor.transpose(tile_psum(c), tile_rows[:, c * P:c * P + P], ident[:, :])
                last.then_inc(tile_transposed, 1)

            pe.wait_ge(tile_loaded, 16)
            tile_transposes()
            pe.sem_inc(chunk_used, HID_SLOTS)
            with pe.Fori(0, EX // 2) as i:
                bounds = expert_bounds(pe, i)
                for a in range(2):
                    lo, hi = bounds[a:a + 2]
                    pe.wait_ge(ew1_loaded[a], i * 32 + 32)
                    pe.sem_inc(loop_entered, 1)
                    with pe.Fori(lo, hi) as t:
                        def down(f):
                            if f == 0:
                                pe.wait_ge(tile_out_ready, t + 1)
                            pe.wait_ge(w2_split, t * FC + f + 1)
                            pe.wait_ge(hid_split, t * FC + f + 1)
                            h, w = f % HID_SLOTS, f % 2
                            nc.tensor.matmul(psum[:, Y_BANK, :], hid_hi[:, h, :], w2_hi[:, w, :], start=(f == 0), stop=False)
                            nc.tensor.matmul(psum[:, Y_BANK, :], hid_lo[:, h, :], w2_hi[:, w, :], start=False, stop=False)
                            nc.tensor.matmul(psum[:, Y_BANK, :], hid_hi[:, h, :], w2_lo[:, w, :], start=False, stop=(f == FC - 1))\
                                .then_inc(chunk_used, 1)

                        pe.wait_ge(tile_T_ready, t + 1)
                        pe.wait_ge(tile_T_half_ready, t + 1)
                        for f in range(FC):
                            pe.wait_ge(gelu_done, t * FC + f + 1)
                            for c in range(C):
                                last = nc.tensor.matmul(psum[:, f % UP_BANKS, 0:P], ew1[a][:, c, f * P:f * P + P], tile_T[:, c, :],
                                                        start=(c == 0), stop=(c == C - 1))
                            last.then_inc(up_done, 1)
                            if f >= 2:
                                down(f - 2)
                        pe.wait_ge(tile_loaded, t * 16 + 32)
                        tile_transposes()
                        down(FC - 2)
                        down(FC - 1)
            count = pe.value_load(first_tile_int[0:1, EX:EX + 1], min_val=EX, max_val=TILES)
            pe.wait_ge(tile_out_ready, count + 1)
            pe.wait_ge(tile_T_ready, count + 1)
            pe.wait_ge(tile_T_half_ready, count + 1)
            open_banks = [claim(pe, ("agg1", t)) for t in range(AGG_OPEN)]
            for s in range(NT):
                if s in (0, NT // 2):
                    pe.wait_ge(loads["adj_T"], 16 + 16 * (s > 0))
                pe.wait_ge(z_ready, s + 1)
                r = rows(s)
                for t, (out_b, full) in enumerate(open_banks):
                    last = nc.tensor.matmul(out_b, adj_in[0:r, s, tile_cols[t]], z_rows[0:r, s, :], start=(s == 0), stop=(s == NT - 1))
                    if s == NT - 1:
                        last.then_inc(full, 1)

            def aggregate(key, rows_ap, t):
                out_b, full = claim(pe, (key, t))
                for s in range(NT):
                    r = rows(s)
                    last = nc.tensor.matmul(out_b, adj_in[0:r, s, tile_cols[t]], rows_ap[0:r, s, :], start=(s == 0), stop=(s == NT - 1))
                last.then_inc(full, 1)

            def project(key, t, lhs, rhs):
                out_b, full = claim(pe, (key, t))
                for c in range(len(rhs)):
                    last = nc.tensor.matmul(out_b[:, 0:rhs[c].shape[1]], lhs[:, c, tile_cols[t]], rhs[c], start=(c == 0), stop=(c == len(rhs) - 1))
                last.then_inc(full, 1)

            for key in agg_order():
                if key[0] == "agg1":
                    aggregate("agg1", z_rows, key[1])
                elif key[0] == "xn2T":
                    transposes(key, chunks(xn2_rows[:, key[1], :]))
                else:
                    drained(pe, ("agg1", key[1]))
                    transposes(key, chunks(ah_rows[:, key[1] % 2, :]))
            pe.wait_ge(loads["gw1"], 16)
            for t in range(NT):
                drained(pe, ("ahT", t))
            for f in range(HC):
                for g, (g0, w) in enumerate(GROUPS):
                    out_b, full = claim(pe, ("h1T", f, g))
                    for c in range(C):
                        last = nc.tensor.matmul(out_b[:, 0:w], gw1[:, c, f * P:f * P + P], ah_T[:, c, g0:g0 + w], start=(c == 0), stop=(c == C - 1))
                    last.then_inc(full, 1)
            for f in range(HC):
                for g in range(len(GROUPS)):
                    drained(pe, ("h1T", f, g))
            pe.wait_ge(loads["gw2_first"], 16)
            for t in range(NT):
                out_b, full = claim(pe, ("y2", t))
                for c in range(HC):
                    if (t, c) == (0, GW2_FIRST):
                        pe.wait_ge(loads["gw2_last"], 16)
                    last = nc.tensor.matmul(out_b, h1_T[:, c, tile_cols[t]], gw2[c], start=(c == 0), stop=(c == HC - 1))
                last.then_inc(full, 1)
            for t in range(NT):
                drained(pe, ("y2", t))
            for t in range(NT):
                aggregate("agg2", z2_rows, t)
            pe.wait_ge(loads["w_qkv"], 16)
            for m in range(C):
                for g, (g0, w) in enumerate(GROUPS):
                    out_b, full = claim(pe, ("kT", m, g))
                    for c in range(C):
                        last = nc.tensor.matmul(out_b[:, 0:w], w_qkv[:, c, D + m * P:D + m * P + P], xn_T[:, c, g0:g0 + w],
                                                start=(c == 0), stop=(c == C - 1))
                    last.then_inc(full, 1)
            for t in range(NT):
                project("q", t, xn_T, [w_qkv[:, c, 0:D] for c in range(C)])
            for t in range(NT):
                project("v", t, xn_T, [w_qkv[:, c, 2 * D:3 * D] for c in range(C)])
            for m in range(C):
                for g in range(len(GROUPS)):
                    drained(pe, ("kT", m, g))
            for t in range(NT):
                out_b, full = claim(pe, ("ek", t))
                r = rows(t)
                for c in range(C):
                    last = nc.tensor.transpose(out_b[0:r, c * P:c * P + P], ek_T[:, c, t * P:t * P + r], ident[:, :])
                last.then_inc(full, 1)
            for t in range(NT):
                drained(pe, ("v", t))
                drained(pe, ("ek", t))
            out_b, full = claim(pe, ("ctxT",))
            for c in range(C):
                for t in range(NT):
                    r = slice(0, rows(t))
                    last = nc.tensor.matmul(out_b[:, c * P:c * P + P], vx_rows[r, t, c * P:c * P + P],
                                            ek_rows[r, t, c * P:c * P + P], start=(t == 0), stop=(t == NT - 1))
            last.then_inc(full, 1)
            drained(pe, ("ctxT",))
            pe.wait_ge(loads["w_att"], 16)
            for c in range(C):
                out_b, full = claim(pe, ("m5", c))
                nc.tensor.matmul(out_b, kv_T[:, c, :], w_att[:, c, :], start=True, stop=True).then_inc(full, 1)
            pe.wait_ge(k_scale_ready, 1)
            for t in range(NT):
                pe.wait_ge(q_ready, t + 1)
                transposes(("qT", t), chunks(q_rows[:, t, :]))
            for c in range(C):
                drained(pe, ("m5", c))
            for t in range(NT):
                drained(pe, ("qT", t))
                project("att", t, q_T, [m5[:, c, :] for c in range(C)])
            def hidden_columns(g, j):
                out_b, full = claim(pe, ("up", g, j))
                n, r, n0 = len(TURN_TILES[g]) * P, hidden_rows(j), TURN_TILES[g][0] * P
                for c in range(C):
                    last = nc.tensor.matmul(out_b[0:r, 0:n], sw1_cols[:, c, j * P:j * P + r], xn_T[:, c, n0:n0 + n],
                                            start=(c == 0), stop=(c == C - 1))
                last.then_inc(full, 1)

            for t in range(NT):
                pe.wait_ge(ln_ready[5], t + 1)
                transposes(("lastT", t), chunks(last_rows[:, t, :]))
                if t == NT // 2:
                    pe.wait_ge(loads["sw1"], 16 * SE)
                    for u in TURN_TILES[0]:
                        drained(pe, ("lastT", u))
                if 0 <= t - NT // 2 < UP_AHEAD:
                    hidden_columns(0, t - NT // 2)
            for t in range(NT):
                drained(pe, ("lastT", t))
            for key in ffn_order():
                if key == ("route",):
                    pe.wait_ge(mean_ready, 1)
                elif key == ("expert_w",):
                    pe.wait_ge(route_weighted, 1)
                elif key == ("b2_mix",):
                    drained(pe, ("expert_w",))
                    pe.wait_ge(loads["shared_b2"], 16)
                elif key[0] == "down":
                    _, g, j = key
                    r = hidden_rows(j)
                    if j == 0:
                        outs = [claim(pe, ("down", u)) for u in TURN_TILES[g]]
                    pe.wait_ge(shid_split, g * SC + j + 1)
                    pe.wait_ge(sw2_split, g * SC + j + 1)
                    for k, (h, w) in enumerate(((shid_hi, w2_hi), (shid_lo, w2_hi), (shid_hi, w2_lo))):
                        for i, (out_b, full) in enumerate(outs):
                            last = nc.tensor.matmul(out_b, h[0:r, g % 2, j, i * P:i * P + P], w[0:r, j % 2, :],
                                                    start=(j == 0 and k == 0), stop=(j == SC - 1 and k == 2))
                            if j == SC - 1 and k == 2:
                                last.then_inc(full, 1)
                    if j < SC - 1:
                        last.then_inc(sw2_used, 1)
                    continue
                else:
                    if key not in [("up", 0, j) for j in range(UP_AHEAD)]:
                        hidden_columns(*key[1:])
                    continue
                out_b, full = claim(pe, key)
                if key == ("route",):
                    for c in range(C):
                        last = nc.tensor.matmul(out_b[0:1, 0:PARTS], mean_col[:, c:c + 1], routers_T[:, c, EX:EX + PARTS],
                                                start=(c == 0), stop=(c == C - 1))
                elif key == ("expert_w",):
                    nc.tensor.matmul(out_b[:, 0:SE], ones_col[0:1, :].to_broadcast([1, P]), expert_w[:, 0, :], start=True, stop=True)
                    last = nc.tensor.matmul(out_b[0:SE, SE:SE + 1], expert_w[:, 0, :], ones_col[0:1, :], start=True, stop=True)
                elif key == ("b2_mix",):
                    last = nc.tensor.matmul(out_b, expert_w_col[:, :].to_broadcast([SE, P]), expert_b2[0:SE, :], start=True, stop=True)
                last.then_inc(full, 1)


def kernel(**inputs):
    import numpy as _np
    import concourse.bacc as _bacc
    from concourse import mybir as _mybir
    from concourse.bass_utils import run_bass_kernel_spmd as _run

    nc = _bacc.Bacc("TRN2", target_bir_lowering=False, num_devices=1)
    arrays, aps = {}, {}
    for name, value in inputs.items():
        a = _np.ascontiguousarray(value)
        arrays[f"in_{name}"] = a
        aps[name] = nc.dram_tensor(f"in_{name}", a.shape, _mybir.dt.from_np(a.dtype), kind="ExternalInput").ap()
    out = nc.dram_tensor("out_x", aps["x"].shape, F32, kind="ExternalOutput").ap()
    graph_block_kernel(nc, aps, out)
    r = _run(nc, [arrays], core_ids=[0])
    return r.results[0]["out_x"]
```
